# Optimizing a Trainium2 kernel written in Bass

```python
import numpy as np
import jax
import jax.numpy as jnp

def _softmax(x, axis=-1):
    return jax.nn.softmax(x, axis=axis)

def _gelu(x):
    return jax.nn.gelu(x, approximate=True)

def _silu(x):
    return jax.nn.silu(x)

def _sigmoid(x):
    return jax.nn.sigmoid(x)

def _layernorm(x, axis=-1, eps=1e-05):
    m = jnp.mean(x, axis=axis, keepdims=True)
    v = jnp.var(x, axis=axis, keepdims=True)
    return (x - m) / jnp.sqrt(v + eps)

def _scatter_add(tgt, idx, src, axis=0):
    return tgt.at[idx].add(src)

def _segment_sum(src, seg, n):
    return jax.ops.segment_sum(src, seg, n)
kernel_name = 'mk_recurrent_d2_jaxref_r4_3d0aa8'

def setup_inputs(seed: int=0):
    np.random.seed(seed)
    _w = jnp.asarray

    def _L0_attn_setup():
        import jax, jax.numpy as jnp
        import numpy as np
        D_MODEL = 256
        D_STATE = 16
        LN_EPS = 1e-05

        def _layernorm(x, w, b):
            mu = jnp.mean(x, axis=-1, keepdims=True)
            var = jnp.mean(jnp.square(x - mu), axis=-1, keepdims=True)
            return (x - mu) * jax.lax.rsqrt(var + LN_EPS) * w + b
        key = jax.random.key(seed)
        ks = jax.random.split(key, 12)
        B, S, D, N = (8, 1024, D_MODEL, D_STATE)
        sD = 1.0 / np.sqrt(D)
        sN = 1.0 / np.sqrt(N)
        return {'x': jax.random.normal(ks[0], (B, S, D), dtype=jnp.float32), 'Ws': jax.random.uniform(ks[1], (N, D), jnp.float32, -sD, sD), 'bs': jax.random.uniform(ks[2], (N,), jnp.float32, -sD, sD), 'Wi': jax.random.uniform(ks[3], (N, D), jnp.float32, -sD, sD), 'bi': jax.random.uniform(ks[4], (N,), jnp.float32, -sD, sD), 'Wo': jax.random.uniform(ks[5], (D, N), jnp.float32, -sN, sN), 'bo': jax.random.uniform(ks[6], (D,), jnp.float32, -sN, sN), 'Wg': jax.random.uniform(ks[7], (D, D), jnp.float32, -sD, sD), 'bg': jax.random.uniform(ks[8], (D,), jnp.float32, -sD, sD), 'ln_w': jnp.ones((D,), jnp.float32), 'ln_b': jnp.zeros((D,), jnp.float32), 'A': jax.random.normal(ks[9], (N, N), dtype=jnp.float32) * 0.01}
    _L0_attn_in = _L0_attn_setup()

    def _L0_ffn_setup():
        import jax, jax.numpy as jnp
        import numpy as np
        D_MODEL = 256
        M = 64
        INNER = 16
        key = jax.random.key(seed)
        ks = jax.random.split(key, 9)

        def init(k, shape, fan_in):
            bound = 1.0 / np.sqrt(fan_in)
            return jax.random.uniform(k, shape, jnp.float32, -bound, bound)
        x = jax.random.normal(ks[0], (16, 1024, D_MODEL), dtype=jnp.float32)
        Win = init(ks[1], (D_MODEL, M), D_MODEL)
        bin_ = init(ks[2], (M,), D_MODEL)
        W1 = init(ks[3], (M, INNER), 1)
        b1 = init(ks[4], (M, INNER), 1)
        W2 = init(ks[5], (M, INNER), INNER)
        b2 = init(ks[6], (M,), INNER)
        Wout = init(ks[7], (M, D_MODEL), M)
        bout = init(ks[8], (D_MODEL,), M)
        return {'x': x, 'Win': Win, 'bin_': bin_, 'W1': W1, 'b1': b1, 'W2': W2, 'b2': b2, 'Wout': Wout, 'bout': bout}
    _L0_ffn_in = _L0_ffn_setup()

    def _L1_attn_setup():
        import jax, jax.numpy as jnp
        import numpy as np
        HEADS = 16
        D_MODEL = 256
        D_K = D_MODEL // HEADS
        SEQ = 512
        BSZ = 2

        def softmax_one(x, axis):
            x = x - jnp.max(x, axis=axis, keepdims=True)
            ex = jnp.exp(x)
            return ex / (1.0 + jnp.sum(ex, axis=axis, keepdims=True))
        key = jax.random.key(seed)
        ks = jax.random.split(key, 7)
        s = 1.0 / np.sqrt(D_MODEL)
        return {'x': jax.random.normal(ks[0], (SEQ, BSZ, D_MODEL), dtype=jnp.float32), 'Wq': jax.random.normal(ks[1], (D_MODEL, D_MODEL), dtype=jnp.float32) * s, 'bq': jnp.zeros((D_MODEL,), dtype=jnp.float32), 'Wk': jax.random.normal(ks[2], (D_MODEL, D_MODEL), dtype=jnp.float32) * s, 'bk': jnp.zeros((D_MODEL,), dtype=jnp.float32), 'Wv': jax.random.normal(ks[3], (D_MODEL, D_MODEL), dtype=jnp.float32) * s, 'bv': jnp.zeros((D_MODEL,), dtype=jnp.float32)}
    _L1_attn_in = _L1_attn_setup()

    def _L1_ffn_setup():
        import jax, jax.numpy as jnp
        import numpy as np
        E = 8
        K = 2
        CAP_FACTOR = 1.0
        key = jax.random.key(seed)
        k0, k1, k2, k3 = jax.random.split(key, 4)
        B, S, M, H = (4, 512, 256, 1024)
        x = jax.random.normal(k0, (B, S, M), jnp.float32)
        wg = jax.random.normal(k1, (M, E), jnp.float32) * 0.02
        w1 = jax.random.normal(k2, (E, M, H), jnp.float32) * 0.02
        b1 = jnp.zeros((E, H), jnp.float32)
        w2 = jax.random.normal(k3, (E, H, M), jnp.float32) * 0.02
        b2 = jnp.zeros((E, M), jnp.float32)
        return {'x': x, 'wg': wg, 'w1': w1, 'b1': b1, 'w2': w2, 'b2': b2}
    _L1_ffn_in = _L1_ffn_setup()
    _d = {'L0_attn_x': _L0_attn_in['x'], 'L0_attn_Ws': _L0_attn_in['Ws'], 'L0_attn_bs': _L0_attn_in['bs'], 'L0_attn_Wi': _L0_attn_in['Wi'], 'L0_attn_bi': _L0_attn_in['bi'], 'L0_attn_Wo': _L0_attn_in['Wo'], 'L0_attn_bo': _L0_attn_in['bo'], 'L0_attn_Wg': _L0_attn_in['Wg'], 'L0_attn_bg': _L0_attn_in['bg'], 'L0_attn_ln_w': _L0_attn_in['ln_w'], 'L0_attn_ln_b': _L0_attn_in['ln_b'], 'L0_attn_A': _L0_attn_in['A'], 'L0_ffn_Win': _L0_ffn_in['Win'], 'L0_ffn_bin_': _L0_ffn_in['bin_'], 'L0_ffn_W1': _L0_ffn_in['W1'], 'L0_ffn_b1': _L0_ffn_in['b1'], 'L0_ffn_W2': _L0_ffn_in['W2'], 'L0_ffn_b2': _L0_ffn_in['b2'], 'L0_ffn_Wout': _L0_ffn_in['Wout'], 'L0_ffn_bout': _L0_ffn_in['bout'], 'L1_attn_Wq': _L1_attn_in['Wq'], 'L1_attn_bq': _L1_attn_in['bq'], 'L1_attn_Wk': _L1_attn_in['Wk'], 'L1_attn_bk': _L1_attn_in['bk'], 'L1_attn_Wv': _L1_attn_in['Wv'], 'L1_attn_bv': _L1_attn_in['bv'], 'L1_ffn_wg': _L1_ffn_in['wg'], 'L1_ffn_w1': _L1_ffn_in['w1'], 'L1_ffn_b1': _L1_ffn_in['b1'], 'L1_ffn_w2': _L1_ffn_in['w2'], 'L1_ffn_b2': _L1_ffn_in['b2']}
    _x0 = _d['L0_attn_x']
    _d['L0_attn_x'] = jax.random.normal(jax.random.fold_in(jax.random.key(seed), 1), (4, 2048, 256), dtype=_x0.dtype)
    del _x0
    return _d

def reference(L0_attn_x, L0_attn_Ws, L0_attn_bs, L0_attn_Wi, L0_attn_bi, L0_attn_Wo, L0_attn_bo, L0_attn_Wg, L0_attn_bg, L0_attn_ln_w, L0_attn_ln_b, L0_attn_A, L0_ffn_Win, L0_ffn_bin_, L0_ffn_W1, L0_ffn_b1, L0_ffn_W2, L0_ffn_b2, L0_ffn_Wout, L0_ffn_bout, L1_attn_Wq, L1_attn_bq, L1_attn_Wk, L1_attn_bk, L1_attn_Wv, L1_attn_bv, L1_ffn_wg, L1_ffn_w1, L1_ffn_b1, L1_ffn_w2, L1_ffn_b2):

    def _L0_attn_ref(x, Ws, bs, Wi, bi, Wo, bo, Wg, bg, ln_w, ln_b, A):
        import jax, jax.numpy as jnp
        import numpy as np
        D_MODEL = 256
        D_STATE = 16
        LN_EPS = 1e-05

        def _layernorm(x, w, b):
            mu = jnp.mean(x, axis=-1, keepdims=True)
            var = jnp.mean(jnp.square(x - mu), axis=-1, keepdims=True)
            return (x - mu) * jax.lax.rsqrt(var + LN_EPS) * w + b
        B, S, D = x.shape
        residual = x
        xn = _layernorm(x, ln_w, ln_b)
        u = jnp.einsum('bsd,nd->bsn', xn, Ws) + bs + jnp.einsum('bsd,nd->bsn', xn, Wi) + bi
        h0 = jnp.zeros((B, A.shape[0]), x.dtype)

        def step(h, u_t):
            h = jnp.tanh(h @ A.T + u_t)
            return (h, h)
        _, H = jax.lax.scan(step, h0, jnp.swapaxes(u, 0, 1))
        H = jnp.swapaxes(H, 0, 1)
        out = jnp.einsum('bsn,dn->bsd', H, Wo) + bo
        gate = jax.nn.sigmoid(jnp.einsum('bsd,ed->bse', xn, Wg) + bg)
        return out * gate + residual

    def _L0_ffn_ref(x, Win, bin_, W1, b1, W2, b2, Wout, bout):
        import jax, jax.numpy as jnp
        import numpy as np
        D_MODEL = 256
        M = 64
        INNER = 16
        s = jnp.einsum('btd,dm->btm', x, Win) + bin_
        h = jax.nn.relu(s[..., None] * W1 + b1)
        g = jnp.einsum('btmh,mh->btm', h, W2) + b2
        out = jnp.einsum('btm,md->btd', g, Wout) + bout
        return out

    def _L1_attn_ref(x, Wq, bq, Wk, bk, Wv, bv):
        import jax, jax.numpy as jnp
        import numpy as np
        HEADS = 16
        D_MODEL = 256
        D_K = D_MODEL // HEADS
        SEQ = 512
        BSZ = 2

        def softmax_one(x, axis):
            x = x - jnp.max(x, axis=axis, keepdims=True)
            ex = jnp.exp(x)
            return ex / (1.0 + jnp.sum(ex, axis=axis, keepdims=True))
        S, B, D = x.shape
        q = (x @ Wq.T + bq).reshape(S, B, HEADS, D_K)
        k = (x @ Wk.T + bk).reshape(S, B, HEADS, D_K)
        v = (x @ Wv.T + bv).reshape(S, B, HEADS, D_K)
        scores = jnp.einsum('ibhd,jbhd->ijbh', q, k) / np.sqrt(D_K).astype(np.float32)
        causal = jnp.tril(jnp.ones((S, S), dtype=bool))[:, :, None, None]
        scores = jnp.where(causal, scores, -jnp.inf)
        attn = softmax_one(scores, axis=1)
        out = jnp.einsum('ijbh,jbhd->ibhd', attn, v)
        return out.reshape(S, B, D)

    def _L1_ffn_ref(x, wg, w1, b1, w2, b2):
        import jax, jax.numpy as jnp
        import numpy as np
        E = 8
        K = 2
        CAP_FACTOR = 1.0
        B, S, M = x.shape
        N = B * S
        capacity = int(CAP_FACTOR * K * N // E)
        xt = x.reshape(N, M)
        logits = xt @ wg
        scores = jax.nn.softmax(logits, axis=-1)
        topv, topi = jax.lax.top_k(scores, K)
        topv = topv / jnp.sum(topv, axis=-1, keepdims=True)
        masks = jax.nn.one_hot(topi.T, E, dtype=jnp.int32)
        flat = masks.reshape(K * N, E)
        locs = jnp.cumsum(flat, axis=0) - 1
        pos = jnp.sum(locs * flat, axis=-1).reshape(K, N).T
        valid = pos < capacity
        gate = topv * valid.astype(topv.dtype)
        pos_c = jnp.where(valid, pos, 0)
        xk = xt[:, None, :] * valid[..., None].astype(xt.dtype)
        disp = jnp.zeros((E, capacity, M), xt.dtype)
        disp = disp.at[topi, pos_c].add(xk)
        h = jax.nn.relu(jnp.einsum('ecm,emh->ech', disp, w1) + b1[:, None, :])
        y = jnp.einsum('ech,ehm->ecm', h, w2) + b2[:, None, :]
        out = jnp.sum(gate[..., None] * y[topi, pos_c], axis=1)
        return out.reshape(B, S, M)
    x = L0_attn_x
    xn = _layernorm(x, axis=-1)
    s = _L0_attn_ref(xn, L0_attn_Ws, L0_attn_bs, L0_attn_Wi, L0_attn_bi, L0_attn_Wo, L0_attn_bo, L0_attn_Wg, L0_attn_bg, L0_attn_ln_w, L0_attn_ln_b, L0_attn_A)
    g = _silu(_L0_ffn_ref(xn, L0_ffn_Win, L0_ffn_bin_, L0_ffn_W1, L0_ffn_b1, L0_ffn_W2, L0_ffn_b2, L0_ffn_Wout, L0_ffn_bout))
    x = x + s * g
    xn = _layernorm(x, axis=-1)
    s = _L1_attn_ref(xn, L1_attn_Wq, L1_attn_bq, L1_attn_Wk, L1_attn_bk, L1_attn_Wv, L1_attn_bv)
    g = _silu(_L1_ffn_ref(xn, L1_ffn_wg, L1_ffn_w1, L1_ffn_b1, L1_ffn_w2, L1_ffn_b2))
    x = x + s * g
    return x

_drawn_inputs = setup_inputs


def setup_inputs(seed=0):
    import zlib

    import numpy as np

    out = dict(_drawn_inputs(seed))
    spreads = {'L0_attn_ln_w': (1.0, 0.6),
     'L0_attn_ln_b': (0.0, 0.8),
     'L1_attn_bq': (0.0, 0.8),
     'L1_attn_bk': (0.0, 2.0),
     'L1_attn_bv': (0.0, 0.8),
     'L1_ffn_b1': (0.0, 0.8),
     'L1_ffn_b2': (0.0, 0.497)}
    factors = {'L0_attn_Ws': 4.208,
     'L0_attn_bs': 24.391,
     'L0_attn_Wi': 4.156,
     'L0_attn_bi': 21.348,
     'L0_attn_Wo': 2.969,
     'L0_attn_bo': 6.363,
     'L0_attn_Wg': 8.0,
     'L0_attn_bg': 35.819,
     'L0_attn_A': 23.9,
     'L0_ffn_bin_': 8.0,
     'L1_attn_Wq': 4.727,
     'L1_attn_Wk': 4.678,
     'L1_ffn_w1': 2.933}
    for name, (base, spread) in spreads.items():
        noise = np.random.default_rng([zlib.crc32(name.encode()), seed]).standard_normal(out[name].shape)
        drawn = base * np.exp(spread * noise) if base else spread * noise
        out[name] = jnp.asarray(drawn.astype(out[name].dtype))
    for name, factor in factors.items():
        out[name] = (out[name] * factor).astype(out[name].dtype)
    return out
```

```python
from contextlib import ExitStack

import concourse.bass as bass
from concourse import mybir

P = 128
B, S, D = 4, 2048, 256
KD = D // P
N = B * S
NT = S // P
M, INNER = 64, 16
NR = INNER // 2
NS = 16
GRP = 32
L = 32
NCH = S // L
CPT = P // L
BANK = 512
H, DK = 16, 16
E, TOPK = 8, 2
HID = 1024
HT = HID // P
CAP = TOPK * N // E
NG = N // P
BLK = 4
GRPS = CAP // (BLK * P)
EPS = 1e-5
SAT = 30.0

F32 = mybir.dt.float32
I32 = mybir.dt.int32
ALU = mybir.AluOpType
ACT = mybir.ActivationFunctionType
AX = mybir.AxisListType

C_ID, C_UP, C_ONE, C_IOTA, C_P, C_SAT, C_E = 0, P, 2 * P, 3 * P, 4 * P, 4 * P + 1, 4 * P + 2
C_G = C_E + E
C_ALL = C_G + TOPK * NG


def constants():
    import numpy as np
    c = np.zeros((P, C_ALL), np.float32)
    c[:, C_ID:C_ID + P] = np.eye(P)
    c[:, C_UP:C_UP + P] = np.triu(np.ones((P, P)), 1)
    c[:, C_ONE:C_ONE + P] = 1
    c[:, C_IOTA:C_IOTA + P] = np.arange(P)
    c[:, C_P] = np.arange(P)
    c[NS::GRP, C_SAT] = SAT
    c[:, C_E:C_E + E] = np.arange(E)
    c[:, C_G:] = (np.arange(TOPK * NG) * P)[None, :] + np.arange(P)[:, None] + 1
    return c


class Shared:
    pass


def program(nc, args):
    v = Shared()
    (v.consts, v.x, v.Ws, v.bs, v.Wi, v.bi, v.Wo, v.bo, v.Wg, v.bg, v.ln_w, v.ln_b, v.A, v.Win, v.bin_, v.W1, v.b1,
     v.W2, v.b2, v.Wout, v.bout, v.Wq, v.bq, v.Wk, v.bk, v.Wv, v.bv, v.wg, v.ew1, v.eb1, v.ew2, v.eb2, v.out) = args
    v.xn3_dram = nc.dram_tensor("xn3_rows", [N, D], F32, kind="Internal").ap()
    v.y_dram = nc.dram_tensor("expert_rows", [TOPK * N, D], F32, kind="Internal").ap()

    stack = ExitStack()
    with stack:
        def sb(name, shape, dt=F32, at=stack):
            return at.enter_context(nc.sbuf_tensor(name, shape, dt))

        v.sem = lambda name: stack.enter_context(nc.semaphore(name))

        v.cst = sb("cst", [P, C_ALL])
        v.ident = v.cst[:, C_ID:C_ID + P]
        v.ones = v.cst[:, C_ONE:C_ONE + P]
        v.iota = v.cst[:, C_IOTA:C_IOTA + P]
        v.prod_st = sb("prod_st", [P, NT, B * D])
        v.x_st = sb("x_st", [P, NT, B * D])
        v.logit_st = sb("logit_st", [P, B, NT, E])
        v.b1t = sb("b1t", [P, E * HT])
        front = stack.enter_context(ExitStack())
        v.wqkv = sb("wqkv", [P, KD, 3 * D], at=front)
        v.bqkv = sb("bqkv", [P, 3, D], at=front)
        v.wgr = sb("wgr", [P, KD, E], at=front)
        v.wo_pad = sb("wo_pad", [P, B, D], at=front)
        v.h_st = sb("h_st", [P, L, NCH], at=front)
        early = stack.enter_context(ExitStack())
        v.wu = sb("wu", [P, KD, P], at=early)
        v.u_bias = sb("u_bias", [P, 1], at=early)
        v.wgate = sb("wgate", [P, KD, D], at=early)
        v.bgate = sb("bgate", [P, D], at=early)
        v.win2 = sb("win2", [P, KD, P], at=early)
        v.bin2 = sb("bin2", [P, 1], at=early)
        v.w1c = sb("w1c", [P, NR], at=early)
        v.nb1c = sb("nb1c", [P, NR], at=early)
        v.dsum = sb("dsum", [P, NR, M], at=early)
        v.gconst = sb("gconst", [M, 1], at=early)
        v.woa = sb("woa", [M + 1, D], at=early)
        v.at_blk = sb("at_blk", [P, P], at=early)
        v.u_st = sb("u_st", [P, L, NCH], at=early)

        prepare(nc, v)
        mix(nc, v)
        recur(nc, v)
        early.close()
        attend(nc, v)
        front.close()
        with ExitStack() as back:
            v.idx = sb("idx", [P, E * CAP // P + 2 * BLK], I32, at=back)
            v.dst = sb("dst", [P, E * CAP // P + 2 * BLK], I32, at=back)
            v.gate = sb("gate", [P, E * CAP // P + 2 * BLK], at=back)
            route(nc, v)
            experts(nc, v)
        combine(nc, v)


def prepare(nc, v):
    ident, cst = v.ident, v.cst
    with ExitStack() as c:
        def sb(name, shape, dt=F32):
            return c.enter_context(nc.sbuf_tensor(name, shape, dt))

        def psum(name, shape):
            return c.enter_context(nc.psum_tensor(name, shape, F32))

        sem = v.sem
        rs = sb("p_rs", [P, D])
        ri = sb("p_ri", [P, D])
        ra = sb("p_ra", [P, P])
        woc = sb("p_woc", [P, KD, NS + 1])
        wop = sb("p_wop", [P, KD, P])
        wot = sb("p_wot", [P, D])
        big = sb("p_big", [P, 4, KD, D])
        win = sb("p_win", [P, KD, M])
        w2c = sb("p_w2c", [P, NR])
        b1c = sb("p_b1c", [P, NR])
        sel = sb("p_sel", [P, M])
        wb = sb("p_wb", [P, NR])
        wbs = sb("p_wbs", [P, 1])
        b2f = sb("p_b2f", [M, 1])
        lnwb = sb("p_lnwb", [P, 2, KD])
        lnb_b = sb("p_lnb_b", [P, KD, P])
        bsi = sb("p_bsi", [P, 2])
        b1r = sb("p_b1r", [E * HT, P])
        wu_raw = sb("p_wu_raw", [P, KD, P])
        zero = sb("p_zero", [P, 8 * D])
        ps = [psum(f"p_ps{n}", [P, BANK]) for n in range(8)]

        cleared = sem("p_cleared")
        loaded = sem("p_loaded")
        tables = sem("p_tables")
        zeroed = sem("p_zeroed")
        chain = sem("p_chain")
        turned = sem("p_turned")
        taken = sem("p_taken")

        loads = []

        def load(dst, src):
            loads.append((dst, src))

        load(cst[:, :], v.consts)
        for g in range(B):
            r = slice(GRP * g, GRP * g + NS)
            load(rs[r, :], v.Ws)
            load(ri[r, :], v.Wi)
            load(ra[r, GRP * g:GRP * g + NS], v.A)
            load(bsi[r, 0:1], v.bs.unsqueeze(1))
            load(bsi[r, 1:2], v.bi.unsqueeze(1))
        for k in range(KD):
            load(woc[:, k, 0:NS], v.Wo[k * P:(k + 1) * P, :])
            load(woc[:, k, NS:NS + 1], v.bo[k * P:(k + 1) * P].unsqueeze(1))
            load(lnwb[:, 0, k:k + 1], v.ln_w[k * P:(k + 1) * P].unsqueeze(1))
            load(lnwb[:, 1, k:k + 1], v.ln_b[k * P:(k + 1) * P].unsqueeze(1))
        for n, w in enumerate((v.Wg, v.Wq, v.Wk, v.Wv)):
            load(big[:, n, :, :], w.rearrange("(k p) d -> p k d", p=P))
        load(win[:, :, :], v.Win.rearrange("(k p) m -> p k m", p=P))
        load(v.wgr[:, :, :], v.wg.rearrange("(k p) e -> p k e", p=P))
        for j in range(2):
            r = slice(M * j, M * j + M)
            load(v.w1c[r, :], v.W1[:, NR * j:NR * j + NR])
            load(b1c[r, :], v.b1[:, NR * j:NR * j + NR])
            load(w2c[r, :], v.W2[:, NR * j:NR * j + NR])
            load(v.bin2[r, :], v.bin_.unsqueeze(1))
        load(b2f[:, :], v.b2.unsqueeze(1))
        load(v.woa[0:M, :], v.Wout)
        load(v.woa[M:M + 1, :], v.bout.unsqueeze(0))
        load(v.bgate[:, :], v.bg.partition_broadcast(P))
        for n, w in enumerate((v.bq, v.bk, v.bv)):
            load(v.bqkv[:, n, :], w.partition_broadcast(P))
        load(b1r[:, :], v.eb1.rearrange("e (t p) -> (e t) p", p=P))

        NCLEAR = 6

        with nc.Block() as block:
            @block.gpsimd
            def _(pool):
                for n, t in enumerate((rs, ri, ra, bsi, v.wo_pad, zero)):
                    pool.memset(t[:], 0.0).then_inc(cleared, 1)
                    pool.wait_ge(cleared, n + 1)

            @block.sync
            def _(sp):
                sp.wait_ge(cleared, NCLEAR)
                for dst, src in loads:
                    sp.dma_start(dst, src).then_inc(loaded, 16)
                sp.wait_ge(loaded, 16 * len(loads))

            @block.scalar
            def _(act):
                act.wait_ge(cleared, NCLEAR)
                for b in range(B):
                    act.dma_start(v.x_st[:, :, b * D:(b + 1) * D],
                                  v.x[b].rearrange("(t p) d -> p t d", p=P)).then_inc(tables, 16)
                rows = TOPK * N // 16
                for n in range(16):
                    act.dma_start(v.y_dram[n * rows:(n + 1) * rows, :].rearrange("(p r) d -> p (r d)", p=P),
                                  zero[:, :]).then_inc(zeroed, 16)
                act.wait_ge(tables, 16 * B)
                act.wait_ge(zeroed, 16 * 16)

            @block.tensor
            def _(pe):
                pe.wait_ge(loaded, 16 * len(loads))
                for n, m in enumerate((1, 2, 3, 0)):
                    for kd in range(KD):
                        if n >= 2:
                            pe.wait_ge(taken, 2 * (n - 2) + kd + 1)
                        for ke in range(KD):
                            last = pe.transpose(ps[2 * (n % 2) + kd][:, ke * P:(ke + 1) * P],
                                                big[:, m, ke, kd * P:(kd + 1) * P], ident)
                        last.then_inc(turned, 1)
                pe.wait_ge(chain, 1)
                for k in range(KD):
                    last = pe.transpose(ps[4][:, k * P:(k + 1) * P], rs[:, k * P:(k + 1) * P], ident)
                last.then_inc(turned, 1)
                pe.transpose(ps[5][:, 0:P], ra[:, :], ident).then_inc(turned, 1)
                pe.wait_ge(chain, 2)
                for k in range(KD):
                    last = pe.transpose(ps[6][:, k * P:(k + 1) * P], wop[:, k, :], ident)
                last.then_inc(turned, 1)
                pe.transpose(ps[7][:, 0:E * HT], b1r[:, :], ident[0:E * HT, 0:E * HT]).then_inc(turned, 1)
                pe.wait_ge(chain, 3)
                pe.wait_ge(taken, 8)
                for k in range(KD):
                    last = pe.matmul(ps[0][:, 0:1], wu_raw[:, k, :], lnwb[:, 1, k:k + 1],
                                     start=(k == 0), stop=(k == KD - 1))
                last.then_inc(turned, 1)
                for k in range(KD):
                    last = pe.matmul(ps[1][:, 0:D], lnb_b[:, k, :], v.wgate[:, k, :],
                                     start=(k == 0), stop=(k == KD - 1))
                last.then_inc(turned, 1)
                pe.matmul(ps[2][0:M, 0:1], sel[:, :], wbs[:, :], start=True, stop=True).then_inc(turned, 1)

            @block.vector
            def _(dve):
                dve.wait_ge(cleared, NCLEAR)
                dve.wait_ge(loaded, 16 * len(loads))
                dve.tensor_tensor(rs[:, :], rs[:, :], ri[:, :], ALU.add).then_inc(chain, 1)
                link = sem("p_link")
                done = [0]

                def linked(ins):
                    done[0] += 1
                    ins.then_inc(link, 1)
                    dve.wait_ge(link, done[0])

                linked(dve.memset(wop[:, :, :], 0.0))
                for g in range(B):
                    last = dve.tensor_scalar(wop[:, :, GRP * g:GRP * g + NS + 1], woc[:, :, :], 0.5, None, ALU.mult)
                last.then_inc(chain, 1)
                linked(dve.tensor_tensor(sel[:, :], ident[:, 0:M], ident[:, M:2 * M], ALU.add))
                for r in range(NR):
                    dve.tensor_scalar(v.dsum[:, r, :], sel[:, :], w2c[:, r:r + 1], None, ALU.mult)
                linked(dve.tensor_tensor(wb[:, :], w2c[:, :], b1c[:, :], ALU.mult))
                linked(dve.tensor_reduce(wbs[:, :], wb[:, :], AX.X, ALU.add))
                dve.tensor_scalar(v.nb1c[:, :], b1c[:, :], -1.0, None, ALU.mult)
                for j in range(2):
                    dve.tensor_copy(v.win2[:, :, j * M:(j + 1) * M], win[:, :, :])
                for k in range(KD):
                    dve.tensor_scalar(lnb_b[:, k, :], v.ones, lnwb[:, 1, k:k + 1], None, ALU.mult)
                linked(dve.tensor_scalar(v.bqkv[:, 0, :], v.bqkv[:, 0, :], DK ** -0.5, None, ALU.mult))
                for n in range(4):
                    for kd in range(KD):
                        dve.wait_ge(turned, 2 * n + kd + 1)
                        src = ps[2 * (n % 2) + kd][:, 0:D]
                        if n == 3:
                            ins = dve.tensor_copy(v.wgate[:, kd, :], src)
                        else:
                            ins = dve.tensor_scalar(v.wqkv[:, kd, n * D:(n + 1) * D], src,
                                                    DK ** -0.5 if n == 0 else 1.0, None, ALU.mult)
                        ins.then_inc(taken, 1)
                dve.wait_ge(turned, 9)
                for k in range(KD):
                    dve.tensor_copy(wu_raw[:, k, :], ps[4][:, k * P:(k + 1) * P])
                    last = dve.tensor_scalar(v.wu[:, k, :], ps[4][:, k * P:(k + 1) * P], lnwb[:, 0, k:k + 1],
                                             None, ALU.mult)
                last.then_inc(chain, 1)
                dve.wait_ge(turned, 10)
                dve.tensor_copy(v.at_blk[:, :], ps[5][:, 0:P])
                dve.wait_ge(turned, 11)
                linked(dve.tensor_copy(wot[:, :], ps[6][:, 0:D]))
                for g in range(B):
                    r = slice(GRP * g, GRP * g + GRP)
                    linked(dve.tensor_copy(v.wo_pad[r, g, :], wot[r, :]))
                dve.wait_ge(turned, 12)
                dve.tensor_copy(v.b1t[:, :], ps[7][:, 0:E * HT])
                dve.wait_ge(turned, 13)
                linked(dve.scalar_tensor_tensor(v.u_bias[:, :], ps[0][:, 0:1], bsi[:, 0:1], bsi[:, 1:2],
                                                ALU.add, ALU.add))
                linked(dve.tensor_tensor(v.u_bias[:, :], v.u_bias[:, :], cst[:, C_SAT:C_SAT + 1], ALU.add))
                dve.wait_ge(turned, 14)
                dve.tensor_tensor(v.bgate[:, :], v.bgate[:, :], ps[1][:, 0:D], ALU.add)
                for k in range(KD):
                    dve.tensor_scalar(v.wgate[:, k, :], v.wgate[:, k, :], lnwb[:, 0, k:k + 1], None, ALU.mult)
                dve.wait_ge(turned, 15)
                linked(dve.tensor_tensor(v.gconst[:, :], ps[2][0:M, 0:1], b2f[:, :], ALU.add))


def pairs(eng, body):
    with eng.Fori(0, NT // 2 - 1) as i:
        for u in range(2):
            body(i, u, True, True)
    for u in range(2):
        body(NT // 2 - 1, u, u == 0, False)


def mix(nc, v):
    ident = v.ident
    with ExitStack() as c:
        def sb(name, shape, dt=F32):
            return c.enter_context(nc.sbuf_tensor(name, shape, dt))

        def psum(name, shape):
            return c.enter_context(nc.psum_tensor(name, shape, F32))

        sem = v.sem
        NHID = 4
        xn = [sb(f"a_xn{n}", [P, B, D]) for n in range(2)]
        x2 = sb("a_x2", [P, B, D])
        xnT = sb("a_xnT", [P, KD, BANK])
        x2T = sb("a_x2T", [P, KD, BANK])
        hid = [sb(f"a_hid{n}", [P, BANK]) for n in range(NHID)]
        s2 = sb("a_s2", [P, BANK])
        gT = sb("a_gT", [M + 1, BANK])
        sf = sb("a_sf", [P, B * D])
        st = sb("a_st", [P, B, 6])
        mv = sb("a_mv", [P, B, 2])
        r1 = sb("a_r1", [P, B])
        r12 = sb("a_r12", [P, B])
        ta = sb("a_ta", [P, B])
        mhalf = sb("a_mhalf", [P, B])
        eps = sb("a_eps", [P, B])

        pT = psum("a_pT", [P, KD, BANK])
        pS = psum("a_pS", [P, BANK])
        pGU = psum("a_pGU", [P, BANK])
        pG = psum("a_pG", [P, B, D])
        pZ = psum("a_pZ", [P, B, D])

        passed = sem("a_passed")
        open_ = sem("a_open")
        bn = sem("a_bn")
        stats = sem("a_stats")
        rchain = sem("a_rchain")
        r_ready = sem("a_r_ready")
        xn_ready = sem("a_xn_ready")
        x2_ready = sem("a_x2_ready")
        t_done = sem("a_t_done")
        t_evac = sem("a_t_evac")
        s_done = sem("a_s_done")
        s2_ready = sem("a_s2_ready")
        u_done = sem("a_u_done")
        u_evac = sem("a_u_evac")
        g_done = sem("a_g_done")
        y_ready = sem("a_y_ready")
        thy_ready = sem("a_thy_ready")
        hid_ready = sem("a_hid_ready")
        hid_used = sem("a_hid_used")
        gT_ready = sem("a_gT_ready")
        z_done = sem("a_z_done")
        sf_ready = sem("a_sf_ready")
        p_done = sem("a_p_done")
        xs_ready = sem("a_xs_ready")
        q_done = sem("a_q_done")

        with nc.Block() as block:
            @block.gpsimd
            def _(pool):
                for s in (q_done,):
                    pool.sem_inc(s, 1)
                for n, (t, value) in enumerate(((gT[M:M + 1, :], 1.0), (mhalf[:, :], -0.5), (eps[:, :], EPS))):
                    pool.memset(t, value).then_inc(open_, 1)
                    pool.wait_ge(open_, n + 1)

                def scales(t):
                    pool.wait_ge(stats, t + 1)
                    pool.tensor_tensor(ta[:, :], mv[:, :, 1], eps[:, :], ALU.add).then_inc(rchain, 1)
                    pool.wait_ge(rchain, 6 * t + 1)
                    pool.tensor_tensor(r1[:, :], ta[:, :], mhalf[:, :], ALU.pow).then_inc(rchain, 1)
                    pool.wait_ge(rchain, 6 * t + 2)
                    pool.tensor_tensor(ta[:, :], mv[:, :, 1], r1[:, :], ALU.mult).then_inc(rchain, 1)
                    pool.wait_ge(rchain, 6 * t + 3)
                    pool.tensor_tensor(ta[:, :], ta[:, :], r1[:, :], ALU.mult).then_inc(rchain, 1)
                    pool.wait_ge(rchain, 6 * t + 4)
                    pool.tensor_tensor(ta[:, :], ta[:, :], eps[:, :], ALU.add).then_inc(rchain, 1)
                    pool.wait_ge(rchain, 6 * t + 5)
                    pool.tensor_tensor(ta[:, :], ta[:, :], mhalf[:, :], ALU.pow).then_inc(rchain, 1)
                    pool.wait_ge(rchain, 6 * t + 6)
                    pool.tensor_tensor(r12[:, :], ta[:, :], r1[:, :], ALU.mult).then_inc(r_ready, 1)

                scales(0)

                def body(i, u, more, two_more):
                    t = 2 * i + u
                    if more:
                        scales(t + 1)
                    pool.wait_ge(sf_ready, t + 1 + 1)
                    xf = xn[u][:, :, :].rearrange("p b d -> p (b d)")
                    pool.tensor_tensor(xf, xf, sf[:, :], ALU.mult).then_inc(xs_ready, 1)
                    pool.wait_ge(xs_ready, t + 1)
                    pool.sem_inc(passed, 1)
                    pool.tensor_tensor(v.x_st[:, t, :], v.x_st[:, t, :], xf, ALU.add).then_inc(q_done, 1)

                pairs(pool, body)

            @block.vector
            def _(dve):
                for s in (hid_ready, p_done, y_ready):
                    dve.sem_inc(s, 1)
                def normalise(t, u, reused=True):
                    for b in range(B):
                        last = dve.bn_stats(st[:, b, :], v.x_st[:, t, b * D:(b + 1) * D])
                    last.then_inc(bn, 1)
                    dve.wait_ge(bn, t + 1)
                    dve.sem_inc(passed, 1)
                    for b in range(B):
                        last = dve.bn_aggr(mv[:, b, :], st[:, b, :])
                    last.then_inc(stats, 1)
                    dve.wait_ge(r_ready, t + 1)
                    if reused:
                        dve.wait_ge(q_done, t - 1 + 1)
                    for b in range(B):
                        last = dve.tensor_scalar(xn[u][:, b, :], v.x_st[:, t, b * D:(b + 1) * D],
                                                 mv[:, b, 0:1], r1[:, b:b + 1], ALU.subtract, ALU.mult)
                    last.then_inc(xn_ready, 1)
                    dve.wait_ge(t_done, 2 * t)
                    for b in range(B):
                        last = dve.tensor_scalar(x2[:, b, :], v.x_st[:, t, b * D:(b + 1) * D],
                                                 mv[:, b, 0:1], r12[:, b:b + 1], ALU.subtract, ALU.mult)
                    last.then_inc(x2_ready, 1)

                normalise(0, 0, reused=False)

                def body(i, u, more, two_more):
                    t = 2 * i + u
                    if more:
                        normalise(t + 1, 1 - u)
                    dve.wait_ge(u_done, t + 1)
                    dve.sem_inc(passed, 1)
                    dve.tensor_copy(v.u_st[:, :, bass.ts(t, CPT)].rearrange("p l c -> p c l"),
                                    pGU[:, 0:P].rearrange("p (c l) -> p c l", l=L)).then_inc(u_evac, 1)
                    dve.wait_ge(s2_ready, t + 1 + 1)
                    for r in range(NR):
                        dve.wait_ge(hid_used, 8 * t + max(0, r - NHID + 1) + 1)
                        dve.tensor_scalar(hid[r % NHID][:, :], s2[:, :], v.w1c[:, r:r + 1], v.nb1c[:, r:r + 1],
                                          ALU.mult, ALU.max).then_inc(hid_ready, 1)
                    dve.wait_ge(g_done, t + 1)
                    dve.sem_inc(passed, 1)
                    dve.tensor_tensor(v.prod_st[:, t, :].rearrange("p (b d) -> p b d", b=B), pG[:, :, :], v.bgate[:, :].unsqueeze(1).broadcast_to([P, B, D]),
                                      ALU.add).then_inc(y_ready, 1)
                    dve.wait_ge(thy_ready, t + 1)
                    dve.wait_ge(sf_ready, t + 1 + 1)
                    dve.scalar_tensor_tensor(v.prod_st[:, t, :], v.prod_st[:, t, :], 1.0,
                                             sf[:, :], ALU.add, ALU.mult).then_inc(p_done, 1)

                pairs(dve, body)

            @block.scalar
            def _(act):
                for s in (s2_ready, gT_ready, sf_ready):
                    act.sem_inc(s, 1)
                def evac(t):
                    act.wait_ge(t_done, 2 * t + 1)
                    act.activation(xnT[:, :, :], pT[:, :, :], ACT.Copy).then_inc(t_evac, 1)
                    act.wait_ge(t_done, 2 * t + 2)
                    act.activation(x2T[:, :, :], pT[:, :, :], ACT.Copy).then_inc(t_evac, 1)

                evac(0)

                def body(i, u, more, two_more):
                    t = 2 * i + u
                    act.wait_ge(s_done, t + 1)
                    act.wait_ge(hid_ready, 8 * t + 1)
                    act.activation(s2[:, :], pS[:, :], ACT.Identity, bias=v.bin2[:, 0:1]).then_inc(s2_ready, 1)
                    act.wait_ge(hid_used, 8 * t + 8 + 1)
                    act.wait_ge(z_done, t + 1)
                    act.activation(gT[0:M, :], pGU[0:M, :], ACT.Identity, bias=v.gconst[:, 0:1]).then_inc(gT_ready, 1)
                    if more:
                        evac(t + 1)
                    act.wait_ge(y_ready, t + 1 + 1)
                    act.sem_inc(passed, 1)
                    act.activation(v.prod_st[:, t, :], v.prod_st[:, t, :], ACT.Tanh, scale=0.5).then_inc(thy_ready, 1)
                    act.wait_ge(z_done, t + 1 + 1)
                    act.wait_ge(q_done, t + 1)
                    act.wait_ge(p_done, t + 1)
                    act.activation(sf[:, :], pZ[:, :, :].rearrange("p b d -> p (b d)"), ACT.Silu).then_inc(sf_ready, 1)

                pairs(act, body)

            @block.tensor
            def _(pe):
                for s in (hid_used, z_done):
                    pe.sem_inc(s, 1)
                pe.wait_ge(open_, 3)

                def turn(t, u):
                    pe.wait_ge(xn_ready, t + 1)
                    pe.wait_ge(t_evac, 2 * t)
                    for k in range(KD):
                        for b in range(B):
                            last = pe.transpose(pT[:, k, b * P:(b + 1) * P], xn[u][:, b, k * P:(k + 1) * P], ident)
                    last.then_inc(t_done, 1)
                    pe.wait_ge(x2_ready, t + 1)
                    pe.wait_ge(t_evac, 2 * t + 1)
                    for k in range(KD):
                        for b in range(B):
                            last = pe.transpose(pT[:, k, b * P:(b + 1) * P], x2[:, b, k * P:(k + 1) * P], ident)
                    last.then_inc(t_done, 1)

                turn(0, 0)

                def body(i, u, more, two_more):
                    t = 2 * i + u
                    pe.wait_ge(t_evac, 2 * t + 2)
                    pe.wait_ge(s2_ready, t + 1)
                    for k in range(KD):
                        last = pe.matmul(pS[:, :], v.win2[:, k, :], xnT[:, k, :], start=(k == 0), stop=(k == KD - 1))
                    last.then_inc(s_done, 1)
                    pe.wait_ge(gT_ready, t + 1)
                    for b in range(B):
                        for k in range(KD):
                            last = pe.matmul(pGU[GRP * b:GRP * b + GRP, 0:P], v.wu[:, k, GRP * b:GRP * b + GRP],
                                             x2T[:, k, b * P:(b + 1) * P], start=(k == 0), stop=(k == KD - 1))
                    last.then_inc(u_done, 1)
                    pe.wait_ge(y_ready, t + 1)
                    for b in range(B):
                        for k in range(KD):
                            last = pe.matmul(pG[:, b, :], x2T[:, k, b * P:(b + 1) * P], v.wgate[:, k, :],
                                             start=(k == 0), stop=(k == KD - 1))
                    last.then_inc(g_done, 1)
                    pe.wait_ge(u_evac, t + 1)
                    for r in range(NR):
                        pe.wait_ge(hid_ready, 8 * t + r + 1 + 1)
                        pe.matmul(pGU[0:M, :], v.dsum[:, r, :], hid[r % NHID][:, :], start=(r == 0),
                                  stop=(r == NR - 1)).then_inc(hid_used, 1)
                    if more:
                        turn(t + 1, 1 - u)
                    pe.wait_ge(gT_ready, t + 1 + 1)
                    pe.wait_ge(sf_ready, t + 1)
                    for b in range(B):
                        last = pe.matmul(pZ[:, b, :], gT[:, b * P:(b + 1) * P], v.woa[:, :], start=True, stop=True)
                    last.then_inc(z_done, 1)

                pairs(pe, body)


def recur(nc, v):
    with ExitStack() as c:
        sem = v.sem
        ends = c.enter_context(nc.sbuf_tensor("r_ends", [P, NCH], F32))
        diff = c.enter_context(nc.sbuf_tensor("r_diff", [P, NCH], F32))
        differs = c.enter_context(nc.sbuf_tensor("r_differs", [P, 1], F32))
        flag = c.enter_context(nc.sbuf_tensor("r_flag", [1, 1], I32))
        pr = c.enter_context(nc.psum_tensor("r_p", [P, L, NCH], F32))
        pf = c.enter_context(nc.psum_tensor("r_pf", [P, BANK], F32))
        STEPS = BANK // NCH

        summed = sem("r_summed")
        state = sem("r_state")
        saved = sem("r_saved")
        compared = sem("r_compared")
        counted = sem("r_counted")
        flagged = sem("r_flagged")

        with nc.Block() as block:
            @block.tensor
            def _(pe):
                def sweep(n, first=False):
                    pe.wait_ge(state, L * n)
                    for q in range(L // STEPS):
                        ins = pe.matmul(pr[:, q * STEPS:(q + 1) * STEPS, :].rearrange("p l c -> p (l c)"), v.ident,
                                        v.u_st[:, q * STEPS:(q + 1) * STEPS, :].rearrange("p l c -> p (l c)"),
                                        start=True, stop=False, skip_group_check=True)
                        if q == 0 and first:
                            ins.then_inc(summed, 1)
                        elif q == 0:
                            pe.matmul(pr[:, 0, 1:NCH], v.at_blk[:, :], v.h_st[:, L - 1, 0:NCH - 1],
                                      start=False, stop=True, skip_group_check=True).then_inc(summed, 1)
                    for l in range(1, L):
                        pe.wait_ge(state, L * n + l)
                        pe.matmul(pr[:, l, :], v.at_blk[:, :], v.h_st[:, l - 1, :],
                                  start=False, stop=True, skip_group_check=True).then_inc(summed, 1)

                sweep(0, first=True)
                sweep(1)
                pe.wait_ge(compared, 2)
                pe.matmul(pf[0:1, 0:1], differs[:, :], v.ones[:, 0:1], start=True, stop=True).then_inc(counted, 1)
                pe.wait_ge(flagged, 1)
                again = pe.value_load(flag[0:1, 0:1], min_val=0, max_val=P)
                with pe.If(again > 0):
                    with pe.Fori(2, NCH + 1) as n:
                        sweep(n)
                pe.nop()

            @block.scalar
            def _(act):
                def sweep(n):
                    for l in range(L):
                        act.wait_ge(summed, L * n + l + 1)
                        act.activation(v.h_st[:, l, :], pr[:, l, :], ACT.Tanh,
                                       bias=v.u_bias[:, 0:1]).then_inc(state, 1)

                sweep(0)
                act.wait_ge(saved, 1)
                sweep(1)
                act.wait_ge(flagged, 1)
                again = act.value_load(flag[0:1, 0:1], min_val=0, max_val=P)
                with act.If(again > 0):
                    with act.Fori(2, NCH + 1) as n:
                        sweep(n)
                act.nop()

            @block.vector
            def _(dve):
                dve.wait_ge(state, L)
                dve.tensor_copy(ends[:, :], v.h_st[:, L - 1, :]).then_inc(saved, 1)
                dve.wait_ge(saved, 1)
                dve.wait_ge(state, 2 * L)
                dve.tensor_tensor(diff[:, :], v.h_st[:, L - 1, :], ends[:, :], ALU.not_equal).then_inc(compared, 1)
                dve.wait_ge(compared, 1)
                dve.tensor_reduce(differs[:, :], diff[:, :], AX.X, ALU.max).then_inc(compared, 1)
                dve.wait_ge(counted, 1)
                dve.tensor_copy(flag[0:1, 0:1], pf[0:1, 0:1]).then_inc(flagged, 1)


def attend(nc, v):
    ident = v.ident
    NP = B * (B + 1) // 2
    PAIR0 = [0, 4, 7, 9]
    with ExitStack() as c:
        def sb(name, shape, dt=F32):
            return c.enter_context(nc.sbuf_tensor(name, shape, dt))

        def psum(name, shape):
            return c.enter_context(nc.psum_tensor(name, shape, F32))

        sem = v.sem
        hs = [sb(f"c_hs{n}", [P, CPT, L]) for n in range(2)]
        tmp = sb("c_tmp", [P, B * D])
        xn = [sb(f"c_xn{n}", [P, B, D]) for n in range(2)]
        xnT = sb("c_xnT", [P, KD, BANK])
        q = sb("c_q", [P, B, D])
        k = sb("c_k", [P, B, D])
        vv = [sb(f"c_v{n}", [P, B, D]) for n in range(2)]
        qk = sb("c_qk", [P, NP, D])
        sc = sb("c_sc", [P, B, B, H])
        ex = sb("c_ex", [P, B, B, H])
        att = [sb(f"c_att{n}", [P, B, B, H]) for n in range(2)]
        mx = sb("c_mx", [P, B * H])
        den = sb("c_den", [P, B * H])
        rden = sb("c_rden", [P, B * H])
        pv = sb("c_pv", [P, B - 1, D])
        st = sb("c_st", [P, B, 6])
        mv = sb("c_mv", [P, B, 2])
        ta = sb("c_ta", [P, B])
        r1 = sb("c_r1", [P, B])
        mhalf = sb("c_mhalf", [P, B])
        eps = sb("c_eps", [P, B])

        pT = psum("c_pT", [P, KD, BANK])
        pX = psum("c_pX", [P, B, D])
        pY = psum("c_pY", [P, B, D])
        pL = psum("c_pL", [P, BANK])

        passed = sem("c_passed")
        open_ = sem("c_open")
        masked = sem("c_masked")
        hs_ready = sem("c_hs_ready")
        o_done = sem("c_o_done")
        op_ready = sem("c_op_ready")
        x1_ready = sem("c_x1_ready")
        bn = sem("c_bn")
        stats = sem("c_stats")
        rchain = sem("c_rchain")
        r_ready = sem("c_r_ready")
        xn_ready = sem("c_xn_ready")
        xn_out = [sem(f"c_xn_out{n}") for n in range(2)]
        t_done = sem("c_t_done")
        t_evac = sem("c_t_evac")
        l_done = sem("c_l_done")
        l_evac = sem("c_l_evac")
        q_done = sem("c_q_done")
        q_evac = sem("c_q_evac")
        k_done = sem("c_k_done")
        k_evac = sem("c_k_evac")
        v_done = sem("c_v_done")
        v_evac = sem("c_v_evac")
        sm = sem("c_sm")
        ex_in = sem("c_ex_in")
        ex_out = sem("c_ex_out")
        att_ready = sem("c_att_ready")
        pv_step = sem("c_pv_step")
        SM = 8

        def spread(ap, n):
            return ap.unsqueeze(1).broadcast_to([P, n, ap.shape[1]])

        with nc.Block() as block:
            @block.sync
            def _(sp):
                for s in xn_out:
                    sp.sem_inc(s, 16)
                rows = v.xn3_dram.rearrange("(b t p) d -> t p b d", b=B, p=P)
                with sp.Fori(0, NT // 2) as i:
                    for u in range(2):
                        t = 2 * i + u
                        sp.wait_ge(xn_ready, t + 1)
                        sp.dma_start(rows[t], xn[u][:, :, :]).then_inc(xn_out[u], 16)
                for u in range(2):
                    sp.wait_ge(xn_out[u], 16 * NT // 2 + 16)

            @block.gpsimd
            def _(pool):
                for s in (pv_step,):
                    pool.sem_inc(s, 1)
                for n, (t, value) in enumerate(((mhalf[:, :], -0.5), (eps[:, :], EPS))):
                    pool.memset(t, value).then_inc(open_, 1)
                    pool.wait_ge(open_, n + 1)

                def scale(t):
                    pool.wait_ge(stats, t + 1)
                    pool.tensor_tensor(ta[:, :], mv[:, :, 1], eps[:, :], ALU.add).then_inc(rchain, 1)
                    pool.wait_ge(rchain, t + 1)
                    pool.tensor_tensor(r1[:, :], ta[:, :], mhalf[:, :], ALU.pow).then_inc(r_ready, 1)

                scale(0)

                def body(i, u, more, two_more):
                    t = 2 * i + u
                    if more:
                        scale(t + 1)
                    n = 0
                    pool.wait_ge(att_ready, t + 1)
                    for j in range(B):
                        w = B - j
                        a = att[u][:, j, j:B, :].unsqueeze(3).broadcast_to([P, w, H, DK])
                        row = vv[u][:, j, :].rearrange("p (h d) -> p h d", d=DK).unsqueeze(1).broadcast_to([P, w, H, DK])
                        o = v.prod_st[:, t, j * D:B * D]
                        part = o if j == 0 else pv[:, 0:w, :].rearrange("p i d -> p (i d)")
                        if n:
                            pool.wait_ge(pv_step, 7 * t + n + 1)
                            pool.sem_inc(passed, 1)
                        pool.tensor_tensor(part.rearrange("p (i h d) -> p i h d", i=w, h=H), a, row,
                                           ALU.mult).then_inc(pv_step, 1)
                        n += 1
                        if j:
                            pool.wait_ge(pv_step, 7 * t + n + 1)
                            pool.sem_inc(passed, 1)
                            pool.tensor_tensor(o, o, part, ALU.add).then_inc(pv_step, 1)
                            n += 1

                pairs(pool, body)

            @block.vector
            def _(dve):
                for s in (k_evac, l_evac, v_evac):
                    dve.sem_inc(s, 1)
                dve.memset(sc[:, :, :, :], -1e30).then_inc(masked, 1)
                dve.wait_ge(masked, 1)

                def layer0(t):
                    dve.wait_ge(o_done, t + 1)
                    dve.tensor_tensor(tmp[:, :], pX[:, :, :].rearrange("p b d -> p (b d)"), v.prod_st[:, t, :],
                                      ALU.mult).then_inc(op_ready, 1)
                    dve.wait_ge(op_ready, t + 1)
                    dve.tensor_tensor(v.x_st[:, t, :], tmp[:, :], v.x_st[:, t, :], ALU.add).then_inc(x1_ready, 1)
                    dve.wait_ge(x1_ready, t + 1)
                    dve.sem_inc(passed, 1)
                    for b in range(B):
                        last = dve.bn_stats(st[:, b, :], v.x_st[:, t, b * D:(b + 1) * D])
                    last.then_inc(bn, 1)
                    dve.wait_ge(bn, t + 1)
                    dve.sem_inc(passed, 1)
                    for b in range(B):
                        last = dve.bn_aggr(mv[:, b, :], st[:, b, :])
                    last.then_inc(stats, 1)

                def normalise(t, u, stores):
                    dve.wait_ge(r_ready, t + 1)
                    dve.wait_ge(xn_out[u], 16 * stores + 16)
                    for b in range(B):
                        last = dve.tensor_scalar(xn[u][:, b, :], v.x_st[:, t, b * D:(b + 1) * D],
                                                 mv[:, b, 0:1], r1[:, b:b + 1], ALU.subtract, ALU.mult)
                    last.then_inc(xn_ready, 1)

                layer0(0)
                normalise(0, 0, 0)

                def body(i, u, more, two_more):
                    t = 2 * i + u
                    if more:
                        layer0(t + 1)
                    for n, (dst, src, done, evac) in enumerate(
                            ((q, pY, q_done, q_evac), (k, pX, k_done, k_evac), (vv[u], pY, v_done, v_evac))):
                        dve.wait_ge(done, t + 1)
                        if n == 2:
                            dve.wait_ge(pv_step, 7 * (t - u) + 1)
                        dve.tensor_tensor(dst[:, :, :], src[:, :, :], spread(v.bqkv[:, n, :], B),
                                          ALU.add).then_inc(evac, 1)
                        if n == 0 and more:
                            normalise(t + 1, 1 - u, i + u)
                    dve.wait_ge(l_done, t + 1)
                    dve.sem_inc(passed, 1)
                    dve.tensor_copy(v.logit_st[:, :, t, :],
                                    pL[:, 0:B * E].rearrange("p (b e) -> p b e", e=E)).then_inc(l_evac, 1)
                    dve.wait_ge(k_evac, t + 1 + 1)
                    for j in range(B):
                        w = B - j
                        last = dve.tensor_tensor(qk[:, PAIR0[j]:PAIR0[j] + w, :], q[:, j:B, :], spread(k[:, j, :], w),
                                                 ALU.mult)
                    last.then_inc(sm, 1)
                    dve.wait_ge(sm, SM * t + 1)
                    for j in range(B):
                        w = B - j
                        last = dve.tensor_reduce(
                            sc[:, j, j:B, :].rearrange("p i h -> p (i h)"),
                            qk[:, PAIR0[j]:PAIR0[j] + w, :].rearrange("p i (h d) -> p (i h) d", d=DK), AX.X, ALU.add)
                    last.then_inc(sm, 1)
                    dve.wait_ge(sm, SM * t + 2)
                    dve.tensor_reduce(mx[:, :], sc[:, :, :, :].rearrange("p j i h -> p (i h) j"), AX.X,
                                      ALU.max).then_inc(sm, 1)
                    dve.wait_ge(sm, SM * t + 3)
                    dve.tensor_tensor(ex[:, :, :, :].rearrange("p j i h -> p j (i h)"),
                                      sc[:, :, :, :].rearrange("p j i h -> p j (i h)"), spread(mx[:, :], B),
                                      ALU.subtract).then_inc(ex_in, 1)
                    dve.wait_ge(ex_out, t + 1)
                    dve.tensor_reduce(den[:, :], ex[:, :, :, :].rearrange("p j i h -> p (i h) j"), AX.X,
                                      ALU.add).then_inc(sm, 1)
                    dve.wait_ge(sm, SM * t + 4)
                    dve.tensor_scalar(den[:, :], den[:, :], 1.0, None, ALU.add).then_inc(sm, 1)
                    dve.wait_ge(sm, SM * t + 5)
                    dve.reciprocal(rden[:, :], den[:, :]).then_inc(sm, SM - 5)
                    dve.wait_ge(sm, SM * t + SM)
                    dve.tensor_tensor(att[u][:, :, :, :].rearrange("p j i h -> p j (i h)"),
                                      ex[:, :, :, :].rearrange("p j i h -> p j (i h)"), spread(rden[:, :], B),
                                      ALU.mult).then_inc(att_ready, 1)

                pairs(dve, body)

            @block.scalar
            def _(act):
                def states(t, u, reused=True):
                    if reused:
                        act.wait_ge(o_done, t - 1)
                        act.sem_inc(passed, 1)
                    act.activation(hs[u][:, :, :], v.h_st[:, :, bass.ts(t, CPT)].rearrange("p l c -> p c l"),
                                   ACT.Copy).then_inc(hs_ready, 1)

                states(0, 0, reused=False)
                states(1, 1, reused=False)

                def body(i, u, more, two_more):
                    t = 2 * i + u
                    act.wait_ge(t_done, t + 1)
                    act.activation(xnT[:, :, :], pT[:, :, :], ACT.Copy).then_inc(t_evac, 1)
                    if two_more:
                        states(t + 2, u)
                    act.wait_ge(ex_in, t + 1)
                    act.activation(ex[:, :, :, :], ex[:, :, :, :], ACT.Exp).then_inc(ex_out, 1)

                pairs(act, body)

            @block.tensor
            def _(pe):
                def output(t, u, reused=True):
                    pe.wait_ge(hs_ready, t + 1)
                    pe.wait_ge(op_ready, t)
                    if reused:
                        pe.wait_ge(k_evac, t - 1 + 1)
                    for n in range(2):
                        last = pe.matmul(pX[:, 2 * n:2 * n + 2, :].rearrange("p b d -> p (b d)"),
                                         hs[u][:, :, :].rearrange("p c l -> p (c l)"),
                                         v.wo_pad[:, 2 * n:2 * n + 2, :].rearrange("p b d -> p (b d)"),
                                         start=True, stop=True)
                    last.then_inc(o_done, 1)

                output(0, 0, reused=False)

                def body(i, u, more, two_more):
                    t = 2 * i + u
                    if more:
                        output(t + 1, 1 - u)
                    pe.wait_ge(xn_ready, t + 1)
                    for kk in range(KD):
                        for b in range(B):
                            last = pe.transpose(pT[:, kk, b * P:(b + 1) * P], xn[u][:, b, kk * P:(kk + 1) * P], ident)
                    last.then_inc(t_done, 1)
                    pe.wait_ge(t_evac, t + 1)
                    pe.wait_ge(l_evac, t + 1)
                    for b in range(B):
                        for kk in range(KD):
                            last = pe.matmul(pL[:, b * E:(b + 1) * E], xnT[:, kk, b * P:(b + 1) * P], v.wgr[:, kk, :],
                                             start=(kk == 0), stop=(kk == KD - 1))
                    last.then_inc(l_done, 1)
                    for n, (dst, done) in enumerate(((pY, q_done), (pX, k_done), (pY, v_done))):
                        if n == 0:
                            pe.wait_ge(v_evac, t + 1)
                        if n == 1:
                            pe.wait_ge(op_ready, t + 2 if more else t + 1)
                        if n == 2:
                            pe.wait_ge(q_evac, t + 1)
                        for b in range(B):
                            for kk in range(KD):
                                last = pe.matmul(dst[:, b, :], xnT[:, kk, b * P:(b + 1) * P],
                                                 v.wqkv[:, kk, n * D:(n + 1) * D], start=(kk == 0), stop=(kk == KD - 1))
                        last.then_inc(done, 1)

                pairs(pe, body)


def route(nc, v):
    W = NG * E
    K2 = TOPK * NG
    with ExitStack() as c:
        def sb(name, shape, dt=F32):
            return c.enter_context(nc.sbuf_tensor(name, shape, dt))

        sem = v.sem
        hot = sb("d_hot", [P, TOPK, NG, E])
        lg2 = sb("d_lg2", [P, NG, E])
        eq = sb("d_eq", [P, NG, E])
        best = sb("d_best", [P, TOPK, NG])
        first = sb("d_first", [P, TOPK, NG])
        total = sb("d_total", [P, E, K2])
        before = sb("d_before", [P, E, K2])
        pos = sb("d_pos", [P, TOPK, NG, E])
        loc = sb("d_loc", [P, K2])
        valid = sb("d_valid", [P, K2])
        loci = sb("d_loci", [P, K2], I32)
        lo_i = sb("d_lo_i", [P, K2], I32)
        hi_i = sb("d_hi_i", [P, K2], I32)
        lo = sb("d_lo", [P, K2])
        hi = sb("d_hi", [P, K2])
        gates = sb("d_gates", [P, TOPK, NG])
        dl = sb("d_dl", [P, NG])
        ee = sb("d_ee", [P, NG])
        ep = sb("d_ep", [P, NG])
        NB = 4
        ohl = [sb(f"d_ohl{n}", [P, P]) for n in range(NB)]
        val = [sb(f"d_val{n}", [P, 2, P]) for n in range(NB)]
        tab = sb("d_tab", [P, 2, P])
        empty = sb("d_empty", [P, P])
        t1 = sb("d_t1", [P, P])
        t2 = sb("d_t2", [P, P])
        zero = sb("d_zero", [P, 2 * P])
        pin = c.enter_context(nc.psum_tensor("d_pin", [P, TOPK, BANK], F32))
        ptot = c.enter_context(nc.psum_tensor("d_ptot", [P, TOPK, BANK], F32))
        ptab = c.enter_context(nc.psum_tensor("d_ptab", [P, BANK], F32))

        link = sem("d_link")
        hot_ready = sem("d_hot_ready")
        counts = sem("d_counts")
        e_in = sem("d_e_in")
        e_out = sem("d_e_out")
        one_ready = sem("d_one_ready")
        one_used = [sem(f"d_one_used{n}") for n in range(NB)]
        table = sem("d_table")
        lg = v.logit_st[:, :, :, :].rearrange("p b t e -> p (b t) e")
        expert = v.cst[:, C_E:C_E + E].unsqueeze(1).broadcast_to([P, NG, E])

        def each(ap):
            return ap.unsqueeze(2).broadcast_to([P, NG, E])

        with nc.Block() as block:
            @block.vector
            def _(dve):
                done = [0]

                def linked(ins):
                    done[0] += 1
                    ins.then_inc(link, 1)
                    dve.wait_ge(link, done[0])

                linked(dve.memset(zero[:, :], 0.0))
                for t in (v.idx, v.dst, v.gate):
                    dve.memset(t[:, E * CAP // P:], 0)
                for k in range(TOPK):
                    src = lg if k == 0 else lg2[:, :, :]
                    linked(dve.tensor_reduce(best[:, k, :], src, AX.X, ALU.max))
                    linked(dve.tensor_tensor(eq[:, :, :], src, each(best[:, k, :]), ALU.is_equal))
                    linked(dve.scalar_tensor_tensor(eq[:, :, :], expert, float(-E), eq[:, :, :], ALU.add, ALU.mult))
                    linked(dve.tensor_reduce(first[:, k, :], eq[:, :, :], AX.X, ALU.min))
                    linked(dve.tensor_scalar(first[:, k, :], first[:, k, :], float(E), None, ALU.add))
                    ins = dve.tensor_tensor(hot[:, k, :, :], expert, each(first[:, k, :]), ALU.is_equal)
                    ins.then_inc(hot_ready, 1)
                    dve.wait_ge(hot_ready, k + 1)
                    if k == 0:
                        linked(dve.scalar_tensor_tensor(lg2[:, :, :], hot[:, 0, :, :], -1e30, lg, ALU.mult, ALU.add))
                dve.tensor_tensor(dl[:, :], best[:, 1, :], best[:, 0, :], ALU.subtract).then_inc(e_in, 1)
                dve.wait_ge(e_out, 1)
                linked(dve.tensor_scalar(ep[:, :], ee[:, :], 1.0, None, ALU.add))
                linked(dve.reciprocal(gates[:, 0, :], ep[:, :]))
                linked(dve.tensor_tensor(gates[:, 1, :], ee[:, :], gates[:, 0, :], ALU.mult))
                dve.wait_ge(counts, 2)
                for k in range(TOPK):
                    linked(dve.tensor_copy(total[:, :, k * NG:(k + 1) * NG],
                                           ptot[:, k, :].rearrange("p (g e) -> p e g", e=E)))
                for e in range(E):
                    linked(dve.tensor_tensor_scan(before[:, e, :], total[:, e, :], zero[:, 0:K2], 0.0,
                                                  ALU.add, ALU.add))
                linked(dve.tensor_tensor(before[:, :, :], before[:, :, :], total[:, :, :], ALU.subtract))
                for k in range(TOPK):
                    linked(dve.tensor_tensor(pos[:, k, :, :], pin[:, k, :].rearrange("p (g e) -> p g e", e=E),
                                             before[:, :, k * NG:(k + 1) * NG].rearrange("p e g -> p g e"), ALU.add))
                linked(dve.tensor_tensor(pos[:, :, :, :], pos[:, :, :, :], hot[:, :, :, :], ALU.mult))
                linked(dve.tensor_reduce(loc[:, :], pos[:, :, :, :].rearrange("p k g e -> p (k g) e"), AX.X, ALU.add))
                linked(dve.tensor_scalar(valid[:, :], loc[:, :], float(CAP), None, ALU.is_lt))
                linked(dve.tensor_copy(loci[:, :], loc[:, :]))
                dve.tensor_scalar(lo_i[:, :], loci[:, :], P - 1, None, ALU.bitwise_and)
                linked(dve.tensor_scalar(hi_i[:, :], loci[:, :], 7, None, ALU.logical_shift_right))
                dve.tensor_copy(lo[:, :], lo_i[:, :])
                linked(dve.tensor_copy(hi[:, :], hi_i[:, :]))
                linked(dve.scalar_tensor_tensor(hi[:, :], first[:, :, :].rearrange("p k g -> p (k g)"),
                                                float(CAP // P), hi[:, :], ALU.mult, ALU.add))
                linked(dve.scalar_tensor_tensor(hi[:, :], hi[:, :], 1.0, valid[:, :], ALU.add, ALU.mult))
                linked(dve.tensor_scalar(hi[:, :], hi[:, :], -1.0, None, ALU.add))
                gat = gates[:, :, :].rearrange("p k g -> p (k g)")
                with dve.Fori(0, K2 // NB) as i:
                    for u in range(NB):
                        n = NB * i + u
                        dve.wait_ge(one_used[u], i + 1)
                        dve.wait_ge(link, done[0])
                        dve.tensor_scalar(ohl[u][:, :], v.iota, lo[:, bass.ds(n, 1)], None, ALU.is_equal)
                        dve.tensor_scalar(val[u][:, 0, :], v.iota, hi[:, bass.ds(n, 1)],
                                          v.cst[:, bass.ds(C_G + n, 1)], ALU.is_equal, ALU.mult)
                        dve.tensor_scalar(val[u][:, 1, :], v.iota, hi[:, bass.ds(n, 1)], gat[:, bass.ds(n, 1)],
                                          ALU.is_equal, ALU.mult).then_inc(one_ready, 1)
                dve.wait_ge(table, 1)
                linked(dve.tensor_copy(tab[:, :, :], ptab[:, 0:2 * P].rearrange("p (a b) -> p a b", a=2)))
                dve.tensor_copy(v.gate[:, 0:P], tab[:, 1, :])
                linked(dve.tensor_scalar(empty[:, :], tab[:, 0, :], 0.0, None, ALU.is_equal))
                linked(dve.scalar_tensor_tensor(t1[:, :], empty[:, :], float(TOPK * N + 1), tab[:, 0, :],
                                                ALU.mult, ALU.add))
                dve.tensor_scalar(v.dst[:, 0:P], t1[:, :], -1.0, None, ALU.add)
                linked(dve.tensor_scalar(t2[:, :], tab[:, 0, :], float(N), float(-N), ALU.is_gt, ALU.mult))
                linked(dve.scalar_tensor_tensor(t2[:, :], t2[:, :], -1.0, tab[:, 0, :], ALU.add, ALU.add))
                linked(dve.tensor_scalar(v.idx[:, 0:P], t2[:, :], 0.0, None, ALU.max))

            @block.scalar
            def _(act):
                act.wait_ge(e_in, 1)
                act.activation(ee[:, :], dl[:, :], ACT.Exp).then_inc(e_out, 1)

            @block.tensor
            def _(pe):
                for s in one_used:
                    pe.sem_inc(s, 1)
                for k in range(TOPK):
                    pe.wait_ge(hot_ready, k + 1)
                    oh = hot[:, k, :, :].rearrange("p g e -> p (g e)")
                    pe.matmul(pin[:, k, :], v.cst[:, C_UP:C_UP + P], oh, start=True, stop=True)
                    pe.matmul(ptot[:, k, :], v.ones, oh, start=True, stop=True).then_inc(counts, 1)
                pe.wait_ge(link, 1)
                pe.matmul(ptab[:, 0:2 * P], v.ident, zero[:, :], start=True, stop=False, skip_group_check=True)
                with pe.Fori(0, K2 // NB) as i:
                    for u in range(NB):
                        pe.wait_ge(one_ready, NB * i + u + 1)
                        pe.matmul(ptab[:, 0:2 * P], ohl[u][:, :], val[u][:, :, :].rearrange("p a b -> p (a b)"),
                                  start=False, stop=False, skip_group_check=True).then_inc(one_used[u], 1)
                pe.matmul(ptab[:, 0:2 * P], v.ident, zero[:, :], start=False, stop=True,
                          skip_group_check=True).then_inc(table, 1)


def experts(nc, v):
    with ExitStack() as c:
        def sb(name, shape, dt=F32):
            return c.enter_context(nc.sbuf_tensor(name, shape, dt))

        def psum(name, shape):
            return c.enter_context(nc.psum_tensor(name, shape, F32))

        sem = v.sem
        W = BLK * P
        w1 = [sb(f"e_w1{n}", [P, KD, HID]) for n in range(2)]
        w2 = [sb(f"e_w2{n}", [P, HT, D]) for n in range(2)]
        b1c = [sb(f"e_b1c{n}", [P, HT]) for n in range(2)]
        b2b = [sb(f"e_b2b{n}", [P, D]) for n in range(2)]
        icol = [sb(f"e_icol{n}", [P, BLK], I32) for n in range(2)]
        dcol = [sb(f"e_dcol{n}", [P, BLK], I32) for n in range(2)]
        gcol = [sb(f"e_gcol{n}", [P, BLK]) for n in range(2)]
        xg = [sb(f"e_xg{n}", [P, BLK, D]) for n in range(2)]
        xgT = sb("e_xgT", [P, KD, W])
        hid = sb("e_hid", [P, HT, W])
        yo = [sb(f"e_yo{n}", [P, BLK, D]) for n in range(2)]

        pT = psum("e_pT", [P, KD, BANK])
        pH = [psum(f"e_pH{n}", [P, BANK]) for n in range(2)]
        pY = [psum(f"e_pY{n}", [P, BLK, D]) for n in range(2)]

        passed = sem("e_passed")
        ready = sem("e_ready")
        w_in = [sem(f"e_w_in{n}") for n in range(2)]
        b1_ready = sem("e_b1_ready")
        cols = sem("e_cols")
        x_in = [sem(f"e_x_in{n}") for n in range(2)]
        t_done = sem("e_t_done")
        t_evac = sem("e_t_evac")
        h_done = sem("e_h_done")
        h_evac = sem("e_h_evac")
        y_done = sem("e_y_done")
        yb_ready = sem("e_yb_ready")
        yo_ready = sem("e_yo_ready")
        y_out = [sem(f"e_y_out{n}") for n in range(2)]
        NGR = E * GRPS

        def groups(eng, body, expert=None):
            with eng.Fori(0, E // 2) as ep:
                for eu in range(2):
                    if expert:
                        expert(ep, eu)
                    with eng.Fori(0, GRPS // 2) as gp:
                        for gu in range(2):
                            j = (2 * ep + eu) * (GRPS // 2) + gp
                            body(2 * j + gu, gu, j, eu)

        with nc.Block() as block:
            @block.sync
            def _(sp):
                w1_v = v.ew1.rearrange("e (k p) h -> e p k h", p=P)
                w2_v = v.ew2.rearrange("e (t p) d -> e p t d", p=P)

                def load(e, eu):
                    sp.dma_start(w1[eu][:, :, :], w1_v[e]).then_inc(w_in[eu], 16)
                    sp.dma_start(w2[eu][:, :, :], w2_v[e]).then_inc(w_in[eu], 16)
                    sp.dma_start(b2b[eu][:, :], v.eb2[e].partition_broadcast(P)).then_inc(w_in[eu], 16)

                load(0, 0)
                load(1, 1)
                with sp.Fori(0, E // 2 - 1) as ep:
                    for eu in range(2):
                        sp.wait_ge(yb_ready, GRPS * (2 * ep + eu + 1))
                        load(2 * ep + eu + 2, eu)

            @block.gpsimd
            def _(pool):
                pool.memset(xg[0][:, 0, 0:1], 0.0).then_inc(ready, 1)
                pool.wait_ge(ready, 1)

                def gather(n, u):
                    pool.wait_ge(cols, n + 1)
                    pool.sem_inc(passed, 1)
                    for q in range(BLK):
                        pool.indirect_dma_start(xg[u][:, q, :], None, v.xn3_dram,
                                                bass.IndirectOffsetOnAxis(icol[u][:, q:q + 1], axis=0),
                                                bounds_check=N - 1, oob_is_err=False).then_inc(x_in[u], 16)

                for u in range(2):
                    gather(u, u)
                with pool.Fori(0, NGR // 2) as i:
                    for u in range(2):
                        pool.wait_ge(yo_ready, 2 * i + u + 1)
                        pool.sem_inc(passed, 1)
                        for q in range(BLK):
                            pool.indirect_dma_start(
                                v.y_dram, bass.IndirectOffsetOnAxis(dcol[u][:, q:q + 1], axis=0), yo[u][:, q, :], None,
                                bounds_check=TOPK * N - 1, oob_is_err=False).then_inc(y_out[u], 16)
                        gather(2 * i + u + 2, u)
                for u in range(2):
                    pool.wait_ge(y_out[u], 16 * BLK * NGR // 2)
                    pool.wait_ge(x_in[u], 16 * BLK * (NGR // 2 + 1))

            @block.vector
            def _(dve):
                def columns(n, u):
                    dve.sem_inc(passed, 1)
                    sl = bass.ts(n, BLK)
                    dve.tensor_copy(icol[u][:, :], v.idx[:, sl])
                    dve.tensor_copy(dcol[u][:, :], v.dst[:, sl])
                    dve.tensor_copy(gcol[u][:, :], v.gate[:, sl]).then_inc(cols, 1)

                columns(0, 0)
                columns(1, 1)

                def expert(ep, eu):
                    dve.tensor_copy(b1c[eu][:, :], v.b1t[:, bass.ts(2 * ep + eu, HT)]).then_inc(b1_ready, 1)

                def body(n, u, j, eu):
                    dve.wait_ge(y_done, n + 1 + 1)
                    dve.tensor_tensor(yo[u][:, :, :], pY[u][:, :, :], b2b[eu][:, :].unsqueeze(1).broadcast_to([P, BLK, D]),
                                      ALU.add).then_inc(yb_ready, 1)
                    dve.wait_ge(y_out[u], 16 * BLK * (j + 1))
                    columns(n + 2, u)

                groups(dve, body, expert)

            @block.scalar
            def _(act):
                for s in (h_evac,):
                    act.sem_inc(s, 1)
                def evac(n):
                    act.wait_ge(t_done, n + 1)
                    act.activation(xgT[:, :, :], pT[:, :, :], ACT.Copy).then_inc(t_evac, 1)

                evac(0)

                def body(n, u, j, eu):
                    act.wait_ge(y_done, n + 1)
                    for h in range(HT):
                        act.wait_ge(h_done, HT * n + h + 1)
                        act.activation(hid[:, h, :], pH[h % 2][:, :], ACT.Relu,
                                       bias=b1c[eu][:, h:h + 1]).then_inc(h_evac, 1)
                    evac(n + 1)
                    act.wait_ge(yb_ready, n + 1)
                    for q in range(BLK):
                        last = act.activation(yo[u][:, q, :], yo[u][:, q, :], ACT.Copy, scale=gcol[u][:, q:q + 1])
                    last.then_inc(yo_ready, 1)

                groups(act, body, lambda ep, eu: act.wait_ge(b1_ready, 2 * ep + eu + 1))

            @block.tensor
            def _(pe):
                for s in (y_done,):
                    pe.sem_inc(s, 1)
                def turn(u, uses):
                    pe.wait_ge(x_in[u], 16 * BLK * uses)
                    for k in range(KD):
                        for q in range(BLK):
                            last = pe.transpose(pT[:, k, q * P:(q + 1) * P], xg[u][:, q, k * P:(k + 1) * P], v.ident)
                    last.then_inc(t_done, 1)

                turn(0, 1)

                def body(n, u, j, eu):
                    pe.wait_ge(t_evac, n + 1)
                    for h in range(HT):
                        pe.wait_ge(h_evac, HT * n + max(h - 1, 0) + 1)
                        for k in range(KD):
                            last = pe.matmul(pH[h % 2][:, :], w1[eu][:, k, h * P:(h + 1) * P], xgT[:, k, :],
                                             start=(k == 0), stop=(k == KD - 1))
                        last.then_inc(h_done, 1)
                    turn(1 - u, j + u + 1)
                    pe.wait_ge(h_evac, HT * n + HT + 1)
                    for q in range(BLK):
                        for h in range(HT):
                            last = pe.matmul(pY[u][:, q, :], hid[:, h, q * P:(q + 1) * P], w2[eu][:, h, :],
                                             start=(h == 0), stop=(h == HT - 1))
                    last.then_inc(y_done, 1)

                def expert(ep, eu):
                    pe.wait_ge(w_in[eu], 48 * ep + 48)
                    pe.sem_inc(passed, 1)

                groups(pe, body, expert)


def combine(nc, v):
    with ExitStack() as c:
        def sb(name, shape, dt=F32):
            return c.enter_context(nc.sbuf_tensor(name, shape, dt))

        sem = v.sem
        ya = [sb(f"f_ya{n}", [P, B * D]) for n in range(2)]
        yb = [sb(f"f_yb{n}", [P, B * D]) for n in range(2)]
        o = [sb(f"f_o{n}", [P, B * D]) for n in range(2)]
        y_in = [sem(f"f_y_in{n}") for n in range(2)]
        sum_ready = sem("f_sum_ready")
        silu_ready = sem("f_silu_ready")
        sg_ready = sem("f_sg_ready")
        o_ready = sem("f_o_ready")
        o_out = [sem(f"f_o_out{n}") for n in range(2)]

        with nc.Block() as block:
            @block.sync
            def _(sp):
                for s in o_out:
                    sp.sem_inc(s, 16)
                rows = v.y_dram.rearrange("(k b t p) d -> t k p b d", k=TOPK, b=B, p=P)
                dst = v.out.rearrange("b (t p) d -> t p b d", p=P)

                def load(t, u):
                    for k, y in enumerate((ya[u], yb[u])):
                        sp.dma_start(y[:, :].rearrange("p (b d) -> p b d", b=B), rows[t, k]).then_inc(y_in[u], 16)

                load(0, 0)
                load(1, 1)

                def body(i, u, more, two_more):
                    t = 2 * i + u
                    sp.wait_ge(o_ready, t + 1)
                    sp.dma_start(dst[t], o[u][:, :].rearrange("p (b d) -> p b d", b=B)).then_inc(o_out[u], 16)
                    if two_more:
                        load(t + 2, u)

                pairs(sp, body)
                for u in range(2):
                    sp.wait_ge(o_out[u], 16 * NT // 2 + 16)

            @block.vector
            def _(dve):
                def add(t, u, uses):
                    dve.wait_ge(y_in[u], 32 * uses)
                    dve.tensor_tensor(ya[u][:, :], ya[u][:, :], yb[u][:, :], ALU.add).then_inc(sum_ready, 1)

                add(0, 0, 1)

                def body(i, u, more, two_more):
                    t = 2 * i + u
                    if more:
                        add(t + 1, 1 - u, i + u + 1)
                    dve.wait_ge(silu_ready, t + 1)
                    dve.wait_ge(o_out[u], 16 * i + 16)
                    dve.tensor_tensor(o[u][:, :], ya[u][:, :], v.prod_st[:, t, :], ALU.mult).then_inc(sg_ready, 1)
                    dve.wait_ge(sg_ready, t + 1)
                    dve.tensor_tensor(o[u][:, :], o[u][:, :], v.x_st[:, t, :], ALU.add).then_inc(o_ready, 1)

                pairs(dve, body)

            @block.scalar
            def _(act):
                def body(i, u, more, two_more):
                    act.wait_ge(sum_ready, 2 * i + u + 1)
                    act.activation(ya[u][:, :], ya[u][:, :], ACT.Silu).then_inc(silu_ready, 1)

                pairs(act, body)


def kernel(**inputs):
    import numpy as np
    import concourse.bacc as bacc
    from concourse.bass_utils import run_bass_kernel_spmd

    nc = bacc.Bacc("TRN2", target_bir_lowering=False, num_devices=1)
    order = ["L0_attn_x", "L0_attn_Ws", "L0_attn_bs", "L0_attn_Wi", "L0_attn_bi", "L0_attn_Wo", "L0_attn_bo",
             "L0_attn_Wg", "L0_attn_bg", "L0_attn_ln_w", "L0_attn_ln_b", "L0_attn_A", "L0_ffn_Win", "L0_ffn_bin_",
             "L0_ffn_W1", "L0_ffn_b1", "L0_ffn_W2", "L0_ffn_b2", "L0_ffn_Wout", "L0_ffn_bout", "L1_attn_Wq",
             "L1_attn_bq", "L1_attn_Wk", "L1_attn_bk", "L1_attn_Wv", "L1_attn_bv", "L1_ffn_wg", "L1_ffn_w1",
             "L1_ffn_b1", "L1_ffn_w2", "L1_ffn_b2"]
    arrays = {"constants": constants()}
    for name in order:
        arrays[name] = np.ascontiguousarray(inputs[name])
    args = [nc.dram_tensor(n, a.shape, mybir.dt.from_np(a.dtype), kind="ExternalInput").ap()
            for n, a in arrays.items()]
    out = nc.dram_tensor("out", (B, S, D), F32, kind="ExternalOutput").ap()
    program(nc, [*args, out])
    r = run_bass_kernel_spmd(nc, [arrays], core_ids=[0])
    return r.results[0]["out"]
```

```python
from contextlib import ExitStack

import concourse.bass as bass
from concourse import mybir

P = 128
B, S, D = 4, 2048, 256
KD = D // P
N = B * S
NT = S // P
M, INNER = 64, 16
NR = INNER // 2
NS = 16
GRP = 32
L = 32
NCH = S // L
CPT = P // L
BANK = 512
H, DK = 16, 16
E, TOPK = 8, 2
HID = 1024
HT = HID // P
CAP = TOPK * N // E
NG = N // P
BLK = 4
GRPS = CAP // (BLK * P)
EPS = 1e-5
RANGE_LOG2 = 14
RANGE = float(1 << RANGE_LOG2)
X_SCALE = float(1 << 10)
LEAST = 2.0 ** -40
EXPONENT = 0xFF << 23
SAT = 30.0

F32 = mybir.dt.float32
I32 = mybir.dt.int32
F16 = mybir.dt.float16
BF16 = mybir.dt.bfloat16
ALU = mybir.AluOpType
ACT = mybir.ActivationFunctionType
AX = mybir.AxisListType

C_ID, C_UP, C_ONE, C_IOTA, C_P, C_SAT, C_E = 0, P, 2 * P, 3 * P, 4 * P, 4 * P + 1, 4 * P + 2
C_G = C_E + E
C_ALL = C_G + TOPK * NG


def constants():
    import numpy as np
    c = np.zeros((P, C_ALL), np.float32)
    c[:, C_ID:C_ID + P] = np.eye(P)
    c[:, C_UP:C_UP + P] = np.triu(np.ones((P, P)), 1)
    c[:, C_ONE:C_ONE + P] = 1
    c[:, C_IOTA:C_IOTA + P] = np.arange(P)
    c[:, C_P] = np.arange(P)
    c[NS::GRP, C_SAT] = SAT
    c[:, C_E:C_E + E] = np.arange(E)
    c[:, C_G:] = (np.arange(TOPK * NG) * P)[None, :] + np.arange(P)[:, None] + 1
    return c


class Shared:
    pass


def program(nc, args):
    v = Shared()
    (v.consts, v.x, v.Ws, v.bs, v.Wi, v.bi, v.Wo, v.bo, v.Wg, v.bg, v.ln_w, v.ln_b, v.A, v.Win, v.bin_, v.W1, v.b1,
     v.W2, v.b2, v.Wout, v.bout, v.Wq, v.bq, v.Wk, v.bk, v.Wv, v.bv, v.wg, v.ew1, v.eb1, v.ew2, v.eb2, v.out) = args
    v.xn3_dram = nc.dram_tensor("xn3_rows", [N, D], F32, kind="Internal").ap()
    v.y_dram = nc.dram_tensor("expert_rows", [TOPK * N, D], F32, kind="Internal").ap()

    stack = ExitStack()
    with stack:
        def sb(name, shape, dt=F32, at=stack):
            return at.enter_context(nc.sbuf_tensor(name, shape, dt))

        v.sem = lambda name: stack.enter_context(nc.semaphore(name))

        v.cst = sb("cst", [P, C_ALL])
        v.ident = v.cst[:, C_ID:C_ID + P]
        v.ones = v.cst[:, C_ONE:C_ONE + P]
        v.iota = v.cst[:, C_IOTA:C_IOTA + P]
        v.prod_st = sb("prod_st", [P, NT, B * D])
        v.x_st = sb("x_st", [P, NT, B * D])
        v.logit_st = sb("logit_st", [P, B, NT, E])
        v.b1t = sb("b1t", [P, (E + 1) * HT])
        front = stack.enter_context(ExitStack())
        v.wqkv = sb("wqkv", [P, KD, 3 * D], at=front)
        v.bqkv = sb("bqkv", [P, 3, D], at=front)
        v.wgr = sb("wgr", [P, KD, E], at=front)
        v.wo_pad = sb("wo_pad", [P, B, D], at=front)
        v.h_st = sb("h_st", [P, L, NCH], at=front)
        early = stack.enter_context(ExitStack())
        v.wu = sb("wu", [P, KD, P], at=early)
        v.u_bias = sb("u_bias", [P, 1], at=early)
        v.wgate = sb("wgate", [P, KD, D], at=early)
        v.bgate = sb("bgate", [P, D], at=early)
        v.win2 = sb("win2", [P, KD, P], at=early)
        v.bin2 = sb("bin2", [P, 1], at=early)
        v.w1c = sb("w1c", [P, NR], at=early)
        v.nb1c = sb("nb1c", [P, NR], at=early)
        v.dsum = sb("dsum", [P, NR, M], at=early)
        v.gconst = sb("gconst", [M, 1], at=early)
        v.woa = sb("woa", [M + 1, D], at=early)
        v.at_blk = sb("at_blk", [P, P], at=early)
        v.u_st = sb("u_st", [P, L, NCH], at=early)

        prepare(nc, v)
        mix(nc, v)
        recur(nc, v)
        early.close()
        attend(nc, v)
        front.close()
        with ExitStack() as back:
            v.idx = sb("idx", [P, E * CAP // P + 2 * BLK], I32, at=back)
            v.dst = sb("dst", [P, E * CAP // P + 2 * BLK], I32, at=back)
            v.gate = sb("gate", [P, E * CAP // P + 2 * BLK], at=back)
            route(nc, v)
            experts(nc, v)
        combine(nc, v)


def prepare(nc, v):
    ident, cst = v.ident, v.cst
    with ExitStack() as c:
        def sb(name, shape, dt=F32):
            return c.enter_context(nc.sbuf_tensor(name, shape, dt))

        def psum(name, shape):
            return c.enter_context(nc.psum_tensor(name, shape, F32))

        sem = v.sem
        rs = sb("p_rs", [P, D])
        ri = sb("p_ri", [P, D])
        ra = sb("p_ra", [P, P])
        woc = sb("p_woc", [P, KD, NS + 1])
        wop = sb("p_wop", [P, KD, P])
        wot = sb("p_wot", [P, D])
        big = sb("p_big", [P, 4, KD, D])
        win = sb("p_win", [P, KD, M])
        w2c = sb("p_w2c", [P, NR])
        b1c = sb("p_b1c", [P, NR])
        sel = sb("p_sel", [P, M])
        wb = sb("p_wb", [P, NR])
        wbs = sb("p_wbs", [P, 1])
        b2f = sb("p_b2f", [M, 1])
        lnwb = sb("p_lnwb", [P, 2, KD])
        lnb_b = sb("p_lnb_b", [P, KD, P])
        bsi = sb("p_bsi", [P, 2])
        b1r = sb("p_b1r", [E * HT, P])
        wu_raw = sb("p_wu_raw", [P, KD, P])
        zero = sb("p_zero", [P, 8 * D])
        ps = [psum(f"p_ps{n}", [P, BANK]) for n in range(8)]

        cleared = sem("p_cleared")
        loaded = sem("p_loaded")
        tables = sem("p_tables")
        zeroed = sem("p_zeroed")
        chain = sem("p_chain")
        turned = sem("p_turned")
        taken = sem("p_taken")

        loads = []

        def load(dst, src):
            loads.append((dst, src))

        load(cst[:, :], v.consts)
        for g in range(B):
            r = slice(GRP * g, GRP * g + NS)
            load(rs[r, :], v.Ws)
            load(ri[r, :], v.Wi)
            load(ra[r, GRP * g:GRP * g + NS], v.A)
            load(bsi[r, 0:1], v.bs.unsqueeze(1))
            load(bsi[r, 1:2], v.bi.unsqueeze(1))
        for k in range(KD):
            load(woc[:, k, 0:NS], v.Wo[k * P:(k + 1) * P, :])
            load(woc[:, k, NS:NS + 1], v.bo[k * P:(k + 1) * P].unsqueeze(1))
            load(lnwb[:, 0, k:k + 1], v.ln_w[k * P:(k + 1) * P].unsqueeze(1))
            load(lnwb[:, 1, k:k + 1], v.ln_b[k * P:(k + 1) * P].unsqueeze(1))
        for n, w in enumerate((v.Wg, v.Wq, v.Wk, v.Wv)):
            load(big[:, n, :, :], w.rearrange("(k p) d -> p k d", p=P))
        load(win[:, :, :], v.Win.rearrange("(k p) m -> p k m", p=P))
        load(v.wgr[:, :, :], v.wg.rearrange("(k p) e -> p k e", p=P))
        for j in range(2):
            r = slice(M * j, M * j + M)
            load(v.w1c[r, :], v.W1[:, NR * j:NR * j + NR])
            load(b1c[r, :], v.b1[:, NR * j:NR * j + NR])
            load(w2c[r, :], v.W2[:, NR * j:NR * j + NR])
            load(v.bin2[r, :], v.bin_.unsqueeze(1))
        load(b2f[:, :], v.b2.unsqueeze(1))
        load(v.woa[0:M, :], v.Wout)
        load(v.woa[M:M + 1, :], v.bout.unsqueeze(0))
        load(v.bgate[:, :], v.bg.partition_broadcast(P))
        for n, w in enumerate((v.bq, v.bk, v.bv)):
            load(v.bqkv[:, n, :], w.partition_broadcast(P))
        load(b1r[:, :], v.eb1.rearrange("e (t p) -> (e t) p", p=P))

        NCLEAR = 6

        with nc.Block() as block:
            @block.gpsimd
            def _(pool):
                for n, t in enumerate((rs, ri, ra, bsi, v.wo_pad, zero)):
                    pool.memset(t[:], 0.0).then_inc(cleared, 1)
                    pool.wait_ge(cleared, n + 1)

            @block.sync
            def _(sp):
                sp.wait_ge(cleared, NCLEAR)
                for dst, src in loads:
                    sp.dma_start(dst, src).then_inc(loaded, 16)
                sp.wait_ge(loaded, 16 * len(loads))

            @block.scalar
            def _(act):
                act.wait_ge(cleared, NCLEAR)
                for b in range(B):
                    act.dma_start(v.x_st[:, :, b * D:(b + 1) * D],
                                  v.x[b].rearrange("(t p) d -> p t d", p=P)).then_inc(tables, 16)
                rows = TOPK * N // 16
                for n in range(16):
                    act.dma_start(v.y_dram[n * rows:(n + 1) * rows, :].rearrange("(p r) d -> p (r d)", p=P),
                                  zero[:, :]).then_inc(zeroed, 16)
                act.wait_ge(tables, 16 * B)
                act.wait_ge(zeroed, 16 * 16)

            @block.tensor
            def _(pe):
                pe.wait_ge(loaded, 16 * len(loads))
                for n, m in enumerate((1, 2, 3, 0)):
                    for kd in range(KD):
                        if n >= 2:
                            pe.wait_ge(taken, 2 * (n - 2) + kd + 1)
                        for ke in range(KD):
                            last = pe.transpose(ps[2 * (n % 2) + kd][:, ke * P:(ke + 1) * P],
                                                big[:, m, ke, kd * P:(kd + 1) * P], ident)
                        last.then_inc(turned, 1)
                pe.wait_ge(chain, 1)
                for k in range(KD):
                    last = pe.transpose(ps[4][:, k * P:(k + 1) * P], rs[:, k * P:(k + 1) * P], ident)
                last.then_inc(turned, 1)
                pe.transpose(ps[5][:, 0:P], ra[:, :], ident).then_inc(turned, 1)
                pe.wait_ge(chain, 2)
                for k in range(KD):
                    last = pe.transpose(ps[6][:, k * P:(k + 1) * P], wop[:, k, :], ident)
                last.then_inc(turned, 1)
                pe.transpose(ps[7][:, 0:E * HT], b1r[:, :], ident[0:E * HT, 0:E * HT]).then_inc(turned, 1)
                pe.wait_ge(chain, 3)
                pe.wait_ge(taken, 8)
                for k in range(KD):
                    last = pe.matmul(ps[0][:, 0:1], wu_raw[:, k, :], lnwb[:, 1, k:k + 1],
                                     start=(k == 0), stop=(k == KD - 1))
                last.then_inc(turned, 1)
                for k in range(KD):
                    last = pe.matmul(ps[1][:, 0:D], lnb_b[:, k, :], v.wgate[:, k, :],
                                     start=(k == 0), stop=(k == KD - 1))
                last.then_inc(turned, 1)
                pe.matmul(ps[2][0:M, 0:1], sel[:, :], wbs[:, :], start=True, stop=True).then_inc(turned, 1)

            @block.vector
            def _(dve):
                dve.wait_ge(cleared, NCLEAR)
                dve.wait_ge(loaded, 16 * len(loads))
                dve.tensor_tensor(rs[:, :], rs[:, :], ri[:, :], ALU.add).then_inc(chain, 1)
                link = sem("p_link")
                done = [0]

                def linked(ins):
                    done[0] += 1
                    ins.then_inc(link, 1)
                    dve.wait_ge(link, done[0])

                linked(dve.memset(wop[:, :, :], 0.0))
                for g in range(B):
                    last = dve.tensor_scalar(wop[:, :, GRP * g:GRP * g + NS + 1], woc[:, :, :], 0.5, None, ALU.mult)
                last.then_inc(chain, 1)
                linked(dve.tensor_tensor(sel[:, :], ident[:, 0:M], ident[:, M:2 * M], ALU.add))
                for r in range(NR):
                    dve.tensor_scalar(v.dsum[:, r, :], sel[:, :], w2c[:, r:r + 1], None, ALU.mult)
                linked(dve.tensor_tensor(wb[:, :], w2c[:, :], b1c[:, :], ALU.mult))
                linked(dve.tensor_reduce(wbs[:, :], wb[:, :], AX.X, ALU.add))
                dve.tensor_scalar(v.nb1c[:, :], b1c[:, :], -1.0, None, ALU.mult)
                for j in range(2):
                    dve.tensor_copy(v.win2[:, :, j * M:(j + 1) * M], win[:, :, :])
                for k in range(KD):
                    dve.tensor_scalar(lnb_b[:, k, :], v.ones, lnwb[:, 1, k:k + 1], None, ALU.mult)
                linked(dve.tensor_scalar(v.bqkv[:, 0, :], v.bqkv[:, 0, :], DK ** -0.5, None, ALU.mult))
                for n in range(4):
                    for kd in range(KD):
                        dve.wait_ge(turned, 2 * n + kd + 1)
                        src = ps[2 * (n % 2) + kd][:, 0:D]
                        if n == 3:
                            ins = dve.tensor_copy(v.wgate[:, kd, :], src)
                        else:
                            ins = dve.tensor_scalar(v.wqkv[:, kd, n * D:(n + 1) * D], src,
                                                    DK ** -0.5 if n == 0 else 1.0, None, ALU.mult)
                        ins.then_inc(taken, 1)
                dve.wait_ge(turned, 9)
                for k in range(KD):
                    dve.tensor_copy(wu_raw[:, k, :], ps[4][:, k * P:(k + 1) * P])
                    last = dve.tensor_scalar(v.wu[:, k, :], ps[4][:, k * P:(k + 1) * P], lnwb[:, 0, k:k + 1],
                                             None, ALU.mult)
                last.then_inc(chain, 1)
                dve.wait_ge(turned, 10)
                dve.tensor_copy(v.at_blk[:, :], ps[5][:, 0:P])
                dve.wait_ge(turned, 11)
                linked(dve.tensor_copy(wot[:, :], ps[6][:, 0:D]))
                for g in range(B):
                    r = slice(GRP * g, GRP * g + GRP)
                    linked(dve.tensor_copy(v.wo_pad[r, g, :], wot[r, :]))
                dve.wait_ge(turned, 12)
                dve.tensor_copy(v.b1t[:, 0:E * HT], ps[7][:, 0:E * HT])
                dve.memset(v.b1t[:, E * HT:], 0.0)
                dve.wait_ge(turned, 13)
                linked(dve.scalar_tensor_tensor(v.u_bias[:, :], ps[0][:, 0:1], bsi[:, 0:1], bsi[:, 1:2],
                                                ALU.add, ALU.add))
                linked(dve.tensor_tensor(v.u_bias[:, :], v.u_bias[:, :], cst[:, C_SAT:C_SAT + 1], ALU.add))
                dve.wait_ge(turned, 14)
                dve.tensor_tensor(v.bgate[:, :], v.bgate[:, :], ps[1][:, 0:D], ALU.add)
                for k in range(KD):
                    dve.tensor_scalar(v.wgate[:, k, :], v.wgate[:, k, :], lnwb[:, 0, k:k + 1], None, ALU.mult)
                dve.wait_ge(turned, 15)
                linked(dve.tensor_tensor(v.gconst[:, :], ps[2][0:M, 0:1], b2f[:, :], ALU.add))


def pairs(eng, body):
    with eng.Fori(0, NT // 2 - 1) as i:
        for u in range(2):
            body(i, u, True, True)
    for u in range(2):
        body(NT // 2 - 1, u, u == 0, False)


def tiles(eng, body):
    with eng.Fori(0, NT // 2 - 2) as i:
        for u in range(2):
            body(i, u, 4)
    for i in (NT // 2 - 2, NT // 2 - 1):
        for u in range(2):
            body(i, u, NT - 1 - 2 * i - u)


def mix(nc, v):
    ident = v.ident
    with ExitStack() as c:
        def sb(name, shape, dt=F32):
            return c.enter_context(nc.sbuf_tensor(name, shape, dt))

        def psum(name, shape):
            return c.enter_context(nc.psum_tensor(name, shape, F32))

        sem = v.sem
        NHID = 4
        xn = [sb(f"a_xn{n}", [P, B, D]) for n in range(2)]
        x2 = sb("a_x2", [P, B, D])
        xnT = sb("a_xnT", [P, KD, BANK])
        x2T = sb("a_x2T", [P, KD, BANK])
        hid = [sb(f"a_hid{n}", [P, BANK]) for n in range(NHID)]
        s2 = sb("a_s2", [P, BANK])
        gT = sb("a_gT", [M + 1, BANK])
        sf = sb("a_sf", [P, B * D])
        st = sb("a_st", [P, B, 6])
        mv = sb("a_mv", [P, B, 2])
        r1 = sb("a_r1", [P, B])
        r12 = sb("a_r12", [P, B])
        ta = sb("a_ta", [P, B])
        mhalf = sb("a_mhalf", [P, B])
        eps = sb("a_eps", [P, B])

        pT = psum("a_pT", [P, KD, BANK])
        pS = psum("a_pS", [P, BANK])
        pGU = psum("a_pGU", [P, BANK])
        pG = psum("a_pG", [P, B, D])
        pZ = psum("a_pZ", [P, B, D])

        passed = sem("a_passed")
        open_ = sem("a_open")
        bn = sem("a_bn")
        stats = sem("a_stats")
        rchain = sem("a_rchain")
        r_ready = sem("a_r_ready")
        xn_ready = sem("a_xn_ready")
        x2_ready = sem("a_x2_ready")
        t_done = sem("a_t_done")
        t_evac = sem("a_t_evac")
        s_done = sem("a_s_done")
        s2_ready = sem("a_s2_ready")
        u_done = sem("a_u_done")
        u_evac = sem("a_u_evac")
        g_done = sem("a_g_done")
        y_ready = sem("a_y_ready")
        thy_ready = sem("a_thy_ready")
        hid_ready = sem("a_hid_ready")
        hid_used = sem("a_hid_used")
        gT_ready = sem("a_gT_ready")
        z_done = sem("a_z_done")
        sf_ready = sem("a_sf_ready")
        p_done = sem("a_p_done")
        xs_ready = sem("a_xs_ready")
        q_done = sem("a_q_done")

        with nc.Block() as block:
            @block.gpsimd
            def _(pool):
                for s in (q_done,):
                    pool.sem_inc(s, 1)
                for n, (t, value) in enumerate(((gT[M:M + 1, :], 1.0), (mhalf[:, :], -0.5), (eps[:, :], EPS))):
                    pool.memset(t, value).then_inc(open_, 1)
                    pool.wait_ge(open_, n + 1)

                def scales(t):
                    pool.wait_ge(stats, t + 1)
                    pool.tensor_tensor(ta[:, :], mv[:, :, 1], eps[:, :], ALU.add).then_inc(rchain, 1)
                    pool.wait_ge(rchain, 6 * t + 1)
                    pool.tensor_tensor(r1[:, :], ta[:, :], mhalf[:, :], ALU.pow).then_inc(rchain, 1)
                    pool.wait_ge(rchain, 6 * t + 2)
                    pool.tensor_tensor(ta[:, :], mv[:, :, 1], r1[:, :], ALU.mult).then_inc(rchain, 1)
                    pool.wait_ge(rchain, 6 * t + 3)
                    pool.tensor_tensor(ta[:, :], ta[:, :], r1[:, :], ALU.mult).then_inc(rchain, 1)
                    pool.wait_ge(rchain, 6 * t + 4)
                    pool.tensor_tensor(ta[:, :], ta[:, :], eps[:, :], ALU.add).then_inc(rchain, 1)
                    pool.wait_ge(rchain, 6 * t + 5)
                    pool.tensor_tensor(ta[:, :], ta[:, :], mhalf[:, :], ALU.pow).then_inc(rchain, 1)
                    pool.wait_ge(rchain, 6 * t + 6)
                    pool.tensor_tensor(r12[:, :], ta[:, :], r1[:, :], ALU.mult).then_inc(r_ready, 1)

                scales(0)

                def body(i, u, more, two_more):
                    t = 2 * i + u
                    if more:
                        scales(t + 1)
                    pool.wait_ge(sf_ready, t + 1 + 1)
                    xf = xn[u][:, :, :].rearrange("p b d -> p (b d)")
                    pool.tensor_tensor(xf, xf, sf[:, :], ALU.mult).then_inc(xs_ready, 1)
                    pool.wait_ge(xs_ready, t + 1)
                    pool.sem_inc(passed, 1)
                    pool.tensor_tensor(v.x_st[:, t, :], v.x_st[:, t, :], xf, ALU.add).then_inc(q_done, 1)

                pairs(pool, body)

            @block.vector
            def _(dve):
                for s in (hid_ready, p_done, y_ready):
                    dve.sem_inc(s, 1)
                def measure(t):
                    for b in range(B):
                        last = dve.bn_stats(st[:, b, :], v.x_st[:, t, b * D:(b + 1) * D])
                    last.then_inc(bn, 1)
                    dve.wait_ge(bn, t + 1)
                    dve.sem_inc(passed, 1)
                    for b in range(B):
                        last = dve.bn_aggr(mv[:, b, :], st[:, b, :])
                    last.then_inc(stats, 1)

                def normalise(t, u, reused=True):
                    dve.wait_ge(r_ready, t + 1)
                    if reused:
                        dve.wait_ge(q_done, t - 1 + 1)
                    for b in range(B):
                        last = dve.tensor_scalar(xn[u][:, b, :], v.x_st[:, t, b * D:(b + 1) * D],
                                                 mv[:, b, 0:1], r1[:, b:b + 1], ALU.subtract, ALU.mult)
                    last.then_inc(xn_ready, 1)
                    dve.wait_ge(t_done, 2 * t)
                    for b in range(B):
                        last = dve.tensor_scalar(x2[:, b, :], v.x_st[:, t, b * D:(b + 1) * D],
                                                 mv[:, b, 0:1], r12[:, b:b + 1], ALU.subtract, ALU.mult)
                    last.then_inc(x2_ready, 1)

                measure(0)
                normalise(0, 0, reused=False)

                def body(i, u, more, two_more):
                    t = 2 * i + u
                    if more:
                        measure(t + 1)
                    dve.wait_ge(s2_ready, t + 1 + 1)
                    for r in range(NR):
                        if r == NHID:
                            dve.wait_ge(u_done, t + 1)
                            dve.sem_inc(passed, 1)
                            dve.tensor_copy(v.u_st[:, :, bass.ts(t, CPT)].rearrange("p l c -> p c l"),
                                            pGU[:, 0:P].rearrange("p (c l) -> p c l", l=L)).then_inc(u_evac, 1)
                        dve.wait_ge(hid_used, 8 * t + max(0, r - NHID + 1) + 1)
                        dve.tensor_scalar(hid[r % NHID][:, :], s2[:, :], v.w1c[:, r:r + 1], v.nb1c[:, r:r + 1],
                                          ALU.mult, ALU.max).then_inc(hid_ready, 1)
                    if more:
                        normalise(t + 1, 1 - u)
                    dve.wait_ge(g_done, t + 1)
                    dve.sem_inc(passed, 1)
                    dve.tensor_tensor(v.prod_st[:, t, :].rearrange("p (b d) -> p b d", b=B), pG[:, :, :], v.bgate[:, :].unsqueeze(1).broadcast_to([P, B, D]),
                                      ALU.add).then_inc(y_ready, 1)
                    dve.wait_ge(thy_ready, t + 1)
                    dve.wait_ge(sf_ready, t + 1 + 1)
                    dve.scalar_tensor_tensor(v.prod_st[:, t, :], v.prod_st[:, t, :], 1.0,
                                             sf[:, :], ALU.add, ALU.mult).then_inc(p_done, 1)

                pairs(dve, body)

            @block.scalar
            def _(act):
                for s in (s2_ready, gT_ready, sf_ready):
                    act.sem_inc(s, 1)
                def evac(t, part):
                    act.wait_ge(t_done, 2 * t + part + 1)
                    act.activation((xnT, x2T)[part][:, :, :], pT[:, :, :], ACT.Copy).then_inc(t_evac, 1)

                evac(0, 0)
                evac(0, 1)

                def body(i, u, more, two_more):
                    t = 2 * i + u
                    act.wait_ge(s_done, t + 1)
                    act.wait_ge(hid_ready, 8 * t + 1)
                    act.activation(s2[:, :], pS[:, :], ACT.Identity, bias=v.bin2[:, 0:1]).then_inc(s2_ready, 1)
                    act.wait_ge(hid_used, 8 * t + 8 + 1)
                    act.wait_ge(z_done, t + 1)
                    act.activation(gT[0:M, :], pGU[0:M, :], ACT.Identity, bias=v.gconst[:, 0:1]).then_inc(gT_ready, 1)
                    if more:
                        evac(t + 1, 0)
                    act.wait_ge(y_ready, t + 1 + 1)
                    act.sem_inc(passed, 1)
                    act.activation(v.prod_st[:, t, :], v.prod_st[:, t, :], ACT.Tanh, scale=0.5).then_inc(thy_ready, 1)
                    if more:
                        evac(t + 1, 1)
                    act.wait_ge(z_done, t + 1 + 1)
                    act.wait_ge(q_done, t + 1)
                    act.wait_ge(p_done, t + 1)
                    act.activation(sf[:, :], pZ[:, :, :].rearrange("p b d -> p (b d)"), ACT.Silu).then_inc(sf_ready, 1)

                pairs(act, body)

            @block.tensor
            def _(pe):
                for s in (hid_used, z_done):
                    pe.sem_inc(s, 1)
                pe.wait_ge(open_, 3)

                def turn(t, part, src, ready):
                    pe.wait_ge(ready, t + 1)
                    pe.wait_ge(t_evac, 2 * t + part)
                    for k in range(KD):
                        for b in range(B):
                            last = pe.transpose(pT[:, k, b * P:(b + 1) * P], src[:, b, k * P:(k + 1) * P], ident)
                    last.then_inc(t_done, 1)

                turn(0, 0, xn[0], xn_ready)
                turn(0, 1, x2, x2_ready)

                def body(i, u, more, two_more):
                    t = 2 * i + u
                    pe.wait_ge(t_evac, 2 * t + 1)
                    pe.wait_ge(s2_ready, t + 1)
                    for k in range(KD):
                        last = pe.matmul(pS[:, :], v.win2[:, k, :], xnT[:, k, :], start=(k == 0), stop=(k == KD - 1))
                    last.then_inc(s_done, 1)
                    pe.wait_ge(t_evac, 2 * t + 2)
                    pe.wait_ge(gT_ready, t + 1)
                    for b in range(B):
                        for k in range(KD):
                            last = pe.matmul(pGU[GRP * b:GRP * b + GRP, 0:P], v.wu[:, k, GRP * b:GRP * b + GRP],
                                             x2T[:, k, b * P:(b + 1) * P], start=(k == 0), stop=(k == KD - 1))
                    last.then_inc(u_done, 1)
                    pe.wait_ge(y_ready, t + 1)
                    for b in range(B):
                        for k in range(KD):
                            last = pe.matmul(pG[:, b, :], x2T[:, k, b * P:(b + 1) * P], v.wgate[:, k, :],
                                             start=(k == 0), stop=(k == KD - 1))
                    last.then_inc(g_done, 1)
                    pe.wait_ge(u_evac, t + 1)
                    for r in range(NR):
                        pe.wait_ge(hid_ready, 8 * t + r + 1 + 1)
                        pe.matmul(pGU[0:M, :], v.dsum[:, r, :], hid[r % NHID][:, :], start=(r == 0),
                                  stop=(r == NR - 1)).then_inc(hid_used, 1)
                    if more:
                        turn(t + 1, 0, xn[1 - u], xn_ready)
                    pe.wait_ge(gT_ready, t + 1 + 1)
                    pe.wait_ge(sf_ready, t + 1)
                    for b in range(B):
                        last = pe.matmul(pZ[:, b, :], gT[:, b * P:(b + 1) * P], v.woa[:, :], start=True, stop=True)
                    last.then_inc(z_done, 1)
                    if more:
                        turn(t + 1, 1, x2, x2_ready)

                pairs(pe, body)


def recur(nc, v):
    with ExitStack() as c:
        sem = v.sem
        ends = c.enter_context(nc.sbuf_tensor("r_ends", [P, NCH], F32))
        diff = c.enter_context(nc.sbuf_tensor("r_diff", [P, NCH], F32))
        differs = c.enter_context(nc.sbuf_tensor("r_differs", [P, 1], F32))
        flag = c.enter_context(nc.sbuf_tensor("r_flag", [1, 1], I32))
        pr = c.enter_context(nc.psum_tensor("r_p", [P, L, NCH], F32))
        pf = c.enter_context(nc.psum_tensor("r_pf", [P, BANK], F32))
        STEPS = BANK // NCH

        summed = sem("r_summed")
        state = sem("r_state")
        saved = sem("r_saved")
        compared = sem("r_compared")
        counted = sem("r_counted")
        flagged = sem("r_flagged")

        with nc.Block() as block:
            @block.tensor
            def _(pe):
                def sweep(n, first=False):
                    pe.wait_ge(state, L * n)
                    for q in range(L // STEPS):
                        ins = pe.matmul(pr[:, q * STEPS:(q + 1) * STEPS, :].rearrange("p l c -> p (l c)"), v.ident,
                                        v.u_st[:, q * STEPS:(q + 1) * STEPS, :].rearrange("p l c -> p (l c)"),
                                        start=True, stop=False, skip_group_check=True)
                        if q == 0 and first:
                            ins.then_inc(summed, 1)
                        elif q == 0:
                            pe.matmul(pr[:, 0, 1:NCH], v.at_blk[:, :], v.h_st[:, L - 1, 0:NCH - 1],
                                      start=False, stop=True, skip_group_check=True).then_inc(summed, 1)
                    for l in range(1, L):
                        pe.wait_ge(state, L * n + l)
                        pe.matmul(pr[:, l, :], v.at_blk[:, :], v.h_st[:, l - 1, :],
                                  start=False, stop=True, skip_group_check=True).then_inc(summed, 1)

                sweep(0, first=True)
                sweep(1)
                pe.wait_ge(compared, 2)
                pe.matmul(pf[0:1, 0:1], differs[:, :], v.ones[:, 0:1], start=True, stop=True).then_inc(counted, 1)
                pe.wait_ge(flagged, 1)
                again = pe.value_load(flag[0:1, 0:1], min_val=0, max_val=P)
                with pe.If(again > 0):
                    with pe.Fori(2, NCH + 1) as n:
                        sweep(n)
                pe.nop()

            @block.scalar
            def _(act):
                def sweep(n):
                    for l in range(L):
                        act.wait_ge(summed, L * n + l + 1)
                        act.activation(v.h_st[:, l, :], pr[:, l, :], ACT.Tanh,
                                       bias=v.u_bias[:, 0:1]).then_inc(state, 1)

                sweep(0)
                act.wait_ge(saved, 1)
                sweep(1)
                act.wait_ge(flagged, 1)
                again = act.value_load(flag[0:1, 0:1], min_val=0, max_val=P)
                with act.If(again > 0):
                    with act.Fori(2, NCH + 1) as n:
                        sweep(n)
                act.nop()

            @block.vector
            def _(dve):
                dve.wait_ge(state, L)
                dve.tensor_copy(ends[:, :], v.h_st[:, L - 1, :]).then_inc(saved, 1)
                dve.wait_ge(saved, 1)
                dve.wait_ge(state, 2 * L)
                dve.tensor_tensor(diff[:, :], v.h_st[:, L - 1, :], ends[:, :], ALU.not_equal).then_inc(compared, 1)
                dve.wait_ge(compared, 1)
                dve.tensor_reduce(differs[:, :], diff[:, :], AX.X, ALU.max).then_inc(compared, 1)
                dve.wait_ge(counted, 1)
                dve.tensor_copy(flag[0:1, 0:1], pf[0:1, 0:1]).then_inc(flagged, 1)


def attend(nc, v):
    ident = v.ident
    NP = B * (B + 1) // 2
    PAIR0 = [0, 4, 7, 9]
    PV = 2 * B - 1
    with ExitStack() as c:
        def sb(name, shape, dt=F32):
            return c.enter_context(nc.sbuf_tensor(name, shape, dt))

        def psum(name, shape):
            return c.enter_context(nc.psum_tensor(name, shape, F32))

        sem = v.sem
        hs = [sb(f"c_hs{n}", [P, CPT, L]) for n in range(2)]
        xn = [sb(f"c_xn{n}", [P, B, D]) for n in range(2)]
        xnT = sb("c_xnT", [P, KD, BANK])
        q = sb("c_q", [P, B, D])
        k = [sb(f"c_k{n}", [P, B, D]) for n in range(2)]
        vv = [sb(f"c_v{n}", [P, B, D]) for n in range(2)]
        qk = sb("c_qk", [P, NP, D])
        sc = sb("c_sc", [P, B, B, H])
        ex = sb("c_ex", [P, B, B, H])
        att = [sb(f"c_att{n}", [P, B, B, H]) for n in range(2)]
        mx = sb("c_mx", [P, B * H])
        den = sb("c_den", [P, B * H])
        rden = sb("c_rden", [P, B * H])
        pv = sb("c_pv", [P, B - 1, D])
        st = sb("c_st", [P, B, 6])
        mv = sb("c_mv", [P, B, 2])
        ta = sb("c_ta", [P, B])
        r1 = sb("c_r1", [P, B])
        mhalf = sb("c_mhalf", [P, B])
        eps = sb("c_eps", [P, B])
        part3 = qk[:, :, :].rearrange("p n d -> p (n d)").bitcast(BF16)[:, 0:9 * D].rearrange("p (a d) -> p a d", a=3)
        rest = pv[:, :, :].rearrange("p i d -> p (i d)")
        bias3 = sb("c_bias3", [P, 3 * D], BF16)
        ones3 = sb("c_ones3", [P, P], BF16)

        pT = psum("c_pT", [P, KD, BANK])
        pX = psum("c_pX", [P, B, D])
        pY = psum("c_pY", [P, B, D])
        pL = psum("c_pL", [P, BANK])

        passed = sem("c_passed")
        open_ = sem("c_open")
        masked = sem("c_masked")
        bias_ready = sem("c_bias_ready")
        hs_ready = sem("c_hs_ready")
        o_done = sem("c_o_done")
        op_ready = sem("c_op_ready")
        x1_ready = sem("c_x1_ready")
        bn = sem("c_bn")
        stats = sem("c_stats")
        rchain = sem("c_rchain")
        r_ready = sem("c_r_ready")
        xn_ready = sem("c_xn_ready")
        xn_out = [sem(f"c_xn_out{n}") for n in range(2)]
        t_done = sem("c_t_done")
        t_evac = sem("c_t_evac")
        l_done = sem("c_l_done")
        l_evac = sem("c_l_evac")
        q_done = sem("c_q_done")
        q_evac = sem("c_q_evac")
        k_done = sem("c_k_done")
        k_evac = sem("c_k_evac")
        v_done = sem("c_v_done")
        v_evac = sem("c_v_evac")
        sm = sem("c_sm")
        ex_in = sem("c_ex_in")
        ex_out = sem("c_ex_out")
        att_ready = sem("c_att_ready")
        pv_step = sem("c_pv_step")
        SM = 6

        def steps_through(t):
            return PV * (t + 1) + PV + 1

        def spread(ap, n):
            return ap.unsqueeze(1).broadcast_to([P, n, ap.shape[1]])

        with nc.Block() as block:
            @block.sync
            def _(sp):
                for s in xn_out:
                    sp.sem_inc(s, 16)
                rows = v.xn3_dram.rearrange("(b t p) d -> t p b d", b=B, p=P)
                with sp.Fori(0, NT // 2) as i:
                    for u in range(2):
                        t = 2 * i + u
                        sp.wait_ge(xn_ready, t + 1)
                        sp.dma_start(rows[t], xn[u][:, :, :]).then_inc(xn_out[u], 16)
                for u in range(2):
                    sp.wait_ge(xn_out[u], 16 * NT // 2 + 16)

            @block.gpsimd
            def _(pool):
                pool.sem_inc(pv_step, PV + 1)
                for n, (t, value) in enumerate(((mhalf[:, :], -0.5), (eps[:, :], EPS))):
                    pool.memset(t, value).then_inc(open_, 1)
                    pool.wait_ge(open_, n + 1)

                def scale(t):
                    pool.wait_ge(stats, t + 1)
                    pool.tensor_tensor(ta[:, :], mv[:, :, 1], eps[:, :], ALU.add).then_inc(rchain, 1)
                    pool.wait_ge(rchain, t + 1)
                    pool.tensor_tensor(r1[:, :], ta[:, :], mhalf[:, :], ALU.pow).then_inc(r_ready, 1)

                for t in range(3):
                    scale(t)

                def body(i, u, left):
                    t = 2 * i + u
                    n = 0
                    pool.wait_ge(att_ready, t + 1)
                    for j in range(B):
                        w = B - j
                        a = att[u][:, j, j:B, :].unsqueeze(3).broadcast_to([P, w, H, DK])
                        row = vv[u][:, j, :].rearrange("p (h d) -> p h d", d=DK).unsqueeze(1).broadcast_to([P, w, H, DK])
                        o = v.prod_st[:, t, j * D:B * D]
                        part = o if j == 0 else pv[:, 0:w, :].rearrange("p i d -> p (i d)")
                        if n:
                            pool.wait_ge(pv_step, steps_through(t - 1) + n)
                            pool.sem_inc(passed, 1)
                        pool.tensor_tensor(part.rearrange("p (i h d) -> p i h d", i=w, h=H), a, row,
                                           ALU.mult).then_inc(pv_step, 1)
                        n += 1
                        if j:
                            pool.wait_ge(pv_step, steps_through(t - 1) + n)
                            pool.sem_inc(passed, 1)
                            pool.tensor_tensor(o, o, part, ALU.add).then_inc(pv_step, 1)
                            n += 1
                        if j == 1 and left >= 3:
                            scale(t + 3)

                tiles(pool, body)

            @block.vector
            def _(dve):
                flat = v.bqkv[:, :, :].rearrange("p n d -> p (n d)")
                dve.memset(bias3[:, :], 0.0).then_inc(masked, 1)
                dve.memset(ones3[:, :], 1.0).then_inc(masked, 1)
                dve.tensor_copy(part3[:, 0, :], flat).then_inc(bias_ready, 1)
                for n in range(1, 3):
                    dve.wait_ge(bias_ready, 2 * n - 1)
                    dve.tensor_tensor(rest[:, :], flat if n == 1 else rest[:, :], part3[:, n - 1, :],
                                      ALU.subtract).then_inc(bias_ready, 1)
                    dve.wait_ge(bias_ready, 2 * n)
                    dve.tensor_copy(part3[:, n, :], rest[:, :]).then_inc(bias_ready, 1)
                dve.wait_ge(bias_ready, 5)
                dve.wait_ge(masked, 2)
                for n in range(3):
                    last = dve.tensor_copy(bias3[GRP * n:GRP * n + 1, :], part3[GRP * n:GRP * n + 1, n, :])
                last.then_inc(bias_ready, 1)
                dve.wait_ge(bias_ready, 6)
                dve.memset(sc[:, :, :, :], -1e30).then_inc(masked, 1)
                dve.wait_ge(masked, 3)

                def layer0(t):
                    dve.wait_ge(o_done, t + 1)
                    dve.tensor_tensor(v.prod_st[:, t, :], pX[:, :, :].rearrange("p b d -> p (b d)"),
                                      v.prod_st[:, t, :], ALU.mult).then_inc(op_ready, 1)
                    dve.wait_ge(op_ready, t + 1)
                    dve.tensor_tensor(v.x_st[:, t, :], v.prod_st[:, t, :], v.x_st[:, t, :], ALU.add).then_inc(x1_ready, 1)
                    dve.wait_ge(x1_ready, t + 1)
                    dve.sem_inc(passed, 1)
                    for b in range(B):
                        last = dve.bn_stats(st[:, b, :], v.x_st[:, t, b * D:(b + 1) * D])
                    last.then_inc(bn, 1)
                    dve.wait_ge(bn, t + 1)
                    dve.sem_inc(passed, 1)
                    for b in range(B):
                        last = dve.bn_aggr(mv[:, b, :], st[:, b, :])
                    last.then_inc(stats, 1)

                def normalise(t, u, stores):
                    dve.wait_ge(r_ready, t + 1)
                    dve.wait_ge(xn_out[u], 16 * stores + 16)
                    for b in range(B):
                        last = dve.tensor_scalar(xn[u][:, b, :], v.x_st[:, t, b * D:(b + 1) * D],
                                                 mv[:, b, 0:1], r1[:, b:b + 1], ALU.subtract, ALU.mult)
                    last.then_inc(xn_ready, 1)

                for t in range(2):
                    layer0(t)
                    normalise(t, t, 0)

                def body(i, u, left):
                    t = 2 * i + u
                    if left >= 2:
                        layer0(t + 2)
                    dve.wait_ge(k_evac, t + 1)
                    dve.wait_ge(q_evac, t + 1)
                    for j in range(B):
                        w = B - j
                        last = dve.tensor_tensor(qk[:, PAIR0[j]:PAIR0[j] + w, :], q[:, j:B, :],
                                                 spread(k[u][:, j, :], w), ALU.mult)
                    last.then_inc(sm, 1)
                    if left >= 2:
                        normalise(t + 2, u, i + 1)
                    dve.wait_ge(sm, SM * t + 1)
                    for j in range(B):
                        w = B - j
                        last = dve.tensor_reduce(
                            sc[:, j, j:B, :].rearrange("p i h -> p (i h)"),
                            qk[:, PAIR0[j]:PAIR0[j] + w, :].rearrange("p i (h d) -> p (i h) d", d=DK), AX.X, ALU.add)
                    last.then_inc(sm, 1)
                    dve.wait_ge(sm, SM * t + 2)
                    dve.tensor_reduce(mx[:, :], sc[:, :, :, :].rearrange("p j i h -> p (i h) j"), AX.X,
                                      ALU.max).then_inc(sm, 1)
                    dve.wait_ge(sm, SM * t + 3)
                    dve.tensor_tensor(ex[:, :, :, :].rearrange("p j i h -> p j (i h)"),
                                      sc[:, :, :, :].rearrange("p j i h -> p j (i h)"), spread(mx[:, :], B),
                                      ALU.subtract).then_inc(ex_in, 1)
                    dve.wait_ge(ex_out, t + 1)
                    dve.tensor_reduce(den[:, :], ex[:, :, :, :].rearrange("p j i h -> p (i h) j"), AX.X,
                                      ALU.add).then_inc(sm, 1)
                    dve.wait_ge(sm, SM * t + 4)
                    dve.tensor_scalar(den[:, :], den[:, :], 1.0, None, ALU.add).then_inc(sm, 1)
                    dve.wait_ge(sm, SM * t + 5)
                    dve.reciprocal(rden[:, :], den[:, :]).then_inc(sm, 1)
                    dve.wait_ge(sm, SM * t + SM)
                    dve.wait_ge(pv_step, steps_through(t - 2))
                    dve.tensor_tensor(att[u][:, :, :, :].rearrange("p j i h -> p j (i h)"),
                                      ex[:, :, :, :].rearrange("p j i h -> p j (i h)"), spread(rden[:, :], B),
                                      ALU.mult).then_inc(att_ready, 1)

                tiles(dve, body)

            @block.scalar
            def _(act):
                for s in (l_evac, v_evac):
                    act.sem_inc(s, 1)

                def states(t, u, reused=True):
                    if reused:
                        act.wait_ge(o_done, t - 1)
                        act.sem_inc(passed, 1)
                    act.activation(hs[u][:, :, :], v.h_st[:, :, bass.ts(t, CPT)].rearrange("p l c -> p c l"),
                                   ACT.Copy).then_inc(hs_ready, 1)

                def take(dst, src, done, evac, t):
                    act.wait_ge(done, t + 1)
                    act.activation(dst[:, :, :], src[:, :, :], ACT.Copy).then_inc(evac, 1)

                def take_qk(t, u, reused=True):
                    if reused:
                        act.wait_ge(sm, SM * (t - 1) + 1)
                    take(q, pY, q_done, q_evac, t)
                    take(k[u], pX, k_done, k_evac, t)

                def take_v(t, u, reused=True):
                    if reused:
                        act.wait_ge(pv_step, steps_through(t - 2))
                    take(vv[u], pY, v_done, v_evac, t)
                    act.wait_ge(l_done, t + 1)
                    act.sem_inc(passed, 1)
                    act.activation(v.logit_st[:, :, t, :], pL[:, 0:B * E].rearrange("p (b e) -> p b e", e=E),
                                   ACT.Copy).then_inc(l_evac, 1)

                states(0, 0, reused=False)
                states(1, 1, reused=False)
                take(xnT, pT, t_done, t_evac, 0)
                states(2, 0)
                take_qk(0, 0, reused=False)
                take_v(0, 0, reused=False)
                take(xnT, pT, t_done, t_evac, 1)
                take_qk(1, 1)

                def body(i, u, left):
                    t = 2 * i + u
                    act.wait_ge(ex_in, t + 1)
                    act.activation(ex[:, :, :, :], ex[:, :, :, :], ACT.Exp).then_inc(ex_out, 1)
                    if left >= 1:
                        take_v(t + 1, 1 - u)
                    if left >= 3:
                        states(t + 3, 1 - u)
                    if left >= 2:
                        take(xnT, pT, t_done, t_evac, t + 2)
                        take_qk(t + 2, u)

                tiles(act, body)

            @block.tensor
            def _(pe):
                def output(t, u):
                    pe.wait_ge(hs_ready, t + 1)
                    for n in range(2):
                        last = pe.matmul(pX[:, 2 * n:2 * n + 2, :].rearrange("p b d -> p (b d)"),
                                         hs[u][:, :, :].rearrange("p c l -> p (c l)"),
                                         v.wo_pad[:, 2 * n:2 * n + 2, :].rearrange("p b d -> p (b d)"),
                                         start=True, stop=True)
                    last.then_inc(o_done, 1)

                def turn(t, u):
                    pe.wait_ge(xn_ready, t + 1)
                    for kk in range(KD):
                        for b in range(B):
                            last = pe.transpose(pT[:, kk, b * P:(b + 1) * P], xn[u][:, b, kk * P:(kk + 1) * P], ident)
                    last.then_inc(t_done, 1)

                output(0, 0)
                pe.wait_ge(op_ready, 1)
                output(1, 1)
                turn(0, 0)
                pe.wait_ge(bias_ready, 6)

                def body(i, u, left):
                    t = 2 * i + u
                    pe.wait_ge(t_evac, t + 1)
                    for n, (dst, done) in enumerate(((pY, q_done), (pX, k_done), (pY, v_done))):
                        if n == 0:
                            pe.wait_ge(v_evac, t + 1)
                        if n == 1:
                            pe.wait_ge(op_ready, t + 2 if left >= 1 else t + 1)
                        if n == 2:
                            pe.wait_ge(l_evac, t + 1)
                            for b in range(B):
                                for kk in range(KD):
                                    last = pe.matmul(pL[:, b * E:(b + 1) * E], xnT[:, kk, b * P:(b + 1) * P], v.wgr[:, kk, :],
                                                     start=(kk == 0), stop=(kk == KD - 1))
                            last.then_inc(l_done, 1)
                            pe.wait_ge(q_evac, t + 1)
                        for m in range(2):
                            pe.matmul(dst[:, 2 * m:2 * m + 2, :], ones3[:, :], spread(bias3[:, n * D:(n + 1) * D], 2),
                                      start=True, stop=False, skip_group_check=True)
                        for b in range(B):
                            for kk in range(KD):
                                last = pe.matmul(dst[:, b, :], xnT[:, kk, b * P:(b + 1) * P],
                                                 v.wqkv[:, kk, n * D:(n + 1) * D], start=False, stop=(kk == KD - 1),
                                                 skip_group_check=True)
                        last.then_inc(done, 1)
                    if left >= 1:
                        turn(t + 1, 1 - u)
                    if left >= 2:
                        pe.wait_ge(k_evac, t + 1)
                        output(t + 2, u)

                tiles(pe, body)


def route(nc, v):
    W = NG * E
    K2 = TOPK * NG
    with ExitStack() as c:
        def sb(name, shape, dt=F32):
            return c.enter_context(nc.sbuf_tensor(name, shape, dt))

        sem = v.sem
        hot = sb("d_hot", [P, TOPK, NG, E])
        lg2 = sb("d_lg2", [P, NG, E])
        eq = sb("d_eq", [P, NG, E])
        best = sb("d_best", [P, TOPK, NG])
        first = sb("d_first", [P, TOPK, NG])
        total = sb("d_total", [P, E, K2])
        before = sb("d_before", [P, E, K2])
        pos = sb("d_pos", [P, TOPK, NG, E])
        loc = sb("d_loc", [P, K2])
        valid = sb("d_valid", [P, K2])
        loci = sb("d_loci", [P, K2], I32)
        lo_i = sb("d_lo_i", [P, K2], I32)
        hi_i = sb("d_hi_i", [P, K2], I32)
        lo = sb("d_lo", [P, K2])
        hi = sb("d_hi", [P, K2])
        gates = sb("d_gates", [P, TOPK, NG])
        dl = sb("d_dl", [P, NG])
        ee = sb("d_ee", [P, NG])
        ep = sb("d_ep", [P, NG])
        NB = 4
        ohl = [sb(f"d_ohl{n}", [P, P]) for n in range(NB)]
        val = [sb(f"d_val{n}", [P, 2, P]) for n in range(NB)]
        tab = sb("d_tab", [P, 2, P])
        empty = sb("d_empty", [P, P])
        t1 = sb("d_t1", [P, P])
        t2 = sb("d_t2", [P, P])
        zero = sb("d_zero", [P, 2 * P])
        pin = c.enter_context(nc.psum_tensor("d_pin", [P, TOPK, BANK], F32))
        ptot = c.enter_context(nc.psum_tensor("d_ptot", [P, TOPK, BANK], F32))
        ptab = c.enter_context(nc.psum_tensor("d_ptab", [P, BANK], F32))

        link = sem("d_link")
        hot_ready = sem("d_hot_ready")
        counts = sem("d_counts")
        e_in = sem("d_e_in")
        e_out = sem("d_e_out")
        one_ready = sem("d_one_ready")
        one_used = [sem(f"d_one_used{n}") for n in range(NB)]
        table = sem("d_table")
        lg = v.logit_st[:, :, :, :].rearrange("p b t e -> p (b t) e")
        expert = v.cst[:, C_E:C_E + E].unsqueeze(1).broadcast_to([P, NG, E])

        def each(ap):
            return ap.unsqueeze(2).broadcast_to([P, NG, E])

        with nc.Block() as block:
            @block.vector
            def _(dve):
                done = [0]

                def linked(ins):
                    done[0] += 1
                    ins.then_inc(link, 1)
                    dve.wait_ge(link, done[0])

                linked(dve.memset(zero[:, :], 0.0))
                for t in (v.idx, v.dst, v.gate):
                    dve.memset(t[:, E * CAP // P:], 0)
                for k in range(TOPK):
                    src = lg if k == 0 else lg2[:, :, :]
                    linked(dve.tensor_reduce(best[:, k, :], src, AX.X, ALU.max))
                    linked(dve.tensor_tensor(eq[:, :, :], src, each(best[:, k, :]), ALU.is_equal))
                    linked(dve.scalar_tensor_tensor(eq[:, :, :], expert, float(-E), eq[:, :, :], ALU.add, ALU.mult))
                    linked(dve.tensor_reduce(first[:, k, :], eq[:, :, :], AX.X, ALU.min))
                    linked(dve.tensor_scalar(first[:, k, :], first[:, k, :], float(E), None, ALU.add))
                    ins = dve.tensor_tensor(hot[:, k, :, :], expert, each(first[:, k, :]), ALU.is_equal)
                    ins.then_inc(hot_ready, 1)
                    dve.wait_ge(hot_ready, k + 1)
                    if k == 0:
                        linked(dve.scalar_tensor_tensor(lg2[:, :, :], hot[:, 0, :, :], -1e30, lg, ALU.mult, ALU.add))
                dve.tensor_tensor(dl[:, :], best[:, 1, :], best[:, 0, :], ALU.subtract).then_inc(e_in, 1)
                dve.wait_ge(e_out, 1)
                linked(dve.tensor_scalar(ep[:, :], ee[:, :], 1.0, None, ALU.add))
                linked(dve.reciprocal(gates[:, 0, :], ep[:, :]))
                linked(dve.tensor_tensor(gates[:, 1, :], ee[:, :], gates[:, 0, :], ALU.mult))
                dve.wait_ge(counts, 2)
                for k in range(TOPK):
                    linked(dve.tensor_copy(total[:, :, k * NG:(k + 1) * NG],
                                           ptot[:, k, :].rearrange("p (g e) -> p e g", e=E)))
                for e in range(E):
                    linked(dve.tensor_tensor_scan(before[:, e, :], total[:, e, :], zero[:, 0:K2], 0.0,
                                                  ALU.add, ALU.add))
                linked(dve.tensor_tensor(before[:, :, :], before[:, :, :], total[:, :, :], ALU.subtract))
                for k in range(TOPK):
                    linked(dve.tensor_tensor(pos[:, k, :, :], pin[:, k, :].rearrange("p (g e) -> p g e", e=E),
                                             before[:, :, k * NG:(k + 1) * NG].rearrange("p e g -> p g e"), ALU.add))
                linked(dve.tensor_tensor(pos[:, :, :, :], pos[:, :, :, :], hot[:, :, :, :], ALU.mult))
                linked(dve.tensor_reduce(loc[:, :], pos[:, :, :, :].rearrange("p k g e -> p (k g) e"), AX.X, ALU.add))
                linked(dve.tensor_scalar(valid[:, :], loc[:, :], float(CAP), None, ALU.is_lt))
                linked(dve.tensor_copy(loci[:, :], loc[:, :]))
                dve.tensor_scalar(lo_i[:, :], loci[:, :], P - 1, None, ALU.bitwise_and)
                linked(dve.tensor_scalar(hi_i[:, :], loci[:, :], 7, None, ALU.logical_shift_right))
                dve.tensor_copy(lo[:, :], lo_i[:, :])
                linked(dve.tensor_copy(hi[:, :], hi_i[:, :]))
                linked(dve.scalar_tensor_tensor(hi[:, :], first[:, :, :].rearrange("p k g -> p (k g)"),
                                                float(CAP // P), hi[:, :], ALU.mult, ALU.add))
                linked(dve.scalar_tensor_tensor(hi[:, :], hi[:, :], 1.0, valid[:, :], ALU.add, ALU.mult))
                linked(dve.tensor_scalar(hi[:, :], hi[:, :], -1.0, None, ALU.add))
                gat = gates[:, :, :].rearrange("p k g -> p (k g)")
                with dve.Fori(0, K2 // NB) as i:
                    for u in range(NB):
                        n = NB * i + u
                        dve.wait_ge(one_used[u], i + 1)
                        dve.wait_ge(link, done[0])
                        dve.tensor_scalar(ohl[u][:, :], v.iota, lo[:, bass.ds(n, 1)], None, ALU.is_equal)
                        dve.tensor_scalar(val[u][:, 0, :], v.iota, hi[:, bass.ds(n, 1)],
                                          v.cst[:, bass.ds(C_G + n, 1)], ALU.is_equal, ALU.mult)
                        dve.tensor_scalar(val[u][:, 1, :], v.iota, hi[:, bass.ds(n, 1)], gat[:, bass.ds(n, 1)],
                                          ALU.is_equal, ALU.mult).then_inc(one_ready, 1)
                dve.wait_ge(table, 1)
                linked(dve.tensor_copy(tab[:, :, :], ptab[:, 0:2 * P].rearrange("p (a b) -> p a b", a=2)))
                dve.tensor_copy(v.gate[:, 0:P], tab[:, 1, :])
                linked(dve.tensor_scalar(empty[:, :], tab[:, 0, :], 0.0, None, ALU.is_equal))
                linked(dve.scalar_tensor_tensor(t1[:, :], empty[:, :], float(TOPK * N + 1), tab[:, 0, :],
                                                ALU.mult, ALU.add))
                dve.tensor_scalar(v.dst[:, 0:P], t1[:, :], -1.0, None, ALU.add)
                linked(dve.tensor_scalar(t2[:, :], tab[:, 0, :], float(N), float(-N), ALU.is_gt, ALU.mult))
                linked(dve.scalar_tensor_tensor(t2[:, :], t2[:, :], -1.0, tab[:, 0, :], ALU.add, ALU.add))
                linked(dve.tensor_scalar(v.idx[:, 0:P], t2[:, :], 0.0, None, ALU.max))

            @block.scalar
            def _(act):
                act.wait_ge(e_in, 1)
                act.activation(ee[:, :], dl[:, :], ACT.Exp).then_inc(e_out, 1)

            @block.tensor
            def _(pe):
                for s in one_used:
                    pe.sem_inc(s, 1)
                for k in range(TOPK):
                    pe.wait_ge(hot_ready, k + 1)
                    oh = hot[:, k, :, :].rearrange("p g e -> p (g e)")
                    pe.matmul(pin[:, k, :], v.cst[:, C_UP:C_UP + P], oh, start=True, stop=True)
                    pe.matmul(ptot[:, k, :], v.ones, oh, start=True, stop=True).then_inc(counts, 1)
                pe.wait_ge(link, 1)
                pe.matmul(ptab[:, 0:2 * P], v.ident, zero[:, :], start=True, stop=False, skip_group_check=True)
                with pe.Fori(0, K2 // NB) as i:
                    for u in range(NB):
                        pe.wait_ge(one_ready, NB * i + u + 1)
                        pe.matmul(ptab[:, 0:2 * P], ohl[u][:, :], val[u][:, :, :].rearrange("p a b -> p (a b)"),
                                  start=False, stop=False, skip_group_check=True).then_inc(one_used[u], 1)
                pe.matmul(ptab[:, 0:2 * P], v.ident, zero[:, :], start=False, stop=True,
                          skip_group_check=True).then_inc(table, 1)


def experts(nc, v):
    with ExitStack() as c:
        def sb(name, shape, dt=F32):
            return c.enter_context(nc.sbuf_tensor(name, shape, dt))

        def psum(name, shape):
            return c.enter_context(nc.psum_tensor(name, shape, F32))

        sem = v.sem
        W = BLK * P
        HALF = KD * HID
        raw = sb("e_raw", [P, 2, HALF])
        w1_hi = sb("e_w1_hi", [P, KD, HID], F16)
        w1_lo = sb("e_w1_lo", [P, KD, HID], F16)
        w2_hi = sb("e_w2_hi", [P, HT, D], F16)
        w2_lo = sb("e_w2_lo", [P, HT, D], F16)
        most = sb("e_most", [P, 3])
        most3 = sb("e_most3", [3, 1])
        diag = sb("e_diag", [3, 3])
        bound = sb("e_bound", [P, 3])
        power = sb("e_power", [P, 3], I32)
        scale = [sb(f"e_scale{n}", [P, 3], I32) for n in range(2)]
        h_scale = [sb(f"e_h_scale{n}", [P, 1]) for n in range(2)]
        y_scale = [sb(f"e_y_scale{n}", [P, 1]) for n in range(2)]
        b1c = [sb(f"e_b1c{n}", [P, HT]) for n in range(2)]
        b2b = [v.logit_st[:, :, :, :].rearrange("p b t e -> p (b t e)")[:, n * D:(n + 1) * D] for n in range(2)]
        icol = [sb(f"e_icol{n}", [P, BLK], I32) for n in range(2)]
        dcol = [sb(f"e_dcol{n}", [P, BLK], I32) for n in range(2)]
        gcol = [sb(f"e_gcol{n}", [P, BLK]) for n in range(2)]
        xg = [sb(f"e_xg{n}", [P, BLK, D]) for n in range(2)]
        x_hi = sb("e_x_hi", [P, KD, W], F16)
        x_lo = sb("e_x_lo", [P, KD, W], F16)
        h_all = [sb(f"e_h_all{n}", [P, W]) for n in range(2)]
        h_hi = sb("e_h_hi", [P, HT, W], F16)
        h_lo = sb("e_h_lo", [P, HT, W], F16)
        yo = [sb(f"e_yo{n}", [P, BLK, D]) for n in range(2)]

        pT = psum("e_pT", [P, KD, BANK])
        NPH = 4
        pH = [psum(f"e_pH{n}", [P, BANK]) for n in range(NPH)]
        pY = psum("e_pY", [P, BLK, D])

        passed = sem("e_passed")
        w1_in = sem("e_w1_in")
        w2_in = sem("e_w2_in")
        w1_hi_ready = sem("e_w1_hi_ready")
        w1_lo_ready = sem("e_w1_lo_ready")
        w2_hi_ready = sem("e_w2_hi_ready")
        w2_lo_ready = sem("e_w2_lo_ready")
        b2_in = [sem(f"e_b2_in{n}") for n in range(2)]
        most_ready = sem("e_most_ready")
        most_turned = sem("e_most_turned")
        diag_ready = sem("e_diag_ready")
        most_spread = sem("e_most_spread")
        step = sem("e_step")
        scales_ready = sem("e_scales_ready")
        icols = sem("e_icols")
        gcols = sem("e_gcols")
        x_in = [sem(f"e_x_in{n}") for n in range(2)]
        t_done = sem("e_t_done")
        x_hi_ready = sem("e_x_hi_ready")
        x_lo_ready = sem("e_x_lo_ready")
        h_done = sem("e_h_done")
        h_ready = sem("e_h_ready")
        odd_ready = sem("e_odd_ready")
        h_lo_ready = sem("e_h_lo_ready")
        y_done = sem("e_y_done")
        yb_ready = sem("e_yb_ready")
        yo_ready = sem("e_yo_ready")
        y_out = [sem(f"e_y_out{n}") for n in range(2)]
        NGR = E * GRPS
        STEPS = 8

        def groups(eng, body):
            with eng.Fori(0, E // 2) as ep:
                for eu in range(2):
                    for g in range(GRPS):
                        e = 2 * ep + eu
                        body(e, eu, g, GRPS * e + g)

        with nc.Block() as block:
            @block.sync
            def _(sp):
                w1_v = v.ew1.rearrange("e (k p) h -> e p k h", p=P)
                w2_v = v.ew2.rearrange("e (t p) d -> e p t d", p=P)

                def load_w1(e):
                    sp.dma_start(raw[:, 0, :].rearrange("p (k h) -> p k h", k=KD), w1_v[e]).then_inc(w1_in, 16)

                def load_w2(e):
                    sp.dma_start(raw[:, 1, :].rearrange("p (t d) -> p t d", t=HT), w2_v[e]).then_inc(w2_in, 16)

                def follow(e, source):
                    sp.wait_ge(w1_hi_ready, e + 1)
                    sp.wait_ge(w1_lo_ready, e + 1)
                    load_w1(source)
                    sp.wait_ge(w2_hi_ready, HT * (e + 1))
                    sp.wait_ge(w2_lo_ready, HT * (e + 1))
                    load_w2(source)

                load_w1(0)
                load_w2(0)
                sp.dma_start(b2b[1], v.eb2[1].partition_broadcast(P)).then_inc(b2_in[1], 16)
                with sp.Fori(0, E // 2 - 1) as ep:
                    for eu in range(2):
                        e = 2 * ep + eu
                        follow(e, e + 1)
                        sp.wait_ge(yb_ready, GRPS * (e + 1) + 1)
                        sp.dma_start(b2b[eu], v.eb2[e + 2].partition_broadcast(P)).then_inc(b2_in[eu], 16)
                follow(E - 2, E - 1)
                follow(E - 1, E - 1)
                sp.wait_ge(w1_in, 16 * (E + 1))
                sp.wait_ge(w2_in, 16 * (E + 1))

            @block.gpsimd
            def _(pool):
                pool.dma_start(b2b[0], v.eb2[0].partition_broadcast(P)).then_inc(y_out[1], 16)

                def gather(n, u):
                    pool.wait_ge(icols, n + 1)
                    pool.sem_inc(passed, 1)
                    for q in range(BLK):
                        pool.indirect_dma_start(xg[u][:, q, :], None, v.xn3_dram,
                                                bass.IndirectOffsetOnAxis(icol[u][:, q:q + 1], axis=0),
                                                bounds_check=N - 1, oob_is_err=False).then_inc(x_in[u], 16)

                for u in range(2):
                    gather(u, u)
                with pool.Fori(0, NGR // 2) as i:
                    for u in range(2):
                        gather(2 * i + u + 2, u)
                        pool.wait_ge(yo_ready, 2 * i + u + 1)
                        pool.sem_inc(passed, 1)
                        for q in range(BLK):
                            pool.indirect_dma_start(
                                v.y_dram, bass.IndirectOffsetOnAxis(dcol[u][:, q:q + 1], axis=0), yo[u][:, q, :], None,
                                bounds_check=TOPK * N - 1, oob_is_err=False).then_inc(y_out[u], 16)
                for u in range(2):
                    pool.wait_ge(y_out[u], 16 * BLK * NGR // 2 + 16 * u)
                    pool.wait_ge(x_in[u], 16 * BLK * (NGR // 2 + 1))

            @block.vector
            def _(dve):
                dve.sem_inc(h_lo_ready, 1)
                dve.sem_inc(yb_ready, 1)
                dve.sem_inc(b2_in[0], 16)

                def take_icol(n, u):
                    dve.tensor_copy(icol[u][:, :], v.idx[:, bass.ts(n, BLK)]).then_inc(icols, 1)

                def take_gcol(n, u):
                    dve.tensor_copy(dcol[u][:, :], v.dst[:, bass.ts(n, BLK)])
                    dve.tensor_copy(gcol[u][:, :], v.gate[:, bass.ts(n, BLK)]).then_inc(gcols, 1)

                def largest(e, eu):
                    dve.wait_ge(w1_in, 16 * (e + 1))
                    dve.wait_ge(w2_in, 16 * (e + 1))
                    dve.sem_inc(passed, 1)
                    dve.tensor_copy(b1c[eu][:, :], v.b1t[:, bass.ts(e, HT)]).then_inc(step, 1)
                    dve.tensor_reduce(most[:, 0:2], raw[:, :, :], AX.X, ALU.max, apply_absolute_value=True)
                    dve.wait_ge(step, STEPS * e + 1)
                    dve.tensor_reduce(most[:, 2:3], b1c[eu][:, :], AX.X, ALU.max,
                                      apply_absolute_value=True).then_inc(most_ready, 1)

                def largest_of_all(e):
                    dve.wait_ge(most_turned, e + 1)
                    dve.tensor_reduce(most3[:, :], pT[0:3, 0, 0:P], AX.X, ALU.max).then_inc(step, 1)
                    dve.wait_ge(step, STEPS * e + 2)
                    dve.tensor_scalar(diag[:, :], v.ident[0:3, 0:3], most3[:, 0:1], None,
                                      ALU.mult).then_inc(diag_ready, 1)

                def scales(e, eu):
                    dve.wait_ge(most_spread, e + 1)
                    dve.sem_inc(passed, 1)
                    dve.tensor_copy(bound[:, :], pT[:, 1, 0:3]).then_inc(step, 1)
                    dve.wait_ge(step, STEPS * e + 3)
                    dve.scalar_tensor_tensor(bound[:, 2:3], bound[:, 0:1], float(D), bound[:, 2:3],
                                             ALU.mult, ALU.add).then_inc(step, 1)
                    dve.wait_ge(step, STEPS * e + 4)
                    dve.tensor_scalar(bound[:, :], bound[:, :], LEAST, None, ALU.max).then_inc(step, 1)
                    dve.wait_ge(step, STEPS * e + 5)
                    dve.tensor_scalar(power[:, :], bound[:, :].bitcast(I32), EXPONENT, None,
                                      ALU.bitwise_and).then_inc(step, 1)
                    dve.wait_ge(step, STEPS * e + 6)
                    dve.tensor_scalar(scale[eu][:, :], power[:, :], -1.0, float((127 + 127 + RANGE_LOG2) << 23),
                                      ALU.mult, ALU.add).then_inc(step, 1)
                    dve.wait_ge(step, STEPS * e + 7)
                    two = power[:, :].bitcast(F32)
                    s = scale[eu][:, :].bitcast(F32)
                    dve.tensor_scalar(h_scale[eu][:, :], two[:, 0:1], s[:, 2:3], 1.0 / (RANGE * X_SCALE),
                                      ALU.mult, ALU.mult)
                    dve.tensor_scalar(y_scale[eu][:, :], two[:, 1:2], two[:, 2:3], 1.0 / (RANGE * RANGE),
                                      ALU.mult, ALU.mult)
                    dve.tensor_scalar(b1c[eu][:, :], b1c[eu][:, :], s[:, 2:3], None, ALU.mult).then_inc(step, 1)
                    dve.wait_ge(step, STEPS * e + STEPS)
                    dve.sem_inc(scales_ready, 1)

                def lower_w1(e, eu):
                    dve.wait_ge(w1_hi_ready, e + 1)
                    dve.scalar_tensor_tensor(w1_lo[:, :, :].rearrange("p k h -> p (k h)"), raw[:, 0, :],
                                             scale[eu][:, 0:1].bitcast(F32),
                                             w1_hi[:, :, :].rearrange("p k h -> p (k h)"),
                                             ALU.mult, ALU.subtract).then_inc(w1_lo_ready, 1)

                def lower_w2(e, eu, h):
                    dve.wait_ge(w2_hi_ready, HT * e + h + 1)
                    dve.scalar_tensor_tensor(w2_lo[:, h, :], raw[:, 1, h * D:(h + 1) * D],
                                             scale[eu][:, 1:2].bitcast(F32), w2_hi[:, h, :],
                                             ALU.mult, ALU.subtract).then_inc(w2_lo_ready, 1)

                def x_lower(n):
                    dve.wait_ge(x_hi_ready, n + 1)
                    dve.sem_inc(passed, 1)
                    dve.scalar_tensor_tensor(x_lo[:, :, :], pT[:, :, :], X_SCALE, x_hi[:, :, :],
                                             ALU.mult, ALU.subtract).then_inc(x_lo_ready, 1)

                take_icol(0, 0)
                take_icol(1, 1)
                take_gcol(0, 0)
                largest(0, 0)
                largest_of_all(0)
                scales(0, 0)
                lower_w1(0, 0)
                x_lower(0)

                def body(e, eu, g, n):
                    u = g % 2
                    for h in range(HT):
                        dve.wait_ge(h_ready, HT * n + h + 1 + 1)
                        if h % 2:
                            dve.sem_inc(passed, 1)
                            dve.tensor_copy(h_hi[:, h, :], h_all[1][:, :]).then_inc(odd_ready, 1)
                            dve.wait_ge(odd_ready, HT // 2 * n + h // 2 + 1)
                        dve.tensor_tensor(h_lo[:, h, :], h_all[h % 2][:, :], h_hi[:, h, :],
                                          ALU.subtract).then_inc(h_lo_ready, 1)
                        if g == 0:
                            lower_w2(e, eu, h)
                        if g == 2 and h == 1:
                            largest_of_all(e + 1)
                    x_lower(n + 1)
                    take_icol(n + 2, u)
                    if g == 1:
                        largest(e + 1, 1 - eu)
                    elif g == 2:
                        scales(e + 1, 1 - eu)
                    elif g == GRPS - 1:
                        lower_w1(e + 1, 1 - eu)
                    if u == 0:
                        dve.wait_ge(y_out[1], 8 * BLK * n + 16)
                    else:
                        dve.wait_ge(y_out[0], 8 * BLK * (n + 1))
                    take_gcol(n + 1, 1 - u)
                    dve.wait_ge(y_done, n + 1)
                    if g == 0:
                        dve.wait_ge(b2_in[eu], 8 * (e - eu) + 16)
                    dve.scalar_tensor_tensor(yo[u][:, :, :], pY[:, :, :], y_scale[eu][:, 0:1],
                                             b2b[eu].unsqueeze(1).broadcast_to([P, BLK, D]),
                                             ALU.mult, ALU.add).then_inc(yb_ready, 1)
                    dve.wait_ge(gcols, n + 1)
                    dve.wait_ge(yb_ready, n + 1 + 1)
                    dve.tensor_tensor(yo[u][:, :, :], yo[u][:, :, :],
                                      gcol[u][:, :].unsqueeze(2).broadcast_to([P, BLK, D]),
                                      ALU.mult).then_inc(yo_ready, 1)

                groups(dve, body)

            @block.scalar
            def _(act):
                act.sem_inc(h_ready, 1)

                def upper_w1(e, eu):
                    act.wait_ge(scales_ready, e + 1)
                    act.sem_inc(passed, 1)
                    act.activation(w1_hi[:, :, :].rearrange("p k h -> p (k h)"), raw[:, 0, :], ACT.Copy,
                                   scale=scale[eu][:, 0:1].bitcast(F32)).then_inc(w1_hi_ready, 1)

                def upper_w2(eu, h):
                    act.activation(w2_hi[:, h, :], raw[:, 1, h * D:(h + 1) * D], ACT.Copy,
                                   scale=scale[eu][:, 1:2].bitcast(F32)).then_inc(w2_hi_ready, 1)

                def x_upper(n):
                    act.wait_ge(t_done, n + 1)
                    act.activation(x_hi[:, :, :], pT[:, :, :], ACT.Copy, scale=X_SCALE).then_inc(x_hi_ready, 1)

                upper_w1(0, 0)
                x_upper(0)

                def body(e, eu, g, n):
                    u = g % 2
                    for h in range(HT):
                        act.wait_ge(h_done, HT * n + h + 1)
                        act.wait_ge(h_lo_ready, HT * n + max(h - 1, 0) + 1)
                        for dst in (h_all[h % 2][:, :], h_hi[:, h, :])[0:2 - h % 2]:
                            last = act.activation(dst, pH[h % NPH][:, :], ACT.Relu, bias=b1c[eu][:, h:h + 1],
                                                  scale=h_scale[eu][:, 0:1])
                        last.then_inc(h_ready, 1)
                        if g == 0:
                            upper_w2(eu, h)
                    x_upper(n + 1)
                    if g == GRPS - 1:
                        upper_w1(e + 1, 1 - eu)

                groups(act, body)

            @block.tensor
            def _(pe):
                def turn(u, uses):
                    pe.wait_ge(x_in[u], 16 * BLK * uses)
                    for k in range(KD):
                        for q in range(BLK):
                            last = pe.transpose(pT[:, k, q * P:(q + 1) * P], xg[u][:, q, k * P:(k + 1) * P], v.ident)
                    last.then_inc(t_done, 1)

                def turn_most(e):
                    pe.wait_ge(most_ready, e + 1)
                    pe.transpose(pT[0:3, 0, 0:P], most[:, :], v.ident).then_inc(most_turned, 1)

                def spread_most(e):
                    pe.wait_ge(diag_ready, e + 1)
                    pe.matmul(pT[:, 1, 0:3], v.ones[0:3, :], diag[:, :], start=True, stop=True).then_inc(most_spread, 1)

                turn_most(0)
                spread_most(0)
                pe.wait_ge(scales_ready, 1)
                turn(0, 1)

                def body(e, eu, g, n):
                    u = g % 2
                    if g == 0:
                        pe.wait_ge(w1_lo_ready, e + 1)
                        pe.sem_inc(passed, 1)
                    pe.wait_ge(x_lo_ready, n + 1)
                    for h in range(HT):
                        pe.wait_ge(h_ready, HT * n + max(h - NPH + 1, 0) + 1)
                        rows = slice(h * P, (h + 1) * P)
                        for k in range(KD):
                            pe.matmul(pH[h % NPH][:, :], w1_hi[:, k, rows], x_hi[:, k, :], start=(k == 0), stop=False)
                            pe.matmul(pH[h % NPH][:, :], w1_hi[:, k, rows], x_lo[:, k, :], start=False, stop=False)
                            last = pe.matmul(pH[h % NPH][:, :], w1_lo[:, k, rows], x_hi[:, k, :],
                                             start=False, stop=(k == KD - 1))
                        last.then_inc(h_done, 1)
                        if g == 2 and h == 0:
                            turn_most(e + 1)
                    if g == 2:
                        pe.wait_ge(diag_ready, e + 2)
                    elif g == 3:
                        pe.wait_ge(scales_ready, e + 2)
                    turn(1 - u, 2 * e + (g + 1) // 2 + 1)
                    pe.wait_ge(yb_ready, n + 1)
                    for q in range(BLK):
                        cols = slice(q * P, (q + 1) * P)
                        for h in range(HT):
                            if q == 0:
                                if g == 0:
                                    pe.wait_ge(w2_lo_ready, HT * e + h + 1)
                                    pe.sem_inc(passed, 1)
                                pe.wait_ge(h_lo_ready, HT * n + h + 1 + 1)
                            pe.matmul(pY[:, q, :], h_hi[:, h, cols], w2_hi[:, h, :], start=(h == 0), stop=False)
                            pe.matmul(pY[:, q, :], h_hi[:, h, cols], w2_lo[:, h, :], start=False, stop=False)
                            last = pe.matmul(pY[:, q, :], h_lo[:, h, cols], w2_hi[:, h, :],
                                             start=False, stop=(h == HT - 1))
                        if g == 2 and q == 1:
                            pe.wait_ge(x_lo_ready, n + 2)
                            spread_most(e + 1)
                    last.then_inc(y_done, 1)

                groups(pe, body)


def combine(nc, v):
    with ExitStack() as c:
        def sb(name, shape, dt=F32):
            return c.enter_context(nc.sbuf_tensor(name, shape, dt))

        sem = v.sem
        ya = [sb(f"f_ya{n}", [P, B * D]) for n in range(2)]
        yb = [sb(f"f_yb{n}", [P, B * D]) for n in range(2)]
        o = [sb(f"f_o{n}", [P, B * D]) for n in range(2)]
        y_in = [sem(f"f_y_in{n}") for n in range(2)]
        sum_ready = sem("f_sum_ready")
        silu_ready = sem("f_silu_ready")
        sg_ready = sem("f_sg_ready")
        o_ready = sem("f_o_ready")
        o_out = [sem(f"f_o_out{n}") for n in range(2)]

        with nc.Block() as block:
            @block.sync
            def _(sp):
                for s in o_out:
                    sp.sem_inc(s, 16)
                rows = v.y_dram.rearrange("(k b t p) d -> t k p b d", k=TOPK, b=B, p=P)
                dst = v.out.rearrange("b (t p) d -> t p b d", p=P)

                def load(t, u):
                    for k, y in enumerate((ya[u], yb[u])):
                        sp.dma_start(y[:, :].rearrange("p (b d) -> p b d", b=B), rows[t, k]).then_inc(y_in[u], 16)

                load(0, 0)
                load(1, 1)

                def body(i, u, more, two_more):
                    t = 2 * i + u
                    sp.wait_ge(o_ready, t + 1)
                    sp.dma_start(dst[t], o[u][:, :].rearrange("p (b d) -> p b d", b=B)).then_inc(o_out[u], 16)
                    if two_more:
                        load(t + 2, u)

                pairs(sp, body)
                for u in range(2):
                    sp.wait_ge(o_out[u], 16 * NT // 2 + 16)

            @block.vector
            def _(dve):
                def add(t, u, uses):
                    dve.wait_ge(y_in[u], 32 * uses)
                    dve.tensor_tensor(ya[u][:, :], ya[u][:, :], yb[u][:, :], ALU.add).then_inc(sum_ready, 1)

                add(0, 0, 1)

                def body(i, u, more, two_more):
                    t = 2 * i + u
                    if more:
                        add(t + 1, 1 - u, i + u + 1)
                    dve.wait_ge(silu_ready, t + 1)
                    dve.wait_ge(o_out[u], 16 * i + 16)
                    dve.tensor_tensor(o[u][:, :], ya[u][:, :], v.prod_st[:, t, :], ALU.mult).then_inc(sg_ready, 1)
                    dve.wait_ge(sg_ready, t + 1)
                    dve.tensor_tensor(o[u][:, :], o[u][:, :], v.x_st[:, t, :], ALU.add).then_inc(o_ready, 1)

                pairs(dve, body)

            @block.scalar
            def _(act):
                def body(i, u, more, two_more):
                    act.wait_ge(sum_ready, 2 * i + u + 1)
                    act.activation(ya[u][:, :], ya[u][:, :], ACT.Silu).then_inc(silu_ready, 1)

                pairs(act, body)


def kernel(**inputs):
    import numpy as np
    import concourse.bacc as bacc
    from concourse.bass_utils import run_bass_kernel_spmd

    nc = bacc.Bacc("TRN2", target_bir_lowering=False, num_devices=1)
    order = ["L0_attn_x", "L0_attn_Ws", "L0_attn_bs", "L0_attn_Wi", "L0_attn_bi", "L0_attn_Wo", "L0_attn_bo",
             "L0_attn_Wg", "L0_attn_bg", "L0_attn_ln_w", "L0_attn_ln_b", "L0_attn_A", "L0_ffn_Win", "L0_ffn_bin_",
             "L0_ffn_W1", "L0_ffn_b1", "L0_ffn_W2", "L0_ffn_b2", "L0_ffn_Wout", "L0_ffn_bout", "L1_attn_Wq",
             "L1_attn_bq", "L1_attn_Wk", "L1_attn_bk", "L1_attn_Wv", "L1_attn_bv", "L1_ffn_wg", "L1_ffn_w1",
             "L1_ffn_b1", "L1_ffn_w2", "L1_ffn_b2"]
    arrays = {"constants": constants()}
    for name in order:
        arrays[name] = np.ascontiguousarray(inputs[name])
    args = [nc.dram_tensor(n, a.shape, mybir.dt.from_np(a.dtype), kind="ExternalInput").ap()
            for n, a in arrays.items()]
    out = nc.dram_tensor("out", (B, S, D), F32, kind="ExternalOutput").ap()
    program(nc, [*args, out])
    r = run_bass_kernel_spmd(nc, [arrays], core_ids=[0])
    return r.results[0]["out"]
```

```python
from contextlib import ExitStack

import concourse.bass as bass
from concourse import mybir

P = 128
B, S, D = 4, 2048, 256
KD = D // P
N = B * S
NT = S // P
M, INNER = 64, 16
NR = INNER // 2
NS = 16
GRP = 32
L = 16
SWEEPS = 3
NCH = S // L
CPT = P // L
BANK = 512
H, DK = 16, 16
E, TOPK = 8, 2
HID = 1024
HT = HID // P
CAP = TOPK * N // E
NG = N // P
BLK = 4
GRPS = CAP // (BLK * P)
EPS = 1e-5
RANGE_LOG2 = 14
RANGE = float(1 << RANGE_LOG2)
X_SCALE = float(1 << 10)
LEAST = 2.0 ** -40
EXPONENT = 0xFF << 23
SAT = 30.0

F32 = mybir.dt.float32
I32 = mybir.dt.int32
F16 = mybir.dt.float16
BF16 = mybir.dt.bfloat16
ALU = mybir.AluOpType
ACT = mybir.ActivationFunctionType
AX = mybir.AxisListType

C_ID, C_UP, C_ONE, C_IOTA, C_P, C_SAT, C_E = 0, P, 2 * P, 3 * P, 4 * P, 4 * P + 1, 4 * P + 2
C_G = C_E + E
C_ALL = C_G + TOPK * NG


def constants():
    import numpy as np
    c = np.zeros((P, C_ALL), np.float32)
    c[:, C_ID:C_ID + P] = np.eye(P)
    c[:, C_UP:C_UP + P] = np.triu(np.ones((P, P)), 1)
    c[:, C_ONE:C_ONE + P] = 1
    c[:, C_IOTA:C_IOTA + P] = np.arange(P)
    c[:, C_P] = np.arange(P) + 1
    c[NS::GRP, C_SAT] = SAT
    c[:, C_E:C_E + E] = np.arange(E)
    c[:, C_G:] = np.arange(TOPK * NG)
    return c


class Shared:
    pass


def program(nc, args):
    v = Shared()
    (v.consts, v.x, v.Ws, v.bs, v.Wi, v.bi, v.Wo, v.bo, v.Wg, v.bg, v.ln_w, v.ln_b, v.A, v.Win, v.bin_, v.W1, v.b1,
     v.W2, v.b2, v.Wout, v.bout, v.Wq, v.bq, v.Wk, v.bk, v.Wv, v.bv, v.wg, v.ew1, v.eb1, v.ew2, v.eb2, v.out) = args
    v.xn3_dram = nc.dram_tensor("xn3_rows", [N, D], F32, kind="Internal").ap()
    v.y_dram = nc.dram_tensor("expert_rows", [TOPK * N, D], F32, kind="Internal").ap()

    stack = ExitStack()
    with stack:
        def sb(name, shape, dt=F32, at=stack):
            return at.enter_context(nc.sbuf_tensor(name, shape, dt))

        v.sem = lambda name: stack.enter_context(nc.semaphore(name))

        v.x_in = v.sem("x_in")
        v.cst = sb("cst", [P, C_ALL])
        v.ident = v.cst[:, C_ID:C_ID + P]
        v.ones = v.cst[:, C_ONE:C_ONE + P]
        v.iota = v.cst[:, C_IOTA:C_IOTA + P]
        v.prod_st = sb("prod_st", [P, NT, B * D])
        v.x_st = sb("x_st", [P, NT, B * D])
        v.logit_st = sb("logit_st", [P, B, NT, E])
        v.b1t = sb("b1t", [P, (E + 1) * HT])
        front = stack.enter_context(ExitStack())
        v.wqkv = sb("wqkv", [P, KD, 3 * D], at=front)
        v.bqkv = sb("bqkv", [P, 3, D], at=front)
        v.wgr = sb("wgr", [P, KD, E], at=front)
        v.wo_pad = sb("wo_pad", [P, B, D], at=front)
        v.h_st = sb("h_st", [P, L, NCH], at=front)
        early = stack.enter_context(ExitStack())
        v.wu = sb("wu", [P, KD, P], at=early)
        v.u_bias = sb("u_bias", [P, 1], at=early)
        v.wgate = sb("wgate", [P, KD, D], at=early)
        v.bgate = sb("bgate", [P, D], at=early)
        v.win2 = sb("win2", [P, KD, P], at=early)
        v.bin2 = sb("bin2", [P, 1], at=early)
        v.w1c = sb("w1c", [P, NR], at=early)
        v.nb1c = sb("nb1c", [P, NR], at=early)
        v.dsum = sb("dsum", [P, NR, M], at=early)
        v.w2c = sb("w2c", [P, NR], at=early)
        v.sel = sb("sel", [P, M], at=early)
        v.gconst = sb("gconst", [M, 1], at=early)
        v.woa = sb("woa", [M + 1, D], at=early)
        v.at_blk = sb("at_blk", [P, P], at=early)
        v.u_st = sb("u_st", [P, L, NCH], at=early)

        prepare(nc, v)
        mix(nc, v)
        recur(nc, v)
        early.close()
        attend(nc, v)
        front.close()
        v.gates = sb("gates", [P, TOPK, NG])
        with ExitStack() as back:
            v.idx = sb("idx", [P, E * CAP // P + 2 * BLK], I32, at=back)
            v.dst = sb("dst", [P, E * CAP // P + 2 * BLK], I32, at=back)
            v.raw = sb("raw", [P, 2, KD * HID], at=back)
            v.w1_in = v.sem("w1_in")
            v.w2_in = v.sem("w2_in")
            route(nc, v)
            experts(nc, v)
        combine(nc, v)


def prepare(nc, v):
    ident, cst = v.ident, v.cst
    with ExitStack() as c:
        def sb(name, shape, dt=F32):
            return c.enter_context(nc.sbuf_tensor(name, shape, dt))

        def psum(name, shape):
            return c.enter_context(nc.psum_tensor(name, shape, F32))

        sem = v.sem
        rs = sb("p_rs", [P, D])
        ri = sb("p_ri", [P, D])
        ra = sb("p_ra", [P, P])
        woc = sb("p_woc", [P, KD, NS + 1])
        wop = sb("p_wop", [P, KD, P])
        wot = sb("p_wot", [P, D])
        big = sb("p_big", [P, 4, KD, D])
        win = sb("p_win", [P, KD, M])
        w2c = v.w2c
        b1c = sb("p_b1c", [P, NR])
        sel = v.sel
        wb = sb("p_wb", [P, NR])
        wbs = sb("p_wbs", [P, 1])
        b2f = sb("p_b2f", [M, 1])
        lnwb = sb("p_lnwb", [P, 2, KD])
        lnb_b = sb("p_lnb_b", [P, KD, P])
        bsi = sb("p_bsi", [P, 2])
        b1r = sb("p_b1r", [E * HT, P])
        wu_raw = sb("p_wu_raw", [P, KD, P])
        ps = [psum(f"p_ps{n}", [P, BANK]) for n in range(8)]

        cleared = sem("p_cleared")
        loaded = sem("p_loaded")
        chain = sem("p_chain")
        turned = sem("p_turned")
        taken = sem("p_taken")

        loads = []
        cleared_loads = []

        def load(dst, src):
            loads.append((dst, src))

        def load_cleared(dst, src):
            cleared_loads.append((dst, src))

        load(cst[:, :], v.consts)
        for g in range(B):
            r = slice(GRP * g, GRP * g + NS)
            load_cleared(rs[r, :], v.Ws)
            load_cleared(ri[r, :], v.Wi)
            load_cleared(ra[r, GRP * g:GRP * g + NS], v.A)
            load_cleared(bsi[r, 0:1], v.bs.unsqueeze(1))
            load_cleared(bsi[r, 1:2], v.bi.unsqueeze(1))
        for k in range(KD):
            load(woc[:, k, 0:NS], v.Wo[k * P:(k + 1) * P, :])
            load(woc[:, k, NS:NS + 1], v.bo[k * P:(k + 1) * P].unsqueeze(1))
            load(lnwb[:, 0, k:k + 1], v.ln_w[k * P:(k + 1) * P].unsqueeze(1))
            load(lnwb[:, 1, k:k + 1], v.ln_b[k * P:(k + 1) * P].unsqueeze(1))
        for n, w in enumerate((v.Wg, v.Wq, v.Wk, v.Wv)):
            load(big[:, n, :, :], w.rearrange("(k p) d -> p k d", p=P))
        load(win[:, :, :], v.Win.rearrange("(k p) m -> p k m", p=P))
        load(v.wgr[:, :, :], v.wg.rearrange("(k p) e -> p k e", p=P))
        for j in range(2):
            r = slice(M * j, M * j + M)
            load(v.w1c[r, :], v.W1[:, NR * j:NR * j + NR])
            load(b1c[r, :], v.b1[:, NR * j:NR * j + NR])
            load(w2c[r, :], v.W2[:, NR * j:NR * j + NR])
            load(v.bin2[r, :], v.bin_.unsqueeze(1))
        load(b2f[:, :], v.b2.unsqueeze(1))
        load(v.woa[0:M, :], v.Wout)
        load(v.woa[M:M + 1, :], v.bout.unsqueeze(0))
        load(v.bgate[:, :], v.bg.partition_broadcast(P))
        for n, w in enumerate((v.bq, v.bk, v.bv)):
            load(v.bqkv[:, n, :], w.partition_broadcast(P))
        load(b1r[:, :], v.eb1.rearrange("e (t p) -> (e t) p", p=P))

        NCLEAR = 5
        ALL = 16 * (len(loads) + len(cleared_loads))

        with nc.Block() as block:
            @block.gpsimd
            def _(pool):
                for n, t in enumerate((rs, ri, ra, bsi, v.wo_pad)):
                    pool.memset(t[:], 0.0).then_inc(cleared, 1)
                    pool.wait_ge(cleared, n + 1)

            @block.sync
            def _(sp):
                for dst, src in loads:
                    sp.dma_start(dst, src).then_inc(loaded, 16)
                sp.wait_ge(loaded, ALL)

            @block.scalar
            def _(act):
                for b in range(B):
                    act.dma_start(v.x_st[:, :, b * D:(b + 1) * D],
                                  v.x[b].rearrange("(t p) d -> p t d", p=P)).then_inc(v.x_in, 16)
                act.wait_ge(cleared, NCLEAR)
                for dst, src in cleared_loads:
                    act.dma_start(dst, src).then_inc(loaded, 16)

            @block.tensor
            def _(pe):
                pe.wait_ge(loaded, ALL)
                for n, m in enumerate((1, 2, 3, 0)):
                    for kd in range(KD):
                        if n >= 2:
                            pe.wait_ge(taken, 2 * (n - 2) + kd + 1)
                        for ke in range(KD):
                            last = pe.transpose(ps[2 * (n % 2) + kd][:, ke * P:(ke + 1) * P],
                                                big[:, m, ke, kd * P:(kd + 1) * P], ident)
                        last.then_inc(turned, 1)
                pe.wait_ge(chain, 1)
                for k in range(KD):
                    last = pe.transpose(ps[4][:, k * P:(k + 1) * P], rs[:, k * P:(k + 1) * P], ident)
                last.then_inc(turned, 1)
                pe.transpose(ps[5][:, 0:P], ra[:, :], ident).then_inc(turned, 1)
                pe.wait_ge(chain, 2)
                for k in range(KD):
                    last = pe.transpose(ps[6][:, k * P:(k + 1) * P], wop[:, k, :], ident)
                last.then_inc(turned, 1)
                pe.transpose(ps[7][:, 0:E * HT], b1r[:, :], ident[0:E * HT, 0:E * HT]).then_inc(turned, 1)
                pe.wait_ge(chain, 3)
                pe.wait_ge(taken, 8)
                for k in range(KD):
                    last = pe.matmul(ps[0][:, 0:1], wu_raw[:, k, :], lnwb[:, 1, k:k + 1],
                                     start=(k == 0), stop=(k == KD - 1))
                last.then_inc(turned, 1)
                for k in range(KD):
                    last = pe.matmul(ps[1][:, 0:D], lnb_b[:, k, :], v.wgate[:, k, :],
                                     start=(k == 0), stop=(k == KD - 1))
                last.then_inc(turned, 1)
                pe.matmul(ps[2][0:M, 0:1], sel[:, :], wbs[:, :], start=True, stop=True).then_inc(turned, 1)

            @block.vector
            def _(dve):
                dve.wait_ge(cleared, NCLEAR)
                dve.wait_ge(loaded, ALL)
                dve.tensor_tensor(rs[:, :], rs[:, :], ri[:, :], ALU.add).then_inc(chain, 1)
                link = sem("p_link")
                done = [0]

                def linked(ins):
                    done[0] += 1
                    ins.then_inc(link, 1)
                    dve.wait_ge(link, done[0])

                linked(dve.memset(wop[:, :, :], 0.0))
                for g in range(B):
                    last = dve.tensor_scalar(wop[:, :, GRP * g:GRP * g + NS + 1], woc[:, :, :], 0.5, None, ALU.mult)
                last.then_inc(chain, 1)
                linked(dve.tensor_tensor(sel[:, :], ident[:, 0:M], ident[:, M:2 * M], ALU.add))
                for r in range(NR):
                    dve.tensor_scalar(v.dsum[:, r, :], sel[:, :], w2c[:, r:r + 1], None, ALU.mult)
                linked(dve.tensor_tensor(wb[:, :], w2c[:, :], b1c[:, :], ALU.mult))
                linked(dve.tensor_reduce(wbs[:, :], wb[:, :], AX.X, ALU.add))
                dve.tensor_scalar(v.nb1c[:, :], b1c[:, :], -1.0, None, ALU.mult)
                for j in range(2):
                    dve.tensor_copy(v.win2[:, :, j * M:(j + 1) * M], win[:, :, :])
                for k in range(KD):
                    dve.tensor_scalar(lnb_b[:, k, :], v.ones, lnwb[:, 1, k:k + 1], None, ALU.mult)
                linked(dve.tensor_scalar(v.bqkv[:, 0, :], v.bqkv[:, 0, :], DK ** -0.5, None, ALU.mult))
                for n in range(4):
                    for kd in range(KD):
                        dve.wait_ge(turned, 2 * n + kd + 1)
                        src = ps[2 * (n % 2) + kd][:, 0:D]
                        if n == 3:
                            ins = dve.tensor_copy(v.wgate[:, kd, :], src)
                        else:
                            ins = dve.tensor_scalar(v.wqkv[:, kd, n * D:(n + 1) * D], src,
                                                    DK ** -0.5 if n == 0 else 1.0, None, ALU.mult)
                        ins.then_inc(taken, 1)
                dve.wait_ge(turned, 9)
                for k in range(KD):
                    dve.tensor_copy(wu_raw[:, k, :], ps[4][:, k * P:(k + 1) * P])
                    last = dve.tensor_scalar(v.wu[:, k, :], ps[4][:, k * P:(k + 1) * P], lnwb[:, 0, k:k + 1],
                                             None, ALU.mult)
                last.then_inc(chain, 1)
                dve.wait_ge(turned, 10)
                dve.tensor_copy(v.at_blk[:, :], ps[5][:, 0:P])
                dve.wait_ge(turned, 11)
                linked(dve.tensor_copy(wot[:, :], ps[6][:, 0:D]))
                for g in range(B):
                    r = slice(GRP * g, GRP * g + GRP)
                    linked(dve.tensor_copy(v.wo_pad[r, g, :], wot[r, :]))
                dve.wait_ge(turned, 12)
                dve.tensor_copy(v.b1t[:, 0:E * HT], ps[7][:, 0:E * HT])
                dve.memset(v.b1t[:, E * HT:], 0.0)
                dve.wait_ge(turned, 13)
                linked(dve.scalar_tensor_tensor(v.u_bias[:, :], ps[0][:, 0:1], bsi[:, 0:1], bsi[:, 1:2],
                                                ALU.add, ALU.add))
                linked(dve.tensor_tensor(v.u_bias[:, :], v.u_bias[:, :], cst[:, C_SAT:C_SAT + 1], ALU.add))
                dve.wait_ge(turned, 14)
                dve.tensor_tensor(v.bgate[:, :], v.bgate[:, :], ps[1][:, 0:D], ALU.add)
                for k in range(KD):
                    dve.tensor_scalar(v.wgate[:, k, :], v.wgate[:, k, :], lnwb[:, 0, k:k + 1], None, ALU.mult)
                dve.wait_ge(turned, 15)
                linked(dve.tensor_tensor(v.gconst[:, :], ps[2][0:M, 0:1], b2f[:, :], ALU.add))


def pairs(eng, body, first=0):
    for i in range(first):
        for u in range(2):
            body(i, u, True, True)
    with eng.Fori(first, NT // 2 - 1) as i:
        for u in range(2):
            body(i, u, True, True)
    for u in range(2):
        body(NT // 2 - 1, u, u == 0, False)


def tiles(eng, body):
    with eng.Fori(0, NT // 2 - 2) as i:
        for u in range(2):
            body(i, u, 4)
    for i in (NT // 2 - 2, NT // 2 - 1):
        for u in range(2):
            body(i, u, NT - 1 - 2 * i - u)


def mix(nc, v):
    ident = v.ident
    with ExitStack() as c:
        def sb(name, shape, dt=F32):
            return c.enter_context(nc.sbuf_tensor(name, shape, dt))

        def psum(name, shape):
            return c.enter_context(nc.psum_tensor(name, shape, F32))

        sem = v.sem
        NPE = NR // 2
        HR = NPE + 1
        MERGE = 8
        xn = [sb(f"a_xn{n}", [P, B, D]) for n in range(2)]
        xnT = sb("a_xnT", [P, KD, BANK])
        hid = [sb(f"a_hid{n}", [P, BANK]) for n in range(NPE)]
        one = [sb(f"a_one{n}", [P, BANK]) for n in range(3)]
        acc = sb("a_acc", [P, BANK])
        us = sb("a_us", [P, P])
        s2 = sb("a_s2", [P, BANK])
        gT = sb("a_gT", [M + 1, BANK])
        sf = sb("a_sf", [P, B * D])
        st = sb("a_st", [P, B, 6])
        mv = sb("a_mv", [P, B, 2])
        r1 = sb("a_r1", [P, B])
        again = [sb(f"a_again{n}", [P, B]) for n in range(2)]
        ta = sb("a_ta", [P, B])
        mhalf = sb("a_mhalf", [P, B])
        eps = sb("a_eps", [P, B])

        pT = psum("a_pT", [P, KD, BANK])
        pS = psum("a_pS", [P, BANK])
        pGU = psum("a_pGU", [P, BANK])
        pG = psum("a_pG", [P, B, D])
        pZ = psum("a_pZ", [P, B, D])

        passed = sem("a_passed")
        open_ = sem("a_open")
        bn = sem("a_bn")
        stats = sem("a_stats")
        rchain = sem("a_rchain")
        r_ready = sem("a_r_ready")
        xn_ready = sem("a_xn_ready")
        again_ready = sem("a_again_ready")
        us_ready = sem("a_us_ready")
        ut_done = sem("a_ut_done")
        merge = sem("a_merge")
        t_done = sem("a_t_done")
        t_evac = sem("a_t_evac")
        s_done = sem("a_s_done")
        s2_ready = sem("a_s2_ready")
        u_done = sem("a_u_done")
        u_evac = sem("a_u_evac")
        g_done = sem("a_g_done")
        y_ready = sem("a_y_ready")
        thy_ready = sem("a_thy_ready")
        hid_ready = sem("a_hid_ready")
        hid_used = sem("a_hid_used")
        gT_ready = sem("a_gT_ready")
        z_done = sem("a_z_done")
        sf_ready = sem("a_sf_ready")
        p_done = sem("a_p_done")
        xs_ready = sem("a_xs_ready")
        q_done = sem("a_q_done")

        with nc.Block() as block:
            @block.gpsimd
            def _(pool):
                for s in (q_done,):
                    pool.sem_inc(s, 1)
                for n, (t, value) in enumerate(((gT[M:M + 1, :], 1.0), (mhalf[:, :], -0.5), (eps[:, :], EPS))):
                    pool.memset(t, value).then_inc(open_, 1)
                    pool.wait_ge(open_, n + 1)

                def scales(t, u):
                    pool.wait_ge(stats, t + 1)
                    pool.tensor_tensor(ta[:, :], mv[:, :, 1], eps[:, :], ALU.add).then_inc(rchain, 1)
                    pool.wait_ge(rchain, 4 * t + 1)
                    pool.tensor_tensor(r1[:, :], ta[:, :], mhalf[:, :], ALU.pow).then_inc(r_ready, 1)
                    pool.wait_ge(r_ready, t + 1)
                    pool.tensor_tensor(ta[:, :], mv[:, :, 1], r1[:, :], ALU.mult).then_inc(rchain, 1)
                    pool.wait_ge(rchain, 4 * t + 2)
                    pool.tensor_tensor(ta[:, :], ta[:, :], r1[:, :], ALU.mult).then_inc(rchain, 1)
                    pool.wait_ge(rchain, 4 * t + 3)
                    pool.tensor_tensor(ta[:, :], ta[:, :], eps[:, :], ALU.add).then_inc(rchain, 1)
                    pool.wait_ge(rchain, 4 * t + 4)
                    pool.tensor_tensor(again[u][:, :], ta[:, :], mhalf[:, :], ALU.pow).then_inc(again_ready, 1)

                scales(0, 0)

                def body(i, u, more, two_more):
                    t = 2 * i + u
                    if more:
                        scales(t + 1, 1 - u)
                    pool.wait_ge(sf_ready, t + 1 + 1)
                    xf = xn[u][:, :, :].rearrange("p b d -> p (b d)")
                    pool.tensor_tensor(xf, xf, sf[:, :], ALU.mult).then_inc(xs_ready, 1)
                    pool.wait_ge(xs_ready, t + 1)
                    pool.sem_inc(passed, 1)
                    pool.tensor_tensor(v.x_st[:, t, :], v.x_st[:, t, :], xf, ALU.add).then_inc(q_done, 1)

                pairs(pool, body)

            @block.vector
            def _(dve):
                for s in (hid_ready, p_done, y_ready, u_evac):
                    dve.sem_inc(s, 1)
                def measure(t, reused=True):
                    for b in range(B):
                        last = dve.bn_stats(st[:, b, :], v.x_st[:, t, b * D:(b + 1) * D])
                    last.then_inc(bn, 1)
                    dve.wait_ge(bn, t + 1)
                    if reused:
                        dve.wait_ge(again_ready, t)
                    dve.sem_inc(passed, 1)
                    for b in range(B):
                        last = dve.bn_aggr(mv[:, b, :], st[:, b, :])
                    last.then_inc(stats, 1)

                def normalise(t, u, reused=True):
                    dve.wait_ge(r_ready, t + 1)
                    if reused:
                        dve.wait_ge(q_done, t - 1 + 1)
                    for b in range(B):
                        last = dve.tensor_scalar(xn[u][:, b, :], v.x_st[:, t, b * D:(b + 1) * D],
                                                 mv[:, b, 0:1], r1[:, b:b + 1], ALU.subtract, ALU.mult)
                    last.then_inc(xn_ready, 1)

                dve.wait_ge(v.x_in, 16 * B)
                measure(0, reused=False)
                normalise(0, 0, reused=False)

                def product(t):
                    dve.wait_ge(thy_ready, t + 1)
                    dve.wait_ge(sf_ready, t + 1 + 1)
                    dve.scalar_tensor_tensor(v.prod_st[:, t, :], v.prod_st[:, t, :], 1.0,
                                             sf[:, :], ALU.add, ALU.mult).then_inc(p_done, 1)

                def body(i, u, more, two_more):
                    t = 2 * i + u
                    if more:
                        measure(t + 1)
                    dve.wait_ge(s2_ready, t + 1 + 1)

                    def unit(dst, r):
                        return dve.tensor_scalar(dst[:, :], s2[:, :], v.w1c[:, r:r + 1], v.nb1c[:, r:r + 1],
                                                 ALU.mult, ALU.max)

                    def add(src, r):
                        return dve.scalar_tensor_tensor(acc[:, :], src[:, :], v.w2c[:, r:r + 1], acc[:, :],
                                                        ALU.mult, ALU.add)

                    for r in range(NPE):
                        dve.wait_ge(hid_used, HR * t + r + 1)
                        unit(hid[r], r).then_inc(hid_ready, 1)
                        if r == 1:
                            dve.wait_ge(again_ready, t + 1)
                            dve.wait_ge(u_done, t + 1)
                            dve.tensor_tensor(us[:, :].rearrange("p (b n) -> p b n", b=B),
                                              pGU[:, 0:P].rearrange("p (b n) -> p b n", b=B),
                                              again[u][:, :].unsqueeze(2).broadcast_to([P, B, GRP]),
                                              ALU.mult).then_inc(us_ready, 1)
                    unit(one[0], NPE).then_inc(merge, 1)
                    unit(one[1], NPE + 1).then_inc(merge, 1)
                    dve.wait_ge(merge, MERGE * t + 1)
                    dve.wait_ge(hid_used, HR * t + HR)
                    dve.tensor_scalar(acc[:, :], one[0][:, :], v.w2c[:, NPE:NPE + 1], None, ALU.mult).then_inc(merge, 1)
                    unit(one[2], NPE + 2).then_inc(merge, 1)
                    dve.wait_ge(merge, MERGE * t + 3)
                    add(one[1], NPE + 1).then_inc(merge, 1)
                    unit(one[0], NPE + 3).then_inc(merge, 1)
                    dve.wait_ge(merge, MERGE * t + 5)
                    add(one[2], NPE + 2).then_inc(merge, 1)
                    dve.wait_ge(merge, MERGE * t + 7)
                    add(one[0], NPE + 3).then_inc(merge, 1)
                    dve.wait_ge(merge, MERGE * t + MERGE)
                    dve.sem_inc(hid_ready, 1)
                    if more:
                        normalise(t + 1, 1 - u)
                    dve.wait_ge(ut_done, t + 1)
                    dve.sem_inc(passed, 1)
                    dve.tensor_copy(v.u_st[:, :, bass.ts(t, CPT)].rearrange("p l c -> p c l"),
                                    pS[:, 0:P].rearrange("p (c l) -> p c l", l=L)).then_inc(u_evac, 1)
                    if not (isinstance(i, int) and t == 0):
                        product(t - 1)
                    dve.wait_ge(g_done, t + 1)
                    dve.sem_inc(passed, 1)
                    for b in range(B):
                        last = dve.scalar_tensor_tensor(v.prod_st[:, t, b * D:(b + 1) * D], pG[:, b, :],
                                                        again[u][:, b:b + 1], v.bgate[:, :], ALU.mult, ALU.add)
                    last.then_inc(y_ready, 1)

                pairs(dve, body, first=1)
                product(NT - 1)

            @block.scalar
            def _(act):
                for s in (s2_ready, gT_ready, sf_ready):
                    act.sem_inc(s, 1)
                def evac(t):
                    act.wait_ge(t_done, t + 1)
                    act.activation(xnT[:, :, :], pT[:, :, :], ACT.Copy).then_inc(t_evac, 1)

                evac(0)

                def body(i, u, more, two_more):
                    t = 2 * i + u
                    act.wait_ge(s_done, t + 1)
                    act.wait_ge(hid_ready, HR * t + 1)
                    act.activation(s2[:, :], pS[:, :], ACT.Identity, bias=v.bin2[:, 0:1]).then_inc(s2_ready, 1)
                    act.wait_ge(hid_used, HR * t + HR + HR)
                    act.wait_ge(z_done, t + 1)
                    act.activation(gT[0:M, :], pGU[0:M, :], ACT.Identity, bias=v.gconst[:, 0:1]).then_inc(gT_ready, 1)
                    if more:
                        evac(t + 1)
                    act.wait_ge(y_ready, t + 1 + 1)
                    act.sem_inc(passed, 1)
                    act.activation(v.prod_st[:, t, :], v.prod_st[:, t, :], ACT.Tanh, scale=0.5).then_inc(thy_ready, 1)
                    act.wait_ge(z_done, t + 1 + 1)
                    act.wait_ge(q_done, t + 1)
                    act.wait_ge(p_done, t + 1)
                    act.activation(sf[:, :], pZ[:, :, :].rearrange("p b d -> p (b d)"), ACT.Silu).then_inc(sf_ready, 1)

                pairs(act, body)

            @block.tensor
            def _(pe):
                pe.sem_inc(z_done, 1)
                pe.sem_inc(hid_used, HR)
                pe.wait_ge(open_, 3)

                def turn(t, u):
                    pe.wait_ge(xn_ready, t + 1)
                    for k in range(KD):
                        for b in range(B):
                            last = pe.transpose(pT[:, k, b * P:(b + 1) * P], xn[u][:, b, k * P:(k + 1) * P], ident)
                    last.then_inc(t_done, 1)

                turn(0, 0)

                def body(i, u, more, two_more):
                    t = 2 * i + u
                    pe.wait_ge(t_evac, t + 1)
                    pe.wait_ge(u_evac, t + 1)
                    for k in range(KD):
                        last = pe.matmul(pS[:, :], v.win2[:, k, :], xnT[:, k, :], start=(k == 0), stop=(k == KD - 1))
                    last.then_inc(s_done, 1)
                    pe.wait_ge(gT_ready, t + 1)
                    for b in range(B):
                        for k in range(KD):
                            last = pe.matmul(pGU[:, GRP * b:GRP * b + GRP], xnT[:, k, b * P:(b + 1) * P],
                                             v.wu[:, k, GRP * b:GRP * b + GRP], start=(k == 0), stop=(k == KD - 1))
                    last.then_inc(u_done, 1)
                    pe.wait_ge(y_ready, t + 1)
                    for b in range(B):
                        for k in range(KD):
                            last = pe.matmul(pG[:, b, :], xnT[:, k, b * P:(b + 1) * P], v.wgate[:, k, :],
                                             start=(k == 0), stop=(k == KD - 1))
                    last.then_inc(g_done, 1)
                    pe.wait_ge(us_ready, t + 1)
                    for r in range(NPE):
                        pe.wait_ge(hid_ready, HR * t + r + 1 + 1)
                        pe.matmul(pGU[0:M, :], v.dsum[:, r, :], hid[r][:, :], start=(r == 0),
                                  stop=False).then_inc(hid_used, 1)
                    pe.wait_ge(s2_ready, t + 1 + 1)
                    pe.transpose(pS[:, 0:P], us[:, :], ident).then_inc(ut_done, 1)
                    pe.wait_ge(hid_ready, HR * t + HR + 1)
                    pe.matmul(pGU[0:M, :], v.sel[:, :], acc[:, :], start=False, stop=True).then_inc(hid_used, 1)
                    if more:
                        turn(t + 1, 1 - u)
                    pe.wait_ge(gT_ready, t + 1 + 1)
                    pe.wait_ge(sf_ready, t + 1)
                    for b in range(B):
                        last = pe.matmul(pZ[:, b, :], gT[:, b * P:(b + 1) * P], v.woa[:, :], start=True, stop=True)
                    last.then_inc(z_done, 1)

                pairs(pe, body)


def recur(nc, v):
    with ExitStack() as c:
        sem = v.sem
        ends = c.enter_context(nc.sbuf_tensor("r_ends", [P, NCH], F32))
        diff = c.enter_context(nc.sbuf_tensor("r_diff", [P, NCH], F32))
        differs = c.enter_context(nc.sbuf_tensor("r_differs", [P, 1], F32))
        flag = c.enter_context(nc.sbuf_tensor("r_flag", [1, 1], I32))
        pr = c.enter_context(nc.psum_tensor("r_p", [P, L, NCH], F32))
        pf = c.enter_context(nc.psum_tensor("r_pf", [P, BANK], F32))
        STEPS = BANK // NCH

        summed = sem("r_summed")
        state = sem("r_state")
        saved = sem("r_saved")
        compared = sem("r_compared")
        counted = sem("r_counted")
        flagged = sem("r_flagged")
        zero = c.enter_context(nc.sbuf_tensor("r_zero", [P, 8 * D], F32))
        cleared = sem("r_cleared")
        zeroed = sem("r_zeroed")

        with nc.Block() as block:
            @block.gpsimd
            def _(pool):
                pool.memset(zero[:, :], 0.0).then_inc(cleared, 1)

            @block.sync
            def _(sp):
                sp.wait_ge(cleared, 1)
                parts = TOPK * N // (P * 8)
                for n in range(parts):
                    rows = slice(n * P * 8, (n + 1) * P * 8)
                    sp.dma_start(v.y_dram[rows, :].rearrange("(p r) d -> p (r d)", p=P), zero[:, :]).then_inc(zeroed, 16)
                sp.wait_ge(zeroed, 16 * parts)

            @block.tensor
            def _(pe):
                def sweep(n, first=False):
                    pe.wait_ge(state, L * n)
                    for q in range(L // STEPS):
                        ins = pe.matmul(pr[:, q * STEPS:(q + 1) * STEPS, :].rearrange("p l c -> p (l c)"), v.ident,
                                        v.u_st[:, q * STEPS:(q + 1) * STEPS, :].rearrange("p l c -> p (l c)"),
                                        start=True, stop=False, skip_group_check=True)
                        if q == 0 and first:
                            ins.then_inc(summed, 1)
                        elif q == 0:
                            pe.matmul(pr[:, 0, 1:NCH], v.at_blk[:, :], v.h_st[:, L - 1, 0:NCH - 1],
                                      start=False, stop=True, skip_group_check=True).then_inc(summed, 1)
                    for l in range(1, L):
                        pe.wait_ge(state, L * n + l)
                        pe.matmul(pr[:, l, :], v.at_blk[:, :], v.h_st[:, l - 1, :],
                                  start=False, stop=True, skip_group_check=True).then_inc(summed, 1)

                sweep(0, first=True)
                for n in range(1, SWEEPS):
                    sweep(n)
                pe.wait_ge(compared, 2)
                pe.matmul(pf[0:1, 0:1], differs[:, :], v.ones[:, 0:1], start=True, stop=True).then_inc(counted, 1)
                pe.wait_ge(flagged, 1)
                again = pe.value_load(flag[0:1, 0:1], min_val=0, max_val=P)
                with pe.If(again > 0):
                    with pe.Fori(SWEEPS, NCH + 1) as n:
                        sweep(n)
                pe.nop()

            @block.scalar
            def _(act):
                def sweep(n):
                    for l in range(L):
                        act.wait_ge(summed, L * n + l + 1)
                        act.activation(v.h_st[:, l, :], pr[:, l, :], ACT.Tanh,
                                       bias=v.u_bias[:, 0:1]).then_inc(state, 1)

                for n in range(SWEEPS - 1):
                    sweep(n)
                act.wait_ge(saved, 1)
                sweep(SWEEPS - 1)
                act.wait_ge(flagged, 1)
                again = act.value_load(flag[0:1, 0:1], min_val=0, max_val=P)
                with act.If(again > 0):
                    with act.Fori(SWEEPS, NCH + 1) as n:
                        sweep(n)
                act.nop()

            @block.vector
            def _(dve):
                dve.wait_ge(state, L * (SWEEPS - 1))
                dve.tensor_copy(ends[:, :], v.h_st[:, L - 1, :]).then_inc(saved, 1)
                dve.wait_ge(saved, 1)
                dve.wait_ge(state, L * SWEEPS)
                dve.tensor_tensor(diff[:, :], v.h_st[:, L - 1, :], ends[:, :], ALU.not_equal).then_inc(compared, 1)
                dve.wait_ge(compared, 1)
                dve.tensor_reduce(differs[:, :], diff[:, :], AX.X, ALU.max).then_inc(compared, 1)
                dve.wait_ge(counted, 1)
                dve.tensor_copy(flag[0:1, 0:1], pf[0:1, 0:1]).then_inc(flagged, 1)


def attend(nc, v):
    ident = v.ident
    NP = B * (B + 1) // 2
    PAIR0 = [0, 4, 7, 9]
    PV = 2 * B - 1
    with ExitStack() as c:
        def sb(name, shape, dt=F32):
            return c.enter_context(nc.sbuf_tensor(name, shape, dt))

        def psum(name, shape):
            return c.enter_context(nc.psum_tensor(name, shape, F32))

        sem = v.sem
        hs = [sb(f"c_hs{n}", [P, CPT, L]) for n in range(2)]
        xn = [sb(f"c_xn{n}", [P, B, D]) for n in range(2)]
        xnT = sb("c_xnT", [P, KD, BANK])
        q = sb("c_q", [P, B, D])
        k = [sb(f"c_k{n}", [P, B, D]) for n in range(2)]
        vv = [sb(f"c_v{n}", [P, B, D]) for n in range(2)]
        qk = sb("c_qk", [P, NP, D])
        sc = sb("c_sc", [P, B, B, H])
        ex = sb("c_ex", [P, B, B, H])
        att = [sb(f"c_att{n}", [P, B, B, H]) for n in range(2)]
        mx = sb("c_mx", [P, B * H])
        den = sb("c_den", [P, B * H])
        rden = sb("c_rden", [P, B * H])
        pv = sb("c_pv", [P, B - 1, D])
        st = sb("c_st", [P, B, 6])
        mv = sb("c_mv", [P, B, 2])
        ta = sb("c_ta", [P, B])
        r1 = sb("c_r1", [P, B])
        mhalf = sb("c_mhalf", [P, B])
        eps = sb("c_eps", [P, B])
        part3 = qk[:, :, :].rearrange("p n d -> p (n d)").bitcast(BF16)[:, 0:9 * D].rearrange("p (a d) -> p a d", a=3)
        rest = pv[:, :, :].rearrange("p i d -> p (i d)")
        bias3 = sb("c_bias3", [P, 3 * D], BF16)
        ones3 = sb("c_ones3", [P, P], BF16)

        pT = psum("c_pT", [P, KD, BANK])
        pX = psum("c_pX", [P, B, D])
        pY = psum("c_pY", [P, B, D])
        pL = psum("c_pL", [P, BANK])

        passed = sem("c_passed")
        open_ = sem("c_open")
        masked = sem("c_masked")
        bias_ready = sem("c_bias_ready")
        hs_ready = sem("c_hs_ready")
        o_done = sem("c_o_done")
        op_ready = sem("c_op_ready")
        x1_ready = sem("c_x1_ready")
        bn = sem("c_bn")
        stats = sem("c_stats")
        rchain = sem("c_rchain")
        r_ready = sem("c_r_ready")
        xn_ready = sem("c_xn_ready")
        xn_out = [sem(f"c_xn_out{n}") for n in range(2)]
        t_done = sem("c_t_done")
        t_evac = sem("c_t_evac")
        l_done = sem("c_l_done")
        l_evac = sem("c_l_evac")
        q_done = sem("c_q_done")
        q_evac = sem("c_q_evac")
        k_done = sem("c_k_done")
        k_evac = sem("c_k_evac")
        v_done = sem("c_v_done")
        v_evac = sem("c_v_evac")
        sm = sem("c_sm")
        ex_in = sem("c_ex_in")
        ex_out = sem("c_ex_out")
        att_ready = sem("c_att_ready")
        pv_step = sem("c_pv_step")
        SM = 6

        def steps_through(t):
            return PV * (t + 1) + PV + 1

        def spread(ap, n):
            return ap.unsqueeze(1).broadcast_to([P, n, ap.shape[1]])

        with nc.Block() as block:
            @block.sync
            def _(sp):
                for s in xn_out:
                    sp.sem_inc(s, 16)
                rows = v.xn3_dram.rearrange("(b t p) d -> t p b d", b=B, p=P)
                with sp.Fori(0, NT // 2) as i:
                    for u in range(2):
                        t = 2 * i + u
                        sp.wait_ge(xn_ready, t + 1)
                        sp.dma_start(rows[t], xn[u][:, :, :]).then_inc(xn_out[u], 16)
                for u in range(2):
                    sp.wait_ge(xn_out[u], 16 * NT // 2 + 16)

            @block.gpsimd
            def _(pool):
                pool.sem_inc(pv_step, PV + 1)
                for n, (t, value) in enumerate(((mhalf[:, :], -0.5), (eps[:, :], EPS))):
                    pool.memset(t, value).then_inc(open_, 1)
                    pool.wait_ge(open_, n + 1)

                def scale(t):
                    pool.wait_ge(stats, t + 1)
                    pool.tensor_tensor(ta[:, :], mv[:, :, 1], eps[:, :], ALU.add).then_inc(rchain, 1)
                    pool.wait_ge(rchain, t + 1)
                    pool.tensor_tensor(r1[:, :], ta[:, :], mhalf[:, :], ALU.pow).then_inc(r_ready, 1)

                for t in range(3):
                    scale(t)

                def body(i, u, left):
                    t = 2 * i + u
                    n = 0
                    pool.wait_ge(att_ready, t + 1)
                    for j in range(B):
                        w = B - j
                        a = att[u][:, j, j:B, :].unsqueeze(3).broadcast_to([P, w, H, DK])
                        row = vv[u][:, j, :].rearrange("p (h d) -> p h d", d=DK).unsqueeze(1).broadcast_to([P, w, H, DK])
                        o = v.prod_st[:, t, j * D:B * D]
                        part = o if j == 0 else pv[:, 0:w, :].rearrange("p i d -> p (i d)")
                        if n:
                            pool.wait_ge(pv_step, steps_through(t - 1) + n)
                            pool.sem_inc(passed, 1)
                        pool.tensor_tensor(part.rearrange("p (i h d) -> p i h d", i=w, h=H), a, row,
                                           ALU.mult).then_inc(pv_step, 1)
                        n += 1
                        if j:
                            pool.wait_ge(pv_step, steps_through(t - 1) + n)
                            pool.sem_inc(passed, 1)
                            pool.tensor_tensor(o, o, part, ALU.add).then_inc(pv_step, 1)
                            n += 1
                        if j == 1 and left >= 3:
                            scale(t + 3)

                tiles(pool, body)

            @block.vector
            def _(dve):
                dve.memset(sc[:, :, :, :], -1e30).then_inc(masked, 1)

                def layer0(t):
                    dve.wait_ge(o_done, t + 1)
                    dve.tensor_tensor(v.prod_st[:, t, :], pX[:, :, :].rearrange("p b d -> p (b d)"),
                                      v.prod_st[:, t, :], ALU.mult).then_inc(op_ready, 1)
                    dve.wait_ge(op_ready, t + 1)
                    dve.tensor_tensor(v.x_st[:, t, :], v.prod_st[:, t, :], v.x_st[:, t, :], ALU.add).then_inc(x1_ready, 1)
                    dve.wait_ge(x1_ready, t + 1)
                    dve.sem_inc(passed, 1)
                    for b in range(B):
                        last = dve.bn_stats(st[:, b, :], v.x_st[:, t, b * D:(b + 1) * D])
                    last.then_inc(bn, 1)
                    dve.wait_ge(bn, t + 1)
                    dve.sem_inc(passed, 1)
                    for b in range(B):
                        last = dve.bn_aggr(mv[:, b, :], st[:, b, :])
                    last.then_inc(stats, 1)

                def normalise(t, u, stores):
                    dve.wait_ge(r_ready, t + 1)
                    dve.wait_ge(xn_out[u], 16 * stores + 16)
                    for b in range(B):
                        last = dve.tensor_scalar(xn[u][:, b, :], v.x_st[:, t, b * D:(b + 1) * D],
                                                 mv[:, b, 0:1], r1[:, b:b + 1], ALU.subtract, ALU.mult)
                    last.then_inc(xn_ready, 1)

                layer0(0)
                normalise(0, 0, 0)
                flat = v.bqkv[:, :, :].rearrange("p n d -> p (n d)")
                dve.memset(bias3[:, :], 0.0).then_inc(masked, 1)
                dve.memset(ones3[:, :], 1.0).then_inc(masked, 1)
                dve.tensor_copy(part3[:, 0, :], flat).then_inc(bias_ready, 1)
                for n in range(1, 3):
                    dve.wait_ge(bias_ready, 2 * n - 1)
                    dve.tensor_tensor(rest[:, :], flat if n == 1 else rest[:, :], part3[:, n - 1, :],
                                      ALU.subtract).then_inc(bias_ready, 1)
                    dve.wait_ge(bias_ready, 2 * n)
                    dve.tensor_copy(part3[:, n, :], rest[:, :]).then_inc(bias_ready, 1)
                dve.wait_ge(bias_ready, 5)
                dve.wait_ge(masked, 3)
                for n in range(3):
                    last = dve.tensor_copy(bias3[GRP * n:GRP * n + 1, :], part3[GRP * n:GRP * n + 1, n, :])
                last.then_inc(bias_ready, 1)
                dve.wait_ge(bias_ready, 6)
                layer0(1)
                normalise(1, 1, 0)

                def body(i, u, left):
                    t = 2 * i + u
                    if left >= 2:
                        layer0(t + 2)
                    dve.wait_ge(k_evac, t + 1)
                    dve.wait_ge(q_evac, t + 1)
                    for j in range(B):
                        w = B - j
                        last = dve.tensor_tensor(qk[:, PAIR0[j]:PAIR0[j] + w, :], q[:, j:B, :],
                                                 spread(k[u][:, j, :], w), ALU.mult)
                    last.then_inc(sm, 1)
                    if left >= 2:
                        normalise(t + 2, u, i + 1)
                    dve.wait_ge(sm, SM * t + 1)
                    for j in range(B):
                        w = B - j
                        last = dve.tensor_reduce(
                            sc[:, j, j:B, :].rearrange("p i h -> p (i h)"),
                            qk[:, PAIR0[j]:PAIR0[j] + w, :].rearrange("p i (h d) -> p (i h) d", d=DK), AX.X, ALU.add)
                    last.then_inc(sm, 1)
                    dve.wait_ge(sm, SM * t + 2)
                    dve.tensor_reduce(mx[:, :], sc[:, :, :, :].rearrange("p j i h -> p (i h) j"), AX.X,
                                      ALU.max).then_inc(sm, 1)
                    dve.wait_ge(sm, SM * t + 3)
                    dve.tensor_tensor(ex[:, :, :, :].rearrange("p j i h -> p j (i h)"),
                                      sc[:, :, :, :].rearrange("p j i h -> p j (i h)"), spread(mx[:, :], B),
                                      ALU.subtract).then_inc(ex_in, 1)
                    dve.wait_ge(ex_out, t + 1)
                    dve.tensor_reduce(den[:, :], ex[:, :, :, :].rearrange("p j i h -> p (i h) j"), AX.X,
                                      ALU.add).then_inc(sm, 1)
                    dve.wait_ge(sm, SM * t + 4)
                    dve.tensor_scalar(den[:, :], den[:, :], 1.0, None, ALU.add).then_inc(sm, 1)
                    dve.wait_ge(sm, SM * t + 5)
                    dve.reciprocal(rden[:, :], den[:, :]).then_inc(sm, 1)
                    dve.wait_ge(sm, SM * t + SM)
                    dve.wait_ge(pv_step, steps_through(t - 2))
                    dve.tensor_tensor(att[u][:, :, :, :].rearrange("p j i h -> p j (i h)"),
                                      ex[:, :, :, :].rearrange("p j i h -> p j (i h)"), spread(rden[:, :], B),
                                      ALU.mult).then_inc(att_ready, 1)

                tiles(dve, body)

            @block.scalar
            def _(act):
                for s in (l_evac, v_evac):
                    act.sem_inc(s, 1)

                def states(t, u, reused=True):
                    if reused:
                        act.wait_ge(o_done, t - 1)
                        act.sem_inc(passed, 1)
                    act.activation(hs[u][:, :, :], v.h_st[:, :, bass.ts(t, CPT)].rearrange("p l c -> p c l"),
                                   ACT.Copy).then_inc(hs_ready, 1)

                def take(dst, src, done, evac, t):
                    act.wait_ge(done, t + 1)
                    act.activation(dst[:, :, :], src[:, :, :], ACT.Copy).then_inc(evac, 1)

                def take_qk(t, u, reused=True):
                    if reused:
                        act.wait_ge(sm, SM * (t - 1) + 1)
                    take(q, pY, q_done, q_evac, t)
                    take(k[u], pX, k_done, k_evac, t)

                def take_v(t, u, reused=True):
                    if reused:
                        act.wait_ge(pv_step, steps_through(t - 2))
                    take(vv[u], pY, v_done, v_evac, t)
                    act.wait_ge(l_done, t + 1)
                    act.sem_inc(passed, 1)
                    act.activation(v.logit_st[:, :, t, :], pL[:, 0:B * E].rearrange("p (b e) -> p b e", e=E),
                                   ACT.Copy).then_inc(l_evac, 1)

                states(0, 0, reused=False)
                states(1, 1, reused=False)
                take(xnT, pT, t_done, t_evac, 0)
                states(2, 0)
                take_qk(0, 0, reused=False)
                take_v(0, 0, reused=False)
                take(xnT, pT, t_done, t_evac, 1)
                take_qk(1, 1)

                def body(i, u, left):
                    t = 2 * i + u
                    if left >= 3:
                        states(t + 3, 1 - u)
                    act.wait_ge(ex_in, t + 1)
                    act.activation(ex[:, :, :, :], ex[:, :, :, :], ACT.Exp).then_inc(ex_out, 1)
                    if left >= 1:
                        take_v(t + 1, 1 - u)
                    if left >= 2:
                        take(xnT, pT, t_done, t_evac, t + 2)
                        take_qk(t + 2, u)

                tiles(act, body)

            @block.tensor
            def _(pe):
                def output(t, u):
                    pe.wait_ge(hs_ready, t + 1)
                    for n in range(2):
                        last = pe.matmul(pX[:, 2 * n:2 * n + 2, :].rearrange("p b d -> p (b d)"),
                                         hs[u][:, :, :].rearrange("p c l -> p (c l)"),
                                         v.wo_pad[:, 2 * n:2 * n + 2, :].rearrange("p b d -> p (b d)"),
                                         start=True, stop=True)
                    last.then_inc(o_done, 1)

                def turn(t, u):
                    pe.wait_ge(xn_ready, t + 1)
                    for kk in range(KD):
                        for b in range(B):
                            last = pe.transpose(pT[:, kk, b * P:(b + 1) * P], xn[u][:, b, kk * P:(kk + 1) * P], ident)
                    last.then_inc(t_done, 1)

                output(0, 0)
                pe.wait_ge(op_ready, 1)
                output(1, 1)
                turn(0, 0)
                pe.wait_ge(bias_ready, 6)

                def body(i, u, left):
                    t = 2 * i + u
                    pe.wait_ge(t_evac, t + 1)
                    for n, (dst, done) in enumerate(((pY, q_done), (pX, k_done), (pY, v_done))):
                        if n == 0:
                            pe.wait_ge(v_evac, t + 1)
                        if n == 1:
                            pe.wait_ge(op_ready, t + 2 if left >= 1 else t + 1)
                        if n == 2:
                            pe.wait_ge(l_evac, t + 1)
                            for b in range(B):
                                for kk in range(KD):
                                    last = pe.matmul(pL[:, b * E:(b + 1) * E], xnT[:, kk, b * P:(b + 1) * P], v.wgr[:, kk, :],
                                                     start=(kk == 0), stop=(kk == KD - 1))
                            last.then_inc(l_done, 1)
                            pe.wait_ge(q_evac, t + 1)
                        for m in range(2):
                            pe.matmul(dst[:, 2 * m:2 * m + 2, :], ones3[:, :], spread(bias3[:, n * D:(n + 1) * D], 2),
                                      start=True, stop=False, skip_group_check=True)
                        for b in range(B):
                            for kk in range(KD):
                                last = pe.matmul(dst[:, b, :], xnT[:, kk, b * P:(b + 1) * P],
                                                 v.wqkv[:, kk, n * D:(n + 1) * D], start=False, stop=(kk == KD - 1),
                                                 skip_group_check=True)
                        last.then_inc(done, 1)
                    if left >= 1:
                        turn(t + 1, 1 - u)
                    if left >= 2:
                        pe.wait_ge(k_evac, t + 1)
                        output(t + 2, u)

                tiles(pe, body)


def route(nc, v):
    W = NG * E
    K2 = TOPK * NG
    with ExitStack() as c:
        def sb(name, shape, dt=F32):
            return c.enter_context(nc.sbuf_tensor(name, shape, dt))

        sem = v.sem
        hot = sb("d_hot", [P, TOPK, NG, E])
        lg2 = sb("d_lg2", [P, NG, E])
        eq = sb("d_eq", [P, NG, E])
        best = sb("d_best", [P, TOPK, NG])
        first = sb("d_first", [P, TOPK, NG])
        total = sb("d_total", [P, E, K2])
        before = sb("d_before", [P, E, K2])
        pos = sb("d_pos", [P, TOPK, NG, E])
        loc = sb("d_loc", [P, K2])
        valid = sb("d_valid", [P, K2])
        loci = sb("d_loci", [P, K2], I32)
        lo_i = sb("d_lo_i", [P, K2], I32)
        hi_i = sb("d_hi_i", [P, K2], I32)
        lo = sb("d_lo", [P, K2])
        hi = sb("d_hi", [P, K2])
        gates = v.gates
        iota = sb("d_iota", [P, P], F16)
        dl = sb("d_dl", [P, NG])
        ee = sb("d_ee", [P, NG])
        ep = sb("d_ep", [P, NG])
        NB = 4
        ohl = [sb(f"d_ohl{n}", [P, NB, P], F16) for n in range(2)]
        off = [sb(f"d_off{n}", [P, NB, P]) for n in range(2)]
        val = [sb(f"d_val{n}", [P, 2, P], F16) for n in range(NB)]
        token = sb("d_token", [P, P])
        tab = sb("d_tab", [P, 2, P])
        empty = sb("d_empty", [P, P])
        t1 = sb("d_t1", [P, P])
        t2 = sb("d_t2", [P, P])
        zero = sb("d_zero", [P, 2 * P])
        ident16 = sb("d_ident", [P, P], F16)
        zero16 = sb("d_zero16", [P, 2 * P], F16)
        pin = c.enter_context(nc.psum_tensor("d_pin", [P, TOPK, BANK], F32))
        ptot = c.enter_context(nc.psum_tensor("d_ptot", [P, TOPK, BANK], F32))
        ptab = c.enter_context(nc.psum_tensor("d_ptab", [P, BANK], F32))

        passed = sem("d_passed")
        link = sem("d_link")
        hot_ready = sem("d_hot_ready")
        counts = sem("d_counts")
        e_in = sem("d_e_in")
        e_out = sem("d_e_out")
        one_ready = sem("d_one_ready")
        one_used = [sem(f"d_one_used{n}") for n in range(NB)]
        lo_ready = sem("d_lo_ready")
        off_ready = sem("d_off_ready")
        squared = sem("d_squared")
        ohl_ready = sem("d_ohl_ready")
        table = sem("d_table")
        lg = v.logit_st[:, :, :, :].rearrange("p b t e -> p (b t) e")
        expert = v.cst[:, C_E:C_E + E].unsqueeze(1).broadcast_to([P, NG, E])

        def each(ap):
            return ap.unsqueeze(2).broadcast_to([P, NG, E])

        with nc.Block() as block:
            @block.sync
            def _(sp):
                sp.dma_start(v.raw[:, 0, :].rearrange("p (k h) -> p k h", k=KD),
                             v.ew1[0].rearrange("(k p) h -> p k h", p=P)).then_inc(v.w1_in, 16)
                sp.dma_start(v.raw[:, 1, :].rearrange("p (t d) -> p t d", t=HT),
                             v.ew2[0].rearrange("(t p) d -> p t d", p=P)).then_inc(v.w2_in, 16)

            @block.vector
            def _(dve):
                done = [0]

                def linked(ins):
                    done[0] += 1
                    ins.then_inc(link, 1)
                    dve.wait_ge(link, done[0])

                dve.memset(zero16[:, :], 0.0)
                dve.tensor_copy(iota[:, :], v.iota)
                dve.tensor_copy(ident16[:, :], v.ident)
                linked(dve.memset(zero[:, :], 0.0))
                for t in (v.idx, v.dst):
                    dve.memset(t[:, E * CAP // P:], 0)
                for k in range(TOPK):
                    src = lg if k == 0 else lg2[:, :, :]
                    linked(dve.tensor_reduce(best[:, k, :], src, AX.X, ALU.max))
                    linked(dve.tensor_tensor(eq[:, :, :], src, each(best[:, k, :]), ALU.is_equal))
                    linked(dve.scalar_tensor_tensor(eq[:, :, :], expert, float(-E), eq[:, :, :], ALU.add, ALU.mult))
                    linked(dve.tensor_reduce(first[:, k, :], eq[:, :, :], AX.X, ALU.min))
                    linked(dve.tensor_scalar(first[:, k, :], first[:, k, :], float(E), None, ALU.add))
                    ins = dve.tensor_tensor(hot[:, k, :, :], expert, each(first[:, k, :]), ALU.is_equal)
                    ins.then_inc(hot_ready, 1)
                    dve.wait_ge(hot_ready, k + 1)
                    if k == 0:
                        linked(dve.scalar_tensor_tensor(lg2[:, :, :], hot[:, 0, :, :], -1e30, lg, ALU.mult, ALU.add))
                dve.tensor_tensor(dl[:, :], best[:, 1, :], best[:, 0, :], ALU.subtract).then_inc(e_in, 1)
                dve.wait_ge(e_out, 1)
                linked(dve.tensor_scalar(ep[:, :], ee[:, :], 1.0, None, ALU.add))
                linked(dve.reciprocal(gates[:, 0, :], ep[:, :]))
                linked(dve.tensor_tensor(gates[:, 1, :], ee[:, :], gates[:, 0, :], ALU.mult))
                dve.wait_ge(counts, 2)
                for k in range(TOPK):
                    linked(dve.tensor_copy(total[:, :, k * NG:(k + 1) * NG],
                                           ptot[:, k, :].rearrange("p (g e) -> p e g", e=E)))
                for e in range(E):
                    linked(dve.tensor_tensor_scan(before[:, e, :], total[:, e, :], zero[:, 0:K2], 0.0,
                                                  ALU.add, ALU.add))
                linked(dve.tensor_tensor(before[:, :, :], before[:, :, :], total[:, :, :], ALU.subtract))
                for k in range(TOPK):
                    linked(dve.tensor_tensor(pos[:, k, :, :], pin[:, k, :].rearrange("p (g e) -> p g e", e=E),
                                             before[:, :, k * NG:(k + 1) * NG].rearrange("p e g -> p g e"), ALU.add))
                linked(dve.tensor_tensor(pos[:, :, :, :], pos[:, :, :, :], hot[:, :, :, :], ALU.mult))
                linked(dve.tensor_reduce(loc[:, :], pos[:, :, :, :].rearrange("p k g e -> p (k g) e"), AX.X, ALU.add))
                linked(dve.tensor_scalar(valid[:, :], loc[:, :], float(CAP), None, ALU.is_lt))
                linked(dve.tensor_copy(loci[:, :], loc[:, :]))
                dve.tensor_scalar(lo_i[:, :], loci[:, :], P - 1, None, ALU.bitwise_and)
                linked(dve.tensor_scalar(hi_i[:, :], loci[:, :], 7, None, ALU.logical_shift_right))
                dve.tensor_copy(lo[:, :], lo_i[:, :])
                linked(dve.tensor_copy(hi[:, :], hi_i[:, :]))
                dve.sem_inc(lo_ready, 1)
                linked(dve.scalar_tensor_tensor(hi[:, :], first[:, :, :].rearrange("p k g -> p (k g)"),
                                                float(CAP // P), hi[:, :], ALU.mult, ALU.add))
                linked(dve.scalar_tensor_tensor(hi[:, :], hi[:, :], 1.0, valid[:, :], ALU.add, ALU.mult))
                linked(dve.tensor_scalar(hi[:, :], hi[:, :], -1.0, None, ALU.add))
                with dve.Fori(0, K2 // NB) as i:
                    for u in range(NB):
                        n = NB * i + u
                        dve.wait_ge(one_used[u], i + 2)
                        dve.wait_ge(link, done[0])
                        dve.tensor_scalar(val[u][:, 0, :], iota[:, :], hi[:, bass.ds(n, 1)],
                                          v.cst[:, bass.ds(C_G + n, 1)], ALU.is_equal, ALU.mult)
                        dve.tensor_scalar(val[u][:, 1, :], iota[:, :], hi[:, bass.ds(n, 1)],
                                          v.cst[:, C_P:C_P + 1], ALU.is_equal, ALU.mult).then_inc(one_ready, 1)
                dve.wait_ge(table, 1)
                linked(dve.tensor_copy(tab[:, :, :], ptab[:, 0:2 * P].rearrange("p (a b) -> p a b", a=2)))
                linked(dve.scalar_tensor_tensor(token[:, :], tab[:, 0, :], float(P), tab[:, 1, :], ALU.mult, ALU.add))
                linked(dve.tensor_scalar(empty[:, :], token[:, :], 0.0, None, ALU.is_equal))
                linked(dve.scalar_tensor_tensor(t1[:, :], empty[:, :], float(TOPK * N + 1), token[:, :],
                                                ALU.mult, ALU.add))
                dve.tensor_scalar(v.dst[:, 0:P], t1[:, :], -1.0, None, ALU.add)
                linked(dve.tensor_scalar(t2[:, :], token[:, :], float(N), float(-N), ALU.is_gt, ALU.mult))
                linked(dve.scalar_tensor_tensor(t2[:, :], t2[:, :], -1.0, token[:, :], ALU.add, ALU.add))
                linked(dve.tensor_scalar(v.idx[:, 0:P], t2[:, :], 0.0, None, ALU.max))

            @block.gpsimd
            def _(pool):
                pool.wait_ge(lo_ready, 1)
                with pool.Fori(0, K2 // NB // 2) as i:
                    for m in range(2):
                        for u in range(NB):
                            pool.wait_ge(one_used[u], 2 * i + m + 1)
                        pool.sem_inc(passed, 1)
                        pool.tensor_tensor(off[m][:, :, :], v.iota.unsqueeze(1).broadcast_to([P, NB, P]),
                                           lo[:, bass.ts(2 * i + m, NB)].unsqueeze(2).broadcast_to([P, NB, P]),
                                           ALU.subtract).then_inc(off_ready, 1)

            @block.scalar
            def _(act):
                act.wait_ge(e_in, 1)
                act.activation(ee[:, :], dl[:, :], ACT.Exp).then_inc(e_out, 1)
                with act.Fori(0, K2 // NB // 2) as i:
                    for m in range(2):
                        act.wait_ge(off_ready, 2 * i + m + 1)
                        act.activation(off[m][:, :, :], off[m][:, :, :], ACT.Square).then_inc(squared, 1)
                        act.wait_ge(squared, 2 * i + m + 1)
                        act.activation(ohl[m][:, :, :], off[m][:, :, :], ACT.Relu, scale=-1.0,
                                       bias=v.ones[:, 0:1]).then_inc(ohl_ready, 1)

            @block.tensor
            def _(pe):
                for s in one_used:
                    pe.sem_inc(s, 2)
                for k in range(TOPK):
                    pe.wait_ge(hot_ready, k + 1)
                    oh = hot[:, k, :, :].rearrange("p g e -> p (g e)")
                    pe.matmul(pin[:, k, :], v.cst[:, C_UP:C_UP + P], oh, start=True, stop=True)
                    pe.matmul(ptot[:, k, :], v.ones, oh, start=True, stop=True).then_inc(counts, 1)
                pe.wait_ge(link, 1)
                pe.matmul(ptab[:, 0:2 * P], ident16[:, :], zero16[:, :], start=True, stop=False, skip_group_check=True)
                with pe.Fori(0, K2 // NB // 2) as i:
                    for m in range(2):
                        pe.wait_ge(ohl_ready, 2 * i + m + 1)
                        for u in range(NB):
                            pe.wait_ge(one_ready, NB * (2 * i + m) + u + 1)
                            pe.matmul(ptab[:, 0:2 * P], ohl[m][:, u, :], val[u][:, :, :].rearrange("p a b -> p (a b)"),
                                      start=False, stop=False, skip_group_check=True).then_inc(one_used[u], 1)
                pe.matmul(ptab[:, 0:2 * P], ident16[:, :], zero16[:, :], start=False, stop=True,
                          skip_group_check=True).then_inc(table, 1)


def experts(nc, v):
    with ExitStack() as c:
        def sb(name, shape, dt=F32):
            return c.enter_context(nc.sbuf_tensor(name, shape, dt))

        def psum(name, shape):
            return c.enter_context(nc.psum_tensor(name, shape, F32))

        sem = v.sem
        W = BLK * P
        HALF = KD * HID
        raw = v.raw
        w1_hi = sb("e_w1_hi", [P, KD, HID], F16)
        w1_lo = sb("e_w1_lo", [P, KD, HID], F16)
        w2_hi = sb("e_w2_hi", [P, HT, D], F16)
        w2_lo = sb("e_w2_lo", [P, HT, D], F16)
        most = sb("e_most", [P, 3])
        most3 = sb("e_most3", [3, 1])
        diag = sb("e_diag", [3, 3])
        bound = sb("e_bound", [P, 3])
        power = sb("e_power", [P, 3], I32)
        scale = [sb(f"e_scale{n}", [P, 3], I32) for n in range(2)]
        h_scale = [sb(f"e_h_scale{n}", [P, 1]) for n in range(2)]
        y_scale = [sb(f"e_y_scale{n}", [P, 1]) for n in range(2)]
        b1c = [sb(f"e_b1c{n}", [P, HT]) for n in range(2)]
        b2b = [v.logit_st[:, :, :, :].rearrange("p b t e -> p (b t e)")[:, n * D:(n + 1) * D] for n in range(2)]
        icol = [sb(f"e_icol{n}", [P, BLK], I32) for n in range(2)]
        dcol = [sb(f"e_dcol{n}", [P, BLK], I32) for n in range(2)]
        xg = [sb(f"e_xg{n}", [P, BLK, D]) for n in range(2)]
        x_hi = sb("e_x_hi", [P, KD, W], F16)
        x_lo = sb("e_x_lo", [P, KD, W], F16)
        h_all = [sb(f"e_h_all{n}", [P, W]) for n in range(2)]
        h_hi = sb("e_h_hi", [P, HT, W], F16)
        h_lo = sb("e_h_lo", [P, HT, W], F16)
        yo = [sb(f"e_yo{n}", [P, BLK, D]) for n in range(2)]

        pT = psum("e_pT", [P, KD, BANK])
        NPH = 4
        pH = [psum(f"e_pH{n}", [P, BANK]) for n in range(NPH)]
        pY = psum("e_pY", [P, BLK, D])

        passed = sem("e_passed")
        w1_in, w2_in = v.w1_in, v.w2_in
        w1_hi_ready = sem("e_w1_hi_ready")
        w1_lo_ready = sem("e_w1_lo_ready")
        w2_hi_ready = sem("e_w2_hi_ready")
        w2_lo_ready = sem("e_w2_lo_ready")
        b2_in = [sem(f"e_b2_in{n}") for n in range(2)]
        most_ready = sem("e_most_ready")
        most_turned = sem("e_most_turned")
        diag_ready = sem("e_diag_ready")
        most_spread = sem("e_most_spread")
        step = sem("e_step")
        scales_ready = sem("e_scales_ready")
        icols = sem("e_icols")
        x_in = [sem(f"e_x_in{n}") for n in range(2)]
        t_done = sem("e_t_done")
        x_hi_ready = sem("e_x_hi_ready")
        x_lo_ready = sem("e_x_lo_ready")
        h_done = sem("e_h_done")
        h_ready = sem("e_h_ready")
        odd_ready = sem("e_odd_ready")
        h_lo_ready = sem("e_h_lo_ready")
        y_done = sem("e_y_done")
        yb_ready = sem("e_yb_ready")
        y_out = [sem(f"e_y_out{n}") for n in range(2)]
        NGR = E * GRPS
        STEPS = 8

        def groups(eng, body):
            with eng.Fori(0, E // 2) as ep:
                for eu in range(2):
                    for g in range(GRPS):
                        e = 2 * ep + eu
                        body(e, eu, g, GRPS * e + g)

        with nc.Block() as block:
            @block.sync
            def _(sp):
                w1_v = v.ew1.rearrange("e (k p) h -> e p k h", p=P)
                w2_v = v.ew2.rearrange("e (t p) d -> e p t d", p=P)

                def load_w1(e):
                    sp.dma_start(raw[:, 0, :].rearrange("p (k h) -> p k h", k=KD), w1_v[e]).then_inc(w1_in, 16)

                def load_w2(e):
                    sp.dma_start(raw[:, 1, :].rearrange("p (t d) -> p t d", t=HT), w2_v[e]).then_inc(w2_in, 16)

                def follow(e, source):
                    sp.wait_ge(w1_hi_ready, e + 1)
                    sp.wait_ge(w1_lo_ready, e + 1)
                    load_w1(source)
                    sp.wait_ge(w2_hi_ready, HT * (e + 1))
                    sp.wait_ge(w2_lo_ready, HT * (e + 1))
                    load_w2(source)

                sp.dma_start(b2b[1], v.eb2[1].partition_broadcast(P)).then_inc(b2_in[1], 16)
                with sp.Fori(0, E // 2 - 1) as ep:
                    for eu in range(2):
                        e = 2 * ep + eu
                        follow(e, e + 1)
                        sp.wait_ge(yb_ready, GRPS * (e + 1) + 1)
                        sp.dma_start(b2b[eu], v.eb2[e + 2].partition_broadcast(P)).then_inc(b2_in[eu], 16)
                follow(E - 2, E - 1)
                follow(E - 1, E - 1)
                sp.wait_ge(w1_in, 16 * (E + 1))
                sp.wait_ge(w2_in, 16 * (E + 1))

            @block.gpsimd
            def _(pool):
                pool.dma_start(b2b[0], v.eb2[0].partition_broadcast(P)).then_inc(y_out[1], 16)

                def gather(n, u):
                    pool.wait_ge(icols, n + 1)
                    pool.sem_inc(passed, 1)
                    for q in range(BLK):
                        pool.indirect_dma_start(xg[u][:, q, :], None, v.xn3_dram,
                                                bass.IndirectOffsetOnAxis(icol[u][:, q:q + 1], axis=0),
                                                bounds_check=N - 1, oob_is_err=False).then_inc(x_in[u], 16)

                for u in range(2):
                    gather(u, u)
                with pool.Fori(0, NGR // 2) as i:
                    for u in range(2):
                        gather(2 * i + u + 2, u)
                        pool.wait_ge(yb_ready, 2 * i + u + 1 + 1)
                        pool.sem_inc(passed, 1)
                        for q in range(BLK):
                            pool.indirect_dma_start(
                                v.y_dram, bass.IndirectOffsetOnAxis(dcol[u][:, q:q + 1], axis=0), yo[u][:, q, :], None,
                                bounds_check=TOPK * N - 1, oob_is_err=False).then_inc(y_out[u], 16)
                for u in range(2):
                    pool.wait_ge(y_out[u], 16 * BLK * NGR // 2 + 16 * u)
                    pool.wait_ge(x_in[u], 16 * BLK * (NGR // 2 + 1))

            @block.vector
            def _(dve):
                dve.sem_inc(h_lo_ready, 1)
                dve.sem_inc(yb_ready, 1)
                dve.sem_inc(b2_in[0], 16)

                def take_icol(n, u):
                    dve.tensor_copy(icol[u][:, :], v.idx[:, bass.ts(n, BLK)]).then_inc(icols, 1)

                def take_dcol(n, u):
                    dve.tensor_copy(dcol[u][:, :], v.dst[:, bass.ts(n, BLK)])

                def largest(e, eu):
                    dve.wait_ge(w1_in, 16 * (e + 1))
                    dve.wait_ge(w2_in, 16 * (e + 1))
                    dve.sem_inc(passed, 1)
                    dve.tensor_copy(b1c[eu][:, :], v.b1t[:, bass.ts(e, HT)]).then_inc(step, 1)
                    dve.tensor_reduce(most[:, 0:2], raw[:, :, :], AX.X, ALU.max, apply_absolute_value=True)
                    dve.wait_ge(step, STEPS * e + 1)
                    dve.tensor_reduce(most[:, 2:3], b1c[eu][:, :], AX.X, ALU.max,
                                      apply_absolute_value=True).then_inc(most_ready, 1)

                def largest_of_all(e):
                    dve.wait_ge(most_turned, e + 1)
                    dve.tensor_reduce(most3[:, :], pT[0:3, 0, 0:P], AX.X, ALU.max).then_inc(step, 1)
                    dve.wait_ge(step, STEPS * e + 2)
                    dve.tensor_scalar(diag[:, :], v.ident[0:3, 0:3], most3[:, 0:1], None,
                                      ALU.mult).then_inc(diag_ready, 1)

                def scales(e, eu):
                    dve.wait_ge(most_spread, e + 1)
                    dve.sem_inc(passed, 1)
                    dve.tensor_copy(bound[:, :], pT[:, 1, 0:3]).then_inc(step, 1)
                    dve.wait_ge(step, STEPS * e + 3)
                    dve.scalar_tensor_tensor(bound[:, 2:3], bound[:, 0:1], float(D), bound[:, 2:3],
                                             ALU.mult, ALU.add).then_inc(step, 1)
                    dve.wait_ge(step, STEPS * e + 4)
                    dve.tensor_scalar(bound[:, :], bound[:, :], LEAST, None, ALU.max).then_inc(step, 1)
                    dve.wait_ge(step, STEPS * e + 5)
                    dve.tensor_scalar(power[:, :], bound[:, :].bitcast(I32), EXPONENT, None,
                                      ALU.bitwise_and).then_inc(step, 1)
                    dve.wait_ge(step, STEPS * e + 6)
                    dve.tensor_scalar(scale[eu][:, :], power[:, :], -1.0, float((127 + 127 + RANGE_LOG2) << 23),
                                      ALU.mult, ALU.add).then_inc(step, 1)
                    dve.wait_ge(step, STEPS * e + 7)
                    two = power[:, :].bitcast(F32)
                    s = scale[eu][:, :].bitcast(F32)
                    dve.tensor_scalar(h_scale[eu][:, :], two[:, 0:1], s[:, 2:3], 1.0 / (RANGE * X_SCALE),
                                      ALU.mult, ALU.mult)
                    dve.tensor_scalar(y_scale[eu][:, :], two[:, 1:2], two[:, 2:3], 1.0 / (RANGE * RANGE),
                                      ALU.mult, ALU.mult)
                    dve.tensor_scalar(b1c[eu][:, :], b1c[eu][:, :], s[:, 2:3], None, ALU.mult).then_inc(step, 1)
                    dve.wait_ge(step, STEPS * e + STEPS)
                    dve.sem_inc(scales_ready, 1)

                def lower_w1(e, eu):
                    dve.wait_ge(w1_hi_ready, e + 1)
                    dve.scalar_tensor_tensor(w1_lo[:, :, :].rearrange("p k h -> p (k h)"), raw[:, 0, :],
                                             scale[eu][:, 0:1].bitcast(F32),
                                             w1_hi[:, :, :].rearrange("p k h -> p (k h)"),
                                             ALU.mult, ALU.subtract).then_inc(w1_lo_ready, 1)

                def lower_w2(e, eu, h):
                    dve.wait_ge(w2_hi_ready, HT * e + h + 1)
                    dve.scalar_tensor_tensor(w2_lo[:, h, :], raw[:, 1, h * D:(h + 1) * D],
                                             scale[eu][:, 1:2].bitcast(F32), w2_hi[:, h, :],
                                             ALU.mult, ALU.subtract).then_inc(w2_lo_ready, 1)

                def x_lower(n):
                    dve.wait_ge(x_hi_ready, n + 1)
                    dve.sem_inc(passed, 1)
                    dve.scalar_tensor_tensor(x_lo[:, :, :], pT[:, :, :], X_SCALE, x_hi[:, :, :],
                                             ALU.mult, ALU.subtract).then_inc(x_lo_ready, 1)

                take_icol(0, 0)
                take_icol(1, 1)
                take_dcol(0, 0)
                largest(0, 0)
                largest_of_all(0)
                scales(0, 0)
                lower_w1(0, 0)
                x_lower(0)

                def body(e, eu, g, n):
                    u = g % 2
                    for h in range(HT):
                        dve.wait_ge(h_ready, HT * n + h + 1 + 1)
                        if h % 2:
                            dve.sem_inc(passed, 1)
                            dve.tensor_copy(h_hi[:, h, :], h_all[1][:, :]).then_inc(odd_ready, 1)
                            dve.wait_ge(odd_ready, HT // 2 * n + h // 2 + 1)
                        dve.tensor_tensor(h_lo[:, h, :], h_all[h % 2][:, :], h_hi[:, h, :],
                                          ALU.subtract).then_inc(h_lo_ready, 1)
                        if g == 0:
                            lower_w2(e, eu, h)
                        if g == 2 and h == 1:
                            largest_of_all(e + 1)
                    x_lower(n + 1)
                    take_icol(n + 2, u)
                    if g == 1:
                        largest(e + 1, 1 - eu)
                    elif g == 2:
                        scales(e + 1, 1 - eu)
                    elif g == GRPS - 1:
                        lower_w1(e + 1, 1 - eu)
                    if u == 0:
                        dve.wait_ge(y_out[1], 8 * BLK * n + 16)
                    else:
                        dve.wait_ge(y_out[0], 8 * BLK * (n + 1))
                    take_dcol(n + 1, 1 - u)
                    dve.wait_ge(y_done, n + 1)
                    if g == 0:
                        dve.wait_ge(b2_in[eu], 8 * (e - eu) + 16)
                    dve.scalar_tensor_tensor(yo[u][:, :, :], pY[:, :, :], y_scale[eu][:, 0:1],
                                             b2b[eu].unsqueeze(1).broadcast_to([P, BLK, D]),
                                             ALU.mult, ALU.add).then_inc(yb_ready, 1)

                groups(dve, body)

            @block.scalar
            def _(act):
                act.sem_inc(h_ready, 1)

                def upper_w1(e, eu):
                    act.wait_ge(scales_ready, e + 1)
                    act.sem_inc(passed, 1)
                    act.activation(w1_hi[:, :, :].rearrange("p k h -> p (k h)"), raw[:, 0, :], ACT.Copy,
                                   scale=scale[eu][:, 0:1].bitcast(F32)).then_inc(w1_hi_ready, 1)

                def upper_w2(eu, h):
                    act.activation(w2_hi[:, h, :], raw[:, 1, h * D:(h + 1) * D], ACT.Copy,
                                   scale=scale[eu][:, 1:2].bitcast(F32)).then_inc(w2_hi_ready, 1)

                def x_upper(n):
                    act.wait_ge(t_done, n + 1)
                    act.activation(x_hi[:, :, :], pT[:, :, :], ACT.Copy, scale=X_SCALE).then_inc(x_hi_ready, 1)

                upper_w1(0, 0)
                x_upper(0)

                def body(e, eu, g, n):
                    u = g % 2
                    for h in range(HT):
                        act.wait_ge(h_done, HT * n + h + 1)
                        act.wait_ge(h_lo_ready, HT * n + max(h - 1, 0) + 1)
                        for dst in (h_all[h % 2][:, :], h_hi[:, h, :])[0:2 - h % 2]:
                            last = act.activation(dst, pH[h % NPH][:, :], ACT.Relu, bias=b1c[eu][:, h:h + 1],
                                                  scale=h_scale[eu][:, 0:1])
                        last.then_inc(h_ready, 1)
                        if g == 0:
                            upper_w2(eu, h)
                    x_upper(n + 1)
                    if g == GRPS - 1:
                        upper_w1(e + 1, 1 - eu)

                groups(act, body)

            @block.tensor
            def _(pe):
                def turn(u, uses):
                    pe.wait_ge(x_in[u], 16 * BLK * uses)
                    for k in range(KD):
                        for q in range(BLK):
                            last = pe.transpose(pT[:, k, q * P:(q + 1) * P], xg[u][:, q, k * P:(k + 1) * P], v.ident)
                    last.then_inc(t_done, 1)

                def turn_most(e):
                    pe.wait_ge(most_ready, e + 1)
                    pe.transpose(pT[0:3, 0, 0:P], most[:, :], v.ident).then_inc(most_turned, 1)

                def spread_most(e):
                    pe.wait_ge(diag_ready, e + 1)
                    pe.matmul(pT[:, 1, 0:3], v.ones[0:3, :], diag[:, :], start=True, stop=True).then_inc(most_spread, 1)

                turn_most(0)
                spread_most(0)
                pe.wait_ge(scales_ready, 1)
                turn(0, 1)

                def body(e, eu, g, n):
                    u = g % 2
                    if g == 0:
                        pe.wait_ge(w1_lo_ready, e + 1)
                        pe.sem_inc(passed, 1)
                    pe.wait_ge(x_lo_ready, n + 1)
                    for h in range(HT):
                        pe.wait_ge(h_ready, HT * n + max(h - NPH + 1, 0) + 1)
                        rows = slice(h * P, (h + 1) * P)
                        for k in range(KD):
                            pe.matmul(pH[h % NPH][:, :], w1_hi[:, k, rows], x_hi[:, k, :], start=(k == 0), stop=False)
                            pe.matmul(pH[h % NPH][:, :], w1_hi[:, k, rows], x_lo[:, k, :], start=False, stop=False)
                            last = pe.matmul(pH[h % NPH][:, :], w1_lo[:, k, rows], x_hi[:, k, :],
                                             start=False, stop=(k == KD - 1))
                        last.then_inc(h_done, 1)
                        if g == 2 and h == 0:
                            turn_most(e + 1)
                    if g == 2:
                        pe.wait_ge(diag_ready, e + 2)
                    elif g == 3:
                        pe.wait_ge(scales_ready, e + 2)
                    turn(1 - u, 2 * e + (g + 1) // 2 + 1)
                    pe.wait_ge(yb_ready, n + 1)
                    for q in range(BLK):
                        cols = slice(q * P, (q + 1) * P)
                        for h in range(HT):
                            if q == 0:
                                if g == 0:
                                    pe.wait_ge(w2_lo_ready, HT * e + h + 1)
                                    pe.sem_inc(passed, 1)
                                pe.wait_ge(h_lo_ready, HT * n + h + 1 + 1)
                            pe.matmul(pY[:, q, :], h_hi[:, h, cols], w2_hi[:, h, :], start=(h == 0), stop=False)
                            pe.matmul(pY[:, q, :], h_hi[:, h, cols], w2_lo[:, h, :], start=False, stop=False)
                            last = pe.matmul(pY[:, q, :], h_lo[:, h, cols], w2_hi[:, h, :],
                                             start=False, stop=(h == HT - 1))
                        if g == 2 and q == 1:
                            pe.wait_ge(x_lo_ready, n + 2)
                            spread_most(e + 1)
                    last.then_inc(y_done, 1)

                groups(pe, body)


def combine(nc, v):
    with ExitStack() as c:
        def sb(name, shape, dt=F32):
            return c.enter_context(nc.sbuf_tensor(name, shape, dt))

        sem = v.sem
        NB = 8
        AHEAD = 6
        ya = [sb(f"f_ya{n}", [P, B * D]) for n in range(NB)]
        yb = [sb(f"f_yb{n}", [P, B * D]) for n in range(NB)]
        y_in = [sem(f"f_y_in{n}") for n in range(NB)]
        passed = sem("f_passed")
        first_ready = sem("f_first_ready")
        sum_ready = sem("f_sum_ready")
        silu_ready = sem("f_silu_ready")
        sg_ready = sem("f_sg_ready")
        o_ready = sem("f_o_ready")
        o_out = [sem(f"f_o_out{n}") for n in range(NB)]

        def rounds(eng, body):
            with eng.Fori(0, NT // NB - 1) as i:
                for n in range(NB):
                    body(i, n, NB)
            for n in range(NB):
                body(NT // NB - 1, n, NB - 1 - n)

        with nc.Block() as block:
            @block.sync
            def _(sp):
                for n in range(NB):
                    sp.sem_inc(o_out[n], 16)
                dst = v.out.rearrange("b (t p) d -> t p b d", p=P)
                rows = v.y_dram.rearrange("(k b t p) d -> t k p b d", k=TOPK, b=B, p=P)

                def load(t, n):
                    for k, y in enumerate((ya[n], yb[n])):
                        sp.dma_start(y[:, :].rearrange("p (b d) -> p b d", b=B), rows[t, k]).then_inc(y_in[n], 16)

                for n in range(AHEAD):
                    load(n, n)

                def body(i, n, left):
                    t = NB * i + n
                    sp.wait_ge(o_ready, t + 1)
                    sp.dma_start(dst[t], ya[n][:, :].rearrange("p (b d) -> p b d", b=B)).then_inc(o_out[n], 16)
                    if left >= AHEAD:
                        m = (n + AHEAD) % NB
                        sp.wait_ge(o_out[m], 16 * (i + (n + AHEAD) // NB) + 16)
                        load(t + AHEAD, m)

                rounds(sp, body)
                for n in range(NB):
                    sp.wait_ge(o_out[n], 16 * (NT // NB) + 16)

            @block.vector
            def _(dve):
                def add(i, n):
                    t = NB * i + n
                    dve.wait_ge(y_in[n], 32 * (i + 1))
                    dve.wait_ge(first_ready, t + 1)
                    for b in range(B):
                        cols = slice(b * D, (b + 1) * D)
                        last = dve.scalar_tensor_tensor(ya[n][:, cols], yb[n][:, cols],
                                                        v.gates[:, 1, bass.ds(b * NT + t, 1)], ya[n][:, cols],
                                                        ALU.mult, ALU.add)
                    last.then_inc(sum_ready, 1)

                add(0, 0)
                add(0, 1)

                def body(i, n, left):
                    t = NB * i + n
                    if left >= 2:
                        add(i + (n + 2) // NB, (n + 2) % NB)
                    dve.wait_ge(silu_ready, t + 1)
                    dve.tensor_tensor(ya[n][:, :], ya[n][:, :], v.prod_st[:, t, :], ALU.mult).then_inc(sg_ready, 1)

                rounds(dve, body)

            @block.gpsimd
            def _(pool):
                def body(i, n, left):
                    t = NB * i + n
                    pool.wait_ge(sg_ready, t + 1)
                    pool.sem_inc(passed, 1)
                    pool.tensor_tensor(ya[n][:, :], ya[n][:, :], v.x_st[:, t, :], ALU.add).then_inc(o_ready, 1)

                rounds(pool, body)

            @block.scalar
            def _(act):
                def silu(t, n):
                    act.wait_ge(sum_ready, t + 1)
                    act.activation(ya[n][:, :], ya[n][:, :], ACT.Silu).then_inc(silu_ready, 1)

                def first(i, n):
                    t = NB * i + n
                    act.wait_ge(y_in[n], 32 * (i + 1))
                    act.sem_inc(passed, 1)
                    for b in range(B):
                        cols = slice(b * D, (b + 1) * D)
                        last = act.activation(ya[n][:, cols], ya[n][:, cols], ACT.Copy,
                                              scale=v.gates[:, 0, bass.ds(b * NT + t, 1)])
                    last.then_inc(first_ready, 1)

                first(0, 0)
                first(0, 1)
                first(0, 2)
                silu(0, 0)

                def body(i, n, left):
                    t = NB * i + n
                    if left >= 3:
                        first(i + (n + 3) // NB, (n + 3) % NB)
                    if left >= 1:
                        silu(t + 1, (n + 1) % NB)

                rounds(act, body)


def kernel(**inputs):
    import numpy as np
    import concourse.bacc as bacc
    from concourse.bass_utils import run_bass_kernel_spmd

    nc = bacc.Bacc("TRN2", target_bir_lowering=False, num_devices=1)
    order = ["L0_attn_x", "L0_attn_Ws", "L0_attn_bs", "L0_attn_Wi", "L0_attn_bi", "L0_attn_Wo", "L0_attn_bo",
             "L0_attn_Wg", "L0_attn_bg", "L0_attn_ln_w", "L0_attn_ln_b", "L0_attn_A", "L0_ffn_Win", "L0_ffn_bin_",
             "L0_ffn_W1", "L0_ffn_b1", "L0_ffn_W2", "L0_ffn_b2", "L0_ffn_Wout", "L0_ffn_bout", "L1_attn_Wq",
             "L1_attn_bq", "L1_attn_Wk", "L1_attn_bk", "L1_attn_Wv", "L1_attn_bv", "L1_ffn_wg", "L1_ffn_w1",
             "L1_ffn_b1", "L1_ffn_w2", "L1_ffn_b2"]
    arrays = {"constants": constants()}
    for name in order:
        arrays[name] = np.ascontiguousarray(inputs[name])
    args = [nc.dram_tensor(n, a.shape, mybir.dt.from_np(a.dtype), kind="ExternalInput").ap()
            for n, a in arrays.items()]
    out = nc.dram_tensor("out", (B, S, D), F32, kind="ExternalOutput").ap()
    program(nc, [*args, out])
    r = run_bass_kernel_spmd(nc, [arrays], core_ids=[0])
    return r.results[0]["out"]
```
